# Optimizing a Trainium2 kernel written in Bass

```python
import numpy as np
import jax
import jax.numpy as jnp

def _softmax(x, axis=-1):
    return jax.nn.softmax(x, axis=axis)

def _gelu(x):
    return jax.nn.gelu(x, approximate=True)

def _silu(x):
    return jax.nn.silu(x)

def _sigmoid(x):
    return jax.nn.sigmoid(x)

def _layernorm(x, axis=-1, eps=1e-05):
    m = jnp.mean(x, axis=axis, keepdims=True)
    v = jnp.var(x, axis=axis, keepdims=True)
    return (x - m) / jnp.sqrt(v + eps)

def _scatter_add(tgt, idx, src, axis=0):
    return tgt.at[idx].add(src)

def _segment_sum(src, seg, n):
    return jax.ops.segment_sum(src, seg, n)
kernel_name = 'mk_gnn_resnorm_d2_gnn_r32_87d361'

def setup_inputs(seed: int=0):
    np.random.seed(seed)
    _w = jnp.asarray

    def _rec_inputs():
        import jax
        import jax.numpy as jnp
        _gk = jax.random.key(seed)
        x = -0.0003713 + 1 * jax.random.normal(jax.random.fold_in(_gk, 1), (3125, 256), jnp.float32)
        src = jax.random.randint(jax.random.fold_in(_gk, 2), (50000,), 0, 3125, jnp.int32)
        dst = jax.random.randint(jax.random.fold_in(_gk, 3), (50000,), 0, 3125, jnp.int32)
        _o = jnp.argsort(dst, stable=True)
        src = src[_o]
        dst = dst[_o]
        edge_attr_16 = 0.000398945 + 1.00003 * jax.random.normal(jax.random.fold_in(_gk, 11), (50000, 16), jnp.float32)
        edge_type_3 = jax.random.randint(jax.random.fold_in(_gk, 13), (50000,), 0, 3, jnp.int32)
        edge_type_8 = jax.random.randint(jax.random.fold_in(_gk, 14), (50000,), 0, 8, jnp.int32)
        node_type_6 = jax.random.randint(jax.random.fold_in(_gk, 15), (3125,), 0, 6, jnp.int32)
        return (x, src, dst, edge_attr_16, edge_type_3, edge_type_8, node_type_6)
    x, src, dst, edge_attr_16, edge_type_3, edge_type_8, node_type_6 = _rec_inputs()

    def _L0_gnn_setup():
        import jax, jax.numpy as jnp
        import numpy as np
        N, E = (50000, 12500)
        IN_DIM = OUT_DIM = 256
        H, DK = (8, 32)
        NT, ET = (6, 3)
        LN_EPS = 1e-05

        def _type_proj(x, node_types, W, b):
            y_all = jnp.einsum('ni,tio->tno', x, W) + b[:, None, :]
            return y_all[node_types, jnp.arange(x.shape[0])]

        def _forward(node_features, edge_index, node_types, edge_types, Wk, bk, Wq, bq, Wv, bv, relation_pri, Wa, Wm, ln_g, ln_b):
            n = node_features.shape[0]
            K = _type_proj(node_features, node_types, Wk, bk).reshape(n, H, DK)
            Q = _type_proj(node_features, node_types, Wq, bq).reshape(n, H, DK)
            V = _type_proj(node_features, node_types, Wv, bv).reshape(n, H, DK)
            src, tgt = (edge_index[0], edge_index[1])
            Ks, Qt, Vs = (K[src], Q[tgt], V[src])
            inv_sqrt_dk = 1.0 / np.sqrt(DK).astype(np.float32)
            msgs = jnp.zeros((edge_types.shape[0], H, DK), jnp.float32)
            for t in range(ET):
                mask = edge_types == t
                Ke = jnp.einsum('ehd,dk->ehk', Ks, Wa[t])
                Ve = jnp.einsum('ehd,dk->ehk', Vs, Wm[t])
                scores = jnp.sum(Ke * Qt, -1) * inv_sqrt_dk * relation_pri[t]
                scores = jnp.where(mask[:, None], scores, -jnp.inf)
                w = jax.nn.softmax(scores, axis=0)
                msgs = msgs + jnp.where(mask[:, None, None], w[..., None] * Ve, 0.0)
            agg = jax.ops.segment_sum(msgs.reshape(-1, OUT_DIM), tgt, num_segments=n)
            out = agg + node_features
            mu = jnp.mean(out, -1, keepdims=True)
            var = jnp.var(out, -1, keepdims=True)
            return (out - mu) * jax.lax.rsqrt(var + LN_EPS) * ln_g + ln_b
        key = jax.random.key(seed)
        ks = jax.random.split(key, 16)
        glorot = lambda k, shape: jax.random.normal(k, shape, jnp.float32) * np.sqrt(2.0 / (shape[-2] + shape[-1]))
        return {'node_features': jax.random.normal(ks[0], (N, IN_DIM), jnp.float32), 'edge_index': jax.random.randint(ks[1], (2, E), 0, N, jnp.int32), 'edge_features': jax.random.normal(ks[2], (E, 16), jnp.float32), 'node_types': jax.random.randint(ks[3], (N,), 0, NT, jnp.int32), 'edge_types': jax.random.randint(ks[4], (E,), 0, ET, jnp.int32), 'Wk': glorot(ks[5], (NT, IN_DIM, OUT_DIM)), 'bk': jnp.zeros((NT, OUT_DIM), jnp.float32), 'Wq': glorot(ks[6], (NT, IN_DIM, OUT_DIM)), 'bq': jnp.zeros((NT, OUT_DIM), jnp.float32), 'Wv': glorot(ks[7], (NT, IN_DIM, OUT_DIM)), 'bv': jnp.zeros((NT, OUT_DIM), jnp.float32), 'relation_pri': jnp.ones((ET, H), jnp.float32), 'Wa': glorot(ks[8], (ET, DK, DK)), 'Wm': glorot(ks[9], (ET, DK, DK)), 'ln_g': jnp.ones((OUT_DIM,), jnp.float32), 'ln_b': jnp.zeros((OUT_DIM,), jnp.float32)}
    _L0_gnn_all = _L0_gnn_setup()
    _L0_gnn_in = {k: v for k, v in _L0_gnn_all.items() if k in ('Wk', 'bk', 'Wq', 'bq', 'Wv', 'bv', 'relation_pri', 'Wa', 'Wm', 'ln_g', 'ln_b')}
    del _L0_gnn_all

    def _L1_gnn_setup():
        import jax, jax.numpy as jnp
        import numpy as np
        N = 50000
        E = 25000
        DIN = 256
        DH = 256
        DOUT = 256
        R = 8
        B = 4

        def rgcn_conv(x, src, dst, edge_type, basis, comp, root, bias):
            xb = jnp.einsum('ni,bio->nbo', x, basis)
            msg = jnp.einsum('eb,ebo->eo', comp[edge_type], xb[src])
            key = dst * R + edge_type
            cnt = jax.ops.segment_sum(jnp.ones((msg.shape[0],), x.dtype), key, num_segments=x.shape[0] * R)
            norm = 1.0 / jnp.maximum(cnt, 1.0)
            agg = jax.ops.segment_sum(msg * norm[key][:, None], dst, num_segments=x.shape[0])
            return agg + x @ root + bias
        key = jax.random.key(seed)
        ks = jax.random.split(key, 12)
        s = 0.05
        return {'x': jax.random.normal(ks[0], (N, DIN), jnp.float32), 'edge_index': jax.random.randint(ks[1], (2, E), 0, N, jnp.int64), 'edge_type': jax.random.randint(ks[2], (E,), 0, R, jnp.int64), 'basis1': jax.random.normal(ks[3], (B, DIN, DH), jnp.float32) * s, 'comp1': jax.random.normal(ks[4], (R, B), jnp.float32) * s, 'root1': jax.random.normal(ks[5], (DIN, DH), jnp.float32) * s, 'bias1': jnp.zeros((DH,), jnp.float32), 'basis2': jax.random.normal(ks[6], (B, DH, DOUT), jnp.float32) * s, 'comp2': jax.random.normal(ks[7], (R, B), jnp.float32) * s, 'root2': jax.random.normal(ks[8], (DH, DOUT), jnp.float32) * s, 'bias2': jnp.zeros((DOUT,), jnp.float32)}
    _L1_gnn_all = _L1_gnn_setup()
    _L1_gnn_in = {k: v for k, v in _L1_gnn_all.items() if k in ('basis1', 'comp1', 'root1', 'bias1', 'basis2', 'comp2', 'root2', 'bias2')}
    del _L1_gnn_all
    return {'x': x, 'src': src, 'dst': dst, 'edge_attr_16': edge_attr_16, 'edge_type_3': edge_type_3, 'edge_type_8': edge_type_8, 'node_type_6': node_type_6, 'L0_gnn_Wk': _L0_gnn_in['Wk'], 'L0_gnn_bk': _L0_gnn_in['bk'], 'L0_gnn_Wq': _L0_gnn_in['Wq'], 'L0_gnn_bq': _L0_gnn_in['bq'], 'L0_gnn_Wv': _L0_gnn_in['Wv'], 'L0_gnn_bv': _L0_gnn_in['bv'], 'L0_gnn_relation_pri': _L0_gnn_in['relation_pri'], 'L0_gnn_Wa': _L0_gnn_in['Wa'], 'L0_gnn_Wm': _L0_gnn_in['Wm'], 'L0_gnn_ln_g': _L0_gnn_in['ln_g'], 'L0_gnn_ln_b': _L0_gnn_in['ln_b'], 'L1_gnn_basis1': _L1_gnn_in['basis1'], 'L1_gnn_comp1': _L1_gnn_in['comp1'], 'L1_gnn_root1': _L1_gnn_in['root1'], 'L1_gnn_bias1': _L1_gnn_in['bias1'], 'L1_gnn_basis2': _L1_gnn_in['basis2'], 'L1_gnn_comp2': _L1_gnn_in['comp2'], 'L1_gnn_root2': _L1_gnn_in['root2'], 'L1_gnn_bias2': _L1_gnn_in['bias2']}

def reference(x, src, dst, edge_attr_16, edge_type_3, edge_type_8, node_type_6, L0_gnn_Wk, L0_gnn_bk, L0_gnn_Wq, L0_gnn_bq, L0_gnn_Wv, L0_gnn_bv, L0_gnn_relation_pri, L0_gnn_Wa, L0_gnn_Wm, L0_gnn_ln_g, L0_gnn_ln_b, L1_gnn_basis1, L1_gnn_comp1, L1_gnn_root1, L1_gnn_bias1, L1_gnn_basis2, L1_gnn_comp2, L1_gnn_root2, L1_gnn_bias2):
    import jax
    import jax.numpy as jnp

    def _L0_gnn_ref(node_features, edge_index, edge_features, node_types, edge_types, Wk, bk, Wq, bq, Wv, bv, relation_pri, Wa, Wm, ln_g, ln_b):
        import jax, jax.numpy as jnp
        import numpy as np
        N, E = (50000, 12500)
        IN_DIM = OUT_DIM = 256
        H, DK = (8, 32)
        NT, ET = (6, 3)
        LN_EPS = 1e-05

        def _type_proj(x, node_types, W, b):
            y_all = jnp.einsum('ni,tio->tno', x, W) + b[:, None, :]
            return y_all[node_types, jnp.arange(x.shape[0])]

        def _forward(node_features, edge_index, node_types, edge_types, Wk, bk, Wq, bq, Wv, bv, relation_pri, Wa, Wm, ln_g, ln_b):
            n = node_features.shape[0]
            K = _type_proj(node_features, node_types, Wk, bk).reshape(n, H, DK)
            Q = _type_proj(node_features, node_types, Wq, bq).reshape(n, H, DK)
            V = _type_proj(node_features, node_types, Wv, bv).reshape(n, H, DK)
            src, tgt = (edge_index[0], edge_index[1])
            Ks, Qt, Vs = (K[src], Q[tgt], V[src])
            inv_sqrt_dk = 1.0 / np.sqrt(DK).astype(np.float32)
            msgs = jnp.zeros((edge_types.shape[0], H, DK), jnp.float32)
            for t in range(ET):
                mask = edge_types == t
                Ke = jnp.einsum('ehd,dk->ehk', Ks, Wa[t])
                Ve = jnp.einsum('ehd,dk->ehk', Vs, Wm[t])
                scores = jnp.sum(Ke * Qt, -1) * inv_sqrt_dk * relation_pri[t]
                scores = jnp.where(mask[:, None], scores, -jnp.inf)
                w = jax.nn.softmax(scores, axis=0)
                msgs = msgs + jnp.where(mask[:, None, None], w[..., None] * Ve, 0.0)
            agg = jax.ops.segment_sum(msgs.reshape(-1, OUT_DIM), tgt, num_segments=n)
            out = agg + node_features
            mu = jnp.mean(out, -1, keepdims=True)
            var = jnp.var(out, -1, keepdims=True)
            return (out - mu) * jax.lax.rsqrt(var + LN_EPS) * ln_g + ln_b
        return _forward(node_features, edge_index, node_types, edge_types, Wk, bk, Wq, bq, Wv, bv, relation_pri, Wa, Wm, ln_g, ln_b)

    def _L1_gnn_ref(x, edge_index, edge_type, basis1, comp1, root1, bias1, basis2, comp2, root2, bias2):
        import jax, jax.numpy as jnp
        import numpy as np
        N = 50000
        E = 25000
        DIN = 256
        DH = 256
        DOUT = 256
        R = 8
        B = 4

        def rgcn_conv(x, src, dst, edge_type, basis, comp, root, bias):
            xb = jnp.einsum('ni,bio->nbo', x, basis)
            msg = jnp.einsum('eb,ebo->eo', comp[edge_type], xb[src])
            key = dst * R + edge_type
            cnt = jax.ops.segment_sum(jnp.ones((msg.shape[0],), x.dtype), key, num_segments=x.shape[0] * R)
            norm = 1.0 / jnp.maximum(cnt, 1.0)
            agg = jax.ops.segment_sum(msg * norm[key][:, None], dst, num_segments=x.shape[0])
            return agg + x @ root + bias
        src, dst = (edge_index[0], edge_index[1])
        h = rgcn_conv(x, src, dst, edge_type, basis1, comp1, root1, bias1)
        h = jax.nn.relu(h)
        out = rgcn_conv(h, src, dst, edge_type, basis2, comp2, root2, bias2)
        return out
    edge_index = jnp.stack([src, dst])
    x = _layernorm(x + _L0_gnn_ref(x, edge_index, edge_attr_16, node_type_6, edge_type_3, L0_gnn_Wk, L0_gnn_bk, L0_gnn_Wq, L0_gnn_bq, L0_gnn_Wv, L0_gnn_bv, L0_gnn_relation_pri, L0_gnn_Wa, L0_gnn_Wm, L0_gnn_ln_g, L0_gnn_ln_b), axis=-1)
    x = _layernorm(x + _L1_gnn_ref(x, edge_index, edge_type_8, L1_gnn_basis1, L1_gnn_comp1, L1_gnn_root1, L1_gnn_bias1, L1_gnn_basis2, L1_gnn_comp2, L1_gnn_root2, L1_gnn_bias2), axis=-1)
    return x

_drawn_inputs = setup_inputs


def setup_inputs(seed=0):
    import zlib

    import numpy as np

    out = dict(_drawn_inputs(seed))
    spreads = {'L0_gnn_bk': (0.0, 0.8),
     'L0_gnn_bq': (0.0, 0.8),
     'L0_gnn_bv': (0.0, 0.8),
     'L0_gnn_relation_pri': (1.0, 0.6),
     'L0_gnn_ln_g': (1.0, 0.2),
     'L0_gnn_ln_b': (0.0, 0.1),
     'L1_gnn_bias1': (0.0, 0.1),
     'L1_gnn_bias2': (0.0, 0.1)}
    factors = {'L0_gnn_Wk': 8.0, 'L0_gnn_Wq': 8.0, 'L0_gnn_Wv': 8.0, 'L0_gnn_Wa': 8.0, 'L0_gnn_Wm': 8.0}
    for name, (base, spread) in spreads.items():
        noise = np.random.default_rng([zlib.crc32(name.encode()), seed]).standard_normal(out[name].shape)
        drawn = base * np.exp(spread * noise) if base else spread * noise
        out[name] = jnp.asarray(drawn.astype(out[name].dtype))
    for name, factor in factors.items():
        out[name] = (out[name] * factor).astype(out[name].dtype)
    return out
```

```python
import concourse.bass as bass
from concourse import mybir
from contextlib import ExitStack

F32 = mybir.dt.float32
BF16 = mybir.dt.bfloat16
I32 = mybir.dt.int32
ALU = mybir.AluOpType
ACT = mybir.ActivationFunctionType
AX = mybir.AxisListType

P = 128
LN_EPS = 1e-5
NB = 3
TPG = 4
WIN = 40
NP = 125
NK = 5
SEM0 = 120
SEM0_POOL = 160
FAR = 20000


def gnn_kernel(nc, x, src, dst, edge_type_3, edge_type_8, node_type_6, Wk, bk, Wq, bq, Wv, bv,
               relation_pri, Wa, Wm, ln_g, ln_b, basis1, comp1, root1, bias1,
               basis2, comp2, root2, bias2, out):
    N, D = x.shape
    E = src.shape[0]
    NT = Wk.shape[0]
    ET, H = relation_pri.shape
    DK = D // H
    R, B = comp1.shape
    FC = D // P
    HC = H // FC
    EG = P * TPG
    NG = -(-E // EG)
    NTILE = N // NP
    NS = NTILE // NK
    SLOTS = (N + NT * (P - 1)) // P
    XR = D + 1
    NW = N + WIN
    QR = WIN * ET
    WB = WIN * B
    PASSES = -(-N // WIN)
    assert NG <= P and NTILE * NP == N and NS * NK == NTILE and NS % 2 == 1 and QR <= P and SLOTS % 2 == 0

    def scratch(name, shape):
        return nc.dram_tensor(name, shape, F32, kind="Internal").ap()

    xs = scratch("xs", [SLOTS * P, XR])
    ktab, vtab = scratch("ktab", [N, D]), scratch("vtab", [N, D])
    qtab = scratch("qtab", [NW, ET * D])
    x1tab, htab = scratch("x1tab", [N, D]), scratch("htab", [N, D])

    ctx = ExitStack()

    def sb(name, shape, dt=F32):
        return ctx.enter_context(nc.sbuf_tensor(name, shape, dt))

    def flat(ap):
        return ap.rearrange("p a b -> p (a b)")

    with ctx:
        ident = sb("ident", [P, P])
        iota_i = sb("iota_i", [P, P], I32)
        iota_f = sb("iota_f", [P, P])
        part_i = sb("part_i", [P, 1], I32)
        part_f = sb("part_f", [P, 1])
        ones = sb("ones", [P, P])
        zero1 = sb("zero1", [P, 1])
        eps1 = sb("eps1", [P, 1])
        src_i = sb("src_i", [P, NG, TPG], I32)
        cell0 = sb("cell0", [P, NG, TPG])
        local0 = sb("local0", [P, NG, TPG])
        cell = sb("cell", [P, NG, TPG])
        local = sb("local", [P, NG, TPG])
        type3 = sb("type3", [P, NG, TPG])
        type8 = sb("type8", [P, NG, TPG])
        base0 = sb("base0", [1, NG], I32)
        base = sb("base", [1, NG], I32)
        slot_type = sb("slot_type", [1, SLOTS], I32)
        n_pass = sb("n_pass", [1, 1], I32)
        score = sb("score", [P, NG, TPG, H])
        coef = sb("coef", [P, NG, TPG, 2 * B])
        count = sb("count", [R, NW])
        comp_sb = sb("comp_sb", [R, 2 * B])
        bd_a = sb("bd_a", [P, FC, ET, P])
        bd_m = sb("bd_m", [P, FC, ET, P])
        small = sb("small", [P, 512])
        acc = sb("acc", [P, FC * NW * B])
        acc_u = acc[:, 0:FC * NW * ET].rearrange("p (f c) -> p f c", f=FC)
        acc_s = acc[:, :].rearrange("p (f c) -> p f c", f=FC)
        AREA = 12000
        area = sb("area", [P, AREA])

        class Carve:

            def __init__(self, of, size):
                self.of, self.at, self.size = of, 0, size

            def __call__(self, n):
                self.at += n
                assert self.at <= self.size, (self.at, self.size)
                return self.of[:, self.at - n:self.at]

            def tiles(self, count, *shape):
                n = 1
                for d in shape:
                    n *= d
                letters = "abcd"[:len(shape)]
                sizes = dict(zip(letters, shape))
                return [self(n).rearrange(f"p ({' '.join(letters)}) -> p {' '.join(letters)}", **sizes)
                        for _ in range(count)]

        iota_c = iota_f[:, :].unsqueeze(1)

        def bc(ap, shape):
            return ap.broadcast_to(shape)

        drawn = [0]

        def fresh(name):
            drawn[0] += 1
            return f"{name}_{drawn[0]}"

        def bank(held, name, shape):
            return held.enter_context(nc.psum_tensor(fresh(name), shape, F32))

        lead = {}

        class Stage:

            def __init__(self, name):
                self.name, self.ctx, self.made, self.of_pool = name, ExitStack(), 0, 0

            def sem(self, name, ahead=0):
                self.made += 1
                assert SEM0 + self.made <= SEM0_POOL
                s = self.ctx.enter_context(nc.semaphore(fresh(f"{self.name}_{name}"), SEM0 + self.made - 1))
                lead[s.name] = ahead
                return s

            def pool_dma_sem(self, name):
                self.of_pool += 1
                return self.ctx.enter_context(nc.semaphore(fresh(f"{self.name}_{name}"), SEM0_POOL + self.of_pool - 1))

            def close(self):
                nc.all_engine_barrier(sems_to_clear=range(SEM0, SEM0 + self.made))
                if self.of_pool:
                    nc.gpsimd.dma_reset(range(SEM0_POOL, SEM0_POOL + self.of_pool))
                    nc.all_engine_barrier(sems_to_clear=range(SEM0_POOL, SEM0_POOL + self.of_pool))
                self.ctx.close()

        def after(sem, n):
            return n + 1 + lead[sem.name]

        def start(eng, *sems):
            for s in sems:
                eng.sem_inc(s, lead[s.name])

        def linker(eng, sem):
            n = [0]

            def link(ins):
                n[0] += 1
                ins.then_inc(sem, 1)
                eng.wait_ge(sem, n[0])
            return link

        st = Stage("setup")
        const_ready, rows_set, rows_in, small_in, w_in, types_in, x_in, fill_out, pad_out = (st.sem(n) for n in (
            "const_ready", "rows_set", "rows_in", "small_in", "w_in", "types_in", "x_in", "fill_out", "pad_out"))
        rows_made, turned, vec, ranked, offset, slotted, filled, zeroed, numbered = (st.sem(n) for n in (
            "rows_made", "turned", "vec", "ranked", "offset", "slotted", "filled", "zeroed", "numbered"))
        sorted_out = st.pool_dma_sem("sorted_out")
        cut = Carve(acc, FC * NW * B)
        w_all, = cut.tiles(1, FC, NT, 3 * D)
        b_all, = cut.tiles(1, NT, 3 * D)
        a_r = cut(4 * EG).bitcast(I32).rearrange("p (a e) -> p a e", a=4)
        a_f, = cut.tiles(1, 6, EG)
        wa_rows, = cut.tiles(1, ET, DK)
        pri_col, = cut.tiles(1, FC, ET)
        cut = Carve(area, AREA)
        JN = N // NP
        x_rows, = cut.tiles(1, JN, XR)
        filler = cut(XR)
        nt_i = cut(JN).bitcast(I32)
        hot6, = cut.tiles(1, NT, JN)
        rank6, = cut.tiles(1, NT, JN)
        slot_f, slot_i = cut(JN), cut(JN).bitcast(I32)
        before_p = cut(P)
        zrow = cut(ET * D)
        tri = cut(SLOTS * NT).rearrange("p (s t) -> p s t", t=NT)
        full = E // EG
        rest = E - full * EG
        FILL = (0, FAR, ET + 2, 0)
        n_small = 16 * (HC * (1 + FC * (1 + ET)) + 2)
        with ExitStack() as ps, nc.Block() as block:
            pt = [bank(ps, f"pt{a}", [P, 512]) for a in range(7)]
            p_n = bank(ps, "p_n", [P, 512])

            @block.gpsimd
            def _(pool):
                nc.gpsimd.iota(iota_i[:, :], pattern=[[1, P]], base=0, channel_multiplier=0).then_inc(const_ready, 1)
                nc.gpsimd.iota(part_i[:, :], pattern=[[0, 1]], base=0, channel_multiplier=1).then_inc(const_ready, 1)
                nc.gpsimd.iota(x_rows[0:NP, :, D:XR].bitcast(I32), pattern=[[1, JN], [0, 1]], base=0,
                               channel_multiplier=JN).then_inc(numbered, 1)
                pool.wait_ge(numbered, 1)
                pool.wait_ge(x_in, 16)
                pool.wait_ge(fill_out, 16)
                pool.wait_ge(slotted, 1)
                for j in range(JN):
                    nc.gpsimd.indirect_dma_start(
                        out=xs, out_offset=bass.IndirectOffsetOnAxis(ap=slot_i[0:NP, j:j + 1], axis=0),
                        in_=x_rows[0:NP, j, :], in_offset=None).then_inc(sorted_out, 16)
                pool.wait_ge(sorted_out, 16 * JN)

            @block.sync
            def _(sp):
                sp.dma_start(nt_i[0:NP, :], node_type_6.rearrange("(p j) -> p j", j=JN)).then_inc(types_in, 16)
                sp.dma_start(x_rows[0:NP, :, 0:D], x.rearrange("(p j) d -> p j d", j=JN)).then_inc(x_in, 16)
                sp.wait_ge(filled, 1)
                sp.dma_start(xs.rearrange("(s p) c -> p s c", p=P), bc(filler.unsqueeze(1), [P, SLOTS, XR]))\
                    .then_inc(fill_out, 16)
                sp.wait_ge(rows_set, 1)
                for a, e in enumerate((src, dst, edge_type_3, edge_type_8)):
                    sp.dma_start(a_r[0:full, a, :], e[0:full * EG].rearrange("(g c) -> g c", c=EG)).then_inc(rows_in, 16)
                    if rest:
                        sp.dma_start(a_r[full:full + 1, a, 0:rest], e[full * EG:E].unsqueeze(0)).then_inc(rows_in, 16)
                for f in range(FC):
                    for k, w in enumerate((Wk, Wv, Wq)):
                        sp.dma_start(w_all[:, f, :, k * D:(k + 1) * D],
                                     w[:, f * P:(f + 1) * P, :].rearrange("t k o -> k t o")).then_inc(w_in, 16)
                for k, b in enumerate((bk, bv, bq)):
                    sp.dma_start(b_all[:, :, k * D:(k + 1) * D], b.unsqueeze(0).broadcast_to([P, NT, D])).then_inc(w_in, 16)
                for j in range(HC):
                    js = slice(j * DK, (j + 1) * DK)
                    sp.dma_start(wa_rows[js], Wa.rearrange("t d k -> d t k")).then_inc(small_in, 16)
                    for f in range(FC):
                        h = f * HC + j
                        sp.dma_start(pri_col[js, f, :], relation_pri[:, h:h + 1].rearrange("t o -> o t").broadcast_to([DK, ET]),
                                     allow_slow_non_contiguous=True).then_inc(small_in, 16)
                        for t in range(ET):
                            sp.dma_start(bd_m[js, f, t, js], Wm[t]).then_inc(small_in, 16)
                sp.dma_start(comp_sb[:, 0:B], comp1).then_inc(small_in, 16)
                sp.dma_start(comp_sb[:, B:2 * B], comp2).then_inc(small_in, 16)
                sp.wait_ge(zeroed, 1)
                sp.dma_start(qtab[N:NW, :], zrow[0:WIN, :]).then_inc(pad_out, 16)
                sp.wait_ge(small_in, n_small)
                sp.wait_ge(w_in, 16 * 3 * (FC + 1))
                sp.wait_ge(pad_out, 16)

            @block.vector
            def _(dve):
                nc.vector.memset(filler[:, 0:D], 0.0)
                nc.vector.memset(filler[:, D:XR].bitcast(I32), FAR).then_inc(filled, 1)
                for a in range(4):
                    nc.vector.memset(a_r[:, a, :], FILL[a])
                nc.vector.memset(bd_a[:, :, :, :], 0.0)
                nc.vector.memset(bd_m[:, :, :, :], 0.0).then_inc(rows_set, 1)
                link = linker(dve, vec)
                nc.vector.memset(zrow, 0.0).then_inc(zeroed, 1)
                nc.vector.memset(eps1[:, :], LN_EPS)
                nc.vector.memset(zero1[:, :], 0.0)
                nc.vector.memset(ones[:, :], 1.0)
                dve.wait_ge(const_ready, 2)
                nc.vector.tensor_copy(iota_f[:, :], iota_i[:, :])
                link(nc.vector.tensor_copy(part_f[:, :], part_i[:, :]))
                nc.vector.tensor_scalar(ident[:, :], iota_f[:, :], part_f[:, 0:1], None, ALU.is_equal)
                link(nc.vector.tensor_scalar(before_p, iota_f[:, :], part_f[:, 0:1], None, ALU.is_gt))

                dve.wait_ge(types_in, 16)
                link(nc.vector.tensor_copy(slot_f[0:NP, :], nt_i[0:NP, :]))
                link(nc.vector.tensor_tensor(hot6[0:NP], bc(slot_f[0:NP, :].unsqueeze(1), [NP, NT, JN]),
                                             bc(iota_f[0:NP, 0:NT].unsqueeze(2), [NP, NT, JN]), ALU.is_equal))
                for t in range(NT):
                    ins = nc.vector.tensor_tensor_scan(rank6[0:NP, t, :], ones[0:NP, 0:JN], hot6[0:NP, t, :], 0.0,
                                                       ALU.mult, ALU.add)
                ins.then_inc(ranked, 1)
                dve.wait_ge(offset, 1)
                tiles_f, upto, off = small[:, 16:16 + NT], small[:, 32:32 + NT], small[:, 48:48 + NT]
                tiles_i = small[:, 64:64 + NT].bitcast(I32)
                link(nc.vector.tensor_scalar(tiles_f, p_n[:, 64:64 + NT], 1.0 / P, (P - 1) / (2.0 * P), ALU.mult, ALU.add))
                link(nc.vector.tensor_copy(tiles_i, tiles_f))
                link(nc.vector.tensor_copy(tiles_f, tiles_i))
                link(nc.vector.tensor_tensor_scan(upto, ones[:, 0:NT], tiles_f, 0.0, ALU.mult, ALU.add))
                link(nc.vector.tensor_tensor(off, upto, tiles_f, ALU.subtract))
                link(nc.vector.tensor_scalar(off, off, float(P), -1.0, ALU.mult, ALU.add))
                link(nc.vector.tensor_tensor(off[0:NP], off[0:NP], p_n[0:NP, 0:NT], ALU.add))
                link(nc.vector.tensor_tensor(rank6[0:NP], rank6[0:NP], bc(off[0:NP].unsqueeze(2), [NP, NT, JN]), ALU.add))
                link(nc.vector.tensor_tensor(rank6[0:NP], rank6[0:NP], hot6[0:NP], ALU.mult))
                link(nc.vector.tensor_reduce(slot_f[0:NP, :], rank6[0:NP].rearrange("p t j -> p j t"), AX.X, ALU.add))
                nc.vector.tensor_copy(slot_i[0:NP, :], slot_f[0:NP, :]).then_inc(slotted, 1)
                link(nc.vector.tensor_tensor(tri[0:1], bc(iota_f[0:1, 0:SLOTS].unsqueeze(2), [1, SLOTS, NT]),
                                             bc(upto[0:1].unsqueeze(1), [1, SLOTS, NT]), ALU.is_ge))
                link(nc.vector.tensor_reduce(small[0:1, 80:80 + SLOTS], tri[0:1], AX.X, ALU.add))
                link(nc.vector.tensor_scalar(small[0:1, 80:80 + SLOTS], small[0:1, 80:80 + SLOTS], float(NT - 1), None, ALU.min))
                nc.vector.tensor_copy(slot_type[:, :], small[0:1, 80:80 + SLOTS])

                dve.wait_ge(rows_in, 16 * (8 if rest else 4))
                link(nc.vector.tensor_copy(a_f[0:NG, 0:4, :], a_r[0:NG, :, :]))
                lo, hi, up = small[0:NG, 0:1], small[0:NG, 1:2], small[0:NG, 2:3]
                link(nc.vector.tensor_reduce(lo, a_f[0:NG, 1, :], AX.X, ALU.min))
                link(nc.vector.tensor_scalar(a_f[0:NG, 5, :], a_f[0:NG, 1, :], float(FAR), None, ALU.is_lt))
                link(nc.vector.tensor_tensor(a_f[0:NG, 5, :], a_f[0:NG, 5, :], a_f[0:NG, 1, :], ALU.mult))
                link(nc.vector.tensor_reduce(hi, a_f[0:NG, 5, :], AX.X, ALU.max))
                link(nc.vector.tensor_tensor(up, hi, lo, ALU.subtract))
                link(nc.vector.tensor_scalar(a_f[0:NG, 5, :], a_f[0:NG, 1, :], lo, None, ALU.subtract))
                nc.vector.scalar_tensor_tensor(a_f[0:NG, 4, :], a_f[0:NG, 5, :], float(ET), a_f[0:NG, 2, :],
                                               ALU.mult, ALU.add).then_inc(rows_made, 1)
                nc.vector.memset(count[:, :], 0.0)
                dve.wait_ge(small_in, n_small)
                for j in range(HC):
                    js = slice(j * DK, (j + 1) * DK)
                    for f in range(FC):
                        for t in range(ET):
                            ins = nc.vector.transpose(bd_a[js, f, t, js], wa_rows[js, t, :])
                link(ins)
                for f in range(FC):
                    for t in range(ET):
                        ins = nc.vector.tensor_scalar(bd_a[:, f, t, :], bd_a[:, f, t, :], pri_col[:, f, t:t + 1],
                                                      float(DK) ** -0.5, ALU.mult, ALU.mult)
                link(ins)
                dve.wait_ge(turned, 1)
                for k, to in enumerate((src_i, type3, type8, cell0, local0)):
                    ins = nc.vector.tensor_copy(to[:, :, :].rearrange("p g q -> p q g"),
                                                pt[k][:, 0:TPG * NG].rearrange("p (q g) -> p q g", q=TPG))
                link(ins)
                nc.vector.tensor_copy(base0[0:1, :], pt[5][0:1, 0:NG])
                nc.vector.tensor_copy(cell[:, :, :], cell0[:, :, :])
                nc.vector.tensor_copy(local[:, :, :], local0[:, :, :])
                link(nc.vector.tensor_reduce(small[0:1, 4:5], pt[6][0:1, 0:NG], AX.X, ALU.max))
                nc.vector.tensor_copy(base[:, :], base0[:, :])
                link(nc.vector.tensor_scalar(small[0:1, 5:6], small[0:1, 4:5], 1.0 / WIN,
                                             1.0 - (WIN - 1) / (2.0 * WIN), ALU.mult, ALU.add))
                link(nc.vector.tensor_copy(n_pass[:, :], small[0:1, 5:6]))

            @block.tensor
            def _(pe):
                pe.wait_ge(ranked, 1)
                totals = rank6[0:NP, :, JN - 1]
                nc.tensor.matmul(p_n[0:NP, 0:NT], before_p[0:NP, 0:NP], totals, start=True, stop=True)
                nc.tensor.matmul(p_n[:, 64:64 + NT], ones[0:NP, :], totals, start=True, stop=True).then_inc(offset, 1)
                pe.wait_ge(rows_made, 1)
                for k, a in enumerate((0, 2, 3, 4, 5)):
                    for q in range(TPG):
                        nc.tensor.transpose(pt[k][:, q * NG:(q + 1) * NG], a_f[0:NG, a, q * P:(q + 1) * P],
                                            ident[0:NG, 0:NG])
                nc.tensor.transpose(pt[5][0:1, 0:NG], small[0:NG, 0:1], ident[0:NG, 0:NG])
                nc.tensor.transpose(pt[6][0:1, 0:NG], small[0:NG, 2:3], ident[0:NG, 0:NG]).then_inc(turned, 1)
        st.close()

        st = Stage("proj")
        NR = 3
        xs_in = [st.sem(f"xs_in{p}") for p in range(NR)]
        xt_made, xt_copied, made, biased, qt_made, qt_copied, typed, typed_copied = (st.sem(n, a) for n, a in (
            ("xt_made", NR), ("xt_copied", 0), ("made", NR), ("biased", 1), ("qt_made", NR), ("qt_copied", 1),
            ("typed", NR), ("typed_copied", 1)))
        stored = [st.pool_dma_sem(f"stored{p}") for p in range(NR)]
        kept, asked = st.sem("kept", NR), st.sem("asked")
        cut = Carve(area, AREA)
        x_sb = cut.tiles(NR, XR)
        xt = cut.tiles(NR, FC, P)
        kv = cut.tiles(NR, 3, D)
        qt = cut.tiles(NR, FC, P)
        qs = cut.tiles(NR, ET * D)

        def slots(eng, body):
            loops = (SLOTS - 1) // NR
            with eng.Fori(0, loops) as i:
                for p in range(NR):
                    body(i * NR + p, p, i + 1)
            for n in range(loops * NR, SLOTS):
                body(n, n % NR, n // NR + 1)

        def more(n):
            return not isinstance(n, int) or n + 1 < SLOTS

        with ExitStack() as ps, nc.Block() as block:
            p_xt = bank(ps, "p_xt", [P, FC, P])
            p_kv = [bank(ps, f"p_kv{p}", [P, 2, D]) for p in range(NR)]
            p_q = bank(ps, "p_q", [P, 512])
            p_qt = bank(ps, "p_qt", [P, FC, P])
            p_ty = bank(ps, "p_ty", [P, 4, D])

            @block.sync
            def _(sp):
                def body(n, p, use):
                    sp.wait_ge(xt_made, after(xt_made, n - NR))
                    sp.wait_ge(kept, after(kept, n - NR))
                    sp.dma_start(x_sb[p], xs[bass.ds(n * P, P), :]).then_inc(xs_in[p], 16)
                slots(sp, body)

            @block.tensor
            def _(pe):
                start(pe, xt_made, made, qt_made, typed)

                def turn(p, use):
                    pe.wait_ge(xs_in[p], use * 16)
                    for f in range(FC):
                        ins = nc.tensor.transpose(p_xt[:, f, :], x_sb[p][:, f * P:(f + 1) * P], ident[:, :])
                    ins.then_inc(xt_made, 1)

                def project(n, p):
                    v = pe.value_load(slot_type[0:1, bass.ds(n, 1)], min_val=0, max_val=NT - 1)
                    pe.wait_ge(biased, after(biased, n - 1))
                    for k, to in ((0, p_kv[p][:, :, :].rearrange("p a d -> p (a d)")), (2, p_q[:, 0:D])):
                        n_col = 2 * D if k == 0 else D
                        for f in range(FC):
                            rhs = w_all[:, f, bass.ds(v, 1), k * D:k * D + n_col].rearrange("p t o -> p (t o)")
                            ins = nc.tensor.matmul(to, xt[p][:, f, :], rhs, start=(f == 0), stop=(f == FC - 1))
                    ins.then_inc(made, 1)

                def turn_queries(n, p):
                    pe.wait_ge(biased, after(biased, n))
                    pe.wait_ge(qt_copied, after(qt_copied, n - 1))
                    for f in range(FC):
                        ins = nc.tensor.transpose(p_qt[:, f, :], kv[p][:, 2, f * P:(f + 1) * P], ident[:, :])
                    ins.then_inc(qt_made, 1)

                def typed_queries(n, p):
                    pe.wait_ge(qt_copied, after(qt_copied, n))
                    pe.wait_ge(typed_copied, after(typed_copied, n - 1))
                    for t in range(ET):
                        for c in range(FC):
                            ins = nc.tensor.matmul(p_ty[:, t, c * P:(c + 1) * P], qt[p][:, c, :], bd_a[:, c, t, :],
                                                   start=True, stop=True)
                    ins.then_inc(typed, 1)

                turn(0, 1)
                pe.wait_ge(xt_copied, after(xt_copied, 0))
                project(0, 0)

                def body(n, p, use):
                    if more(n):
                        turn((p + 1) % NR, use if p < NR - 1 else use + 1)
                    turn_queries(n, p)
                    if more(n):
                        pe.wait_ge(xt_copied, after(xt_copied, n + 1))
                        project(n + 1, (p + 1) % NR)
                    typed_queries(n, p)
                slots(pe, body)

            @block.scalar
            def _(act):
                start(act, qt_copied, typed_copied)

                def copy_xt(n, p):
                    act.wait_ge(xt_made, after(xt_made, n))
                    act.wait_ge(made, after(made, n - NR))
                    nc.scalar.copy(xt[p], p_xt[:, :, :]).then_inc(xt_copied, 1)

                copy_xt(0, 0)

                def body(n, p, use):
                    if more(n):
                        copy_xt(n + 1, (p + 1) % NR)
                    act.wait_ge(qt_made, after(qt_made, n))
                    act.wait_ge(typed, after(typed, n - NR))
                    nc.scalar.copy(qt[p], p_qt[:, :, :]).then_inc(qt_copied, 1)
                    act.wait_ge(typed, after(typed, n))
                    act.wait_ge(kept, after(kept, n - NR))
                    nc.scalar.copy(qs[p].rearrange("p (t d) -> p t d", t=ET), p_ty[:, 0:ET, :]).then_inc(typed_copied, 1)
                slots(act, body)

            @block.vector
            def _(dve):
                start(dve, biased)

                def body(n, p, use):
                    v = dve.value_load(slot_type[0:1, bass.ds(n, 1)], min_val=0, max_val=NT - 1)
                    dve.wait_ge(made, after(made, n))
                    dve.wait_ge(kept, after(kept, n - NR))
                    dve.wait_ge(qt_made, after(qt_made, n - NR))
                    own = b_all[:, bass.ds(v, 1), :].rearrange("p t (a d) -> p (t a) d", d=D)
                    nc.vector.tensor_tensor(kv[p][:, 2, :], p_q[:, 0:D], own[:, 2, :], ALU.add)
                    nc.vector.tensor_tensor(kv[p][:, 0:2, :], p_kv[p][:, :, :], own[:, 0:2, :], ALU.add).then_inc(biased, 1)
                slots(dve, body)

            @block.gpsimd
            def _(pool):
                start(pool, kept)

                def body(n, p, use):
                    where = x_sb[p][:, D:XR].bitcast(I32)
                    to = bass.IndirectOffsetOnAxis(ap=where, axis=0)
                    pool.wait_ge(biased, after(biased, n))
                    pool.wait_ge(typed_copied, after(typed_copied, n))
                    pool.wait_ge(xs_in[p], use * 16)
                    pool.sem_inc(asked, 1)
                    for table, rows in ((ktab, kv[p][:, 0, :]), (vtab, kv[p][:, 1, :]), (qtab, qs[p])):
                        nc.gpsimd.indirect_dma_start(out=table, out_offset=to, in_=rows, in_offset=None,
                                                     bounds_check=N - 1, oob_is_err=False).then_inc(stored[p], 16)
                    pool.wait_ge(stored[p], use * 48)
                    pool.sem_inc(kept, 1)
                slots(pool, body)
        st.close()

        def groups(eng, body):
            with eng.Fori(0, NG // NB) as i:
                for b in range(NB):
                    body(i * NB + b, b, i + 1)
            for g in range(NG // NB * NB, NG):
                body(g, g % NB, g // NB + 1)

        def exists(g, k):
            return not isinstance(g, int) or g + k < NG

        def ring(b, k):
            return (b + k) % NB

        def gathers(pool, table, rows, idx, idx_ready, free, asked, landed):
            def body(g, b, use):
                pool.wait_ge(idx_ready, after(idx_ready, g))
                pool.wait_ge(free, after(free, g - NB))
                pool.sem_inc(asked, 1)
                for q in range(TPG):
                    nc.gpsimd.indirect_dma_start(
                        out=rows[b][:, q, :], out_offset=None, in_=table,
                        in_offset=bass.IndirectOffsetOnAxis(ap=idx[b][:, q:q + 1], axis=0),
                    ).then_inc(landed[b], 16)
            groups(pool, body)
            for b in range(NB):
                pool.wait_ge(landed[b], len(range(b, NG, NB)) * 16 * TPG)

        def group(a, g):
            return a[:, bass.ds(g, 1), :].rearrange("p g q -> p (g q)")

        def copy_indices(act, g, b, idx, idx_ready):
            nc.scalar.copy(idx[b], group(src_i, g)).then_inc(idx_ready, 1)

        def hot(to, which, g, width):
            return nc.vector.tensor_tensor(to, bc(group(which, g).unsqueeze(2), [P, TPG, width]),
                                           bc(iota_c[:, :, 0:width], [P, TPG, width]), ALU.is_equal)

        def scores(first):
            st = Stage("score")
            idx_ready, products, hots, turned, copied, expanded = (st.sem(n, a) for n, a in (
                ("idx_ready", 0), ("products", NB), ("hots", 0), ("turned", 1), ("copied", 0), ("expanded", NB)))
            scored, counted, added, summed, asked = (st.sem(n, a) for n, a in (
                ("scored", 1), ("counted", 1), ("added", 1), ("summed", 0), ("asked", 0)))
            landed = [st.pool_dma_sem(f"landed{b}") for b in range(NB)]
            q_in = [st.sem(f"q_in{b}") for b in range(NB)]
            cut = Carve(area, AREA)
            rows = cut.tiles(NB, TPG, D)
            terms = cut.tiles(NB, TPG, D)
            idx = [cut(TPG).bitcast(I32) for _ in range(NB)]
            hot_q, hot_n, hot_r = cut.tiles(NB, TPG, QR), cut.tiles(NB, TPG, WIN), cut.tiles(NB, TPG, R)
            q_win = [a[0:QR] for a in cut.tiles(NB, D)]
            hot_t = [a[0:QR] for a in cut.tiles(NB, TPG, P)]
            again = cut(TPG * H)
            with ExitStack() as ps, nc.Block() as block:
                p_t = bank(ps, "p_t", [QR, TPG, P])
                p_q = [bank(ps, f"p_qe{b}", [P, TPG, D]) for b in range(NB)]
                p_c = bank(ps, "p_c", [R, 512])

                @block.gpsimd
                def _(pool):
                    gathers(pool, ktab, rows, idx, idx_ready, products, asked, landed)

                @block.sync
                def _(sp):
                    def body(g, b, use):
                        v = sp.value_load(base[0:1, bass.ds(g, 1)], min_val=0, max_val=N)
                        sp.wait_ge(expanded, after(expanded, g - NB))
                        sp.dma_start(q_win[b], qtab.rearrange("n (t d) -> (n t) d", t=ET)[bass.ds(v * ET, QR), :])\
                            .then_inc(q_in[b], 16)
                    groups(sp, body)

                @block.scalar
                def _(act):
                    copy_indices(act, 0, 0, idx, idx_ready)
                    copy_indices(act, 1, 1, idx, idx_ready)
                    if first:
                        nc.scalar.activation(acc_u[:, :, :], bc(zero1[:, 0:1].unsqueeze(2), [P, FC, NW * ET]), ACT.Copy)

                    def body(g, b, use):
                        act.wait_ge(turned, after(turned, g))
                        act.wait_ge(expanded, after(expanded, g - NB))
                        nc.scalar.copy(hot_t[b], p_t[:, :, :]).then_inc(copied, 1)
                        if exists(g, 2):
                            act.wait_ge(products, after(products, g - 1))
                            copy_indices(act, g + 2, ring(b, 2), idx, idx_ready)
                    groups(act, body)

                @block.vector
                def _(dve):
                    start(dve, products, scored, added)

                    def hot_all(g, b):
                        hot(hot_q[b], cell, g, QR)
                        hot(hot_n[b], local, g, WIN)
                        hot(hot_r[b], type8, g, R).then_inc(hots, 1)

                    hot_all(0, 0)
                    hot_all(1, 1)

                    def body(g, b, use):
                        v = dve.value_load(base[0:1, bass.ds(g, 1)], min_val=0, max_val=N)
                        if exists(g, 2):
                            dve.wait_ge(turned, after(turned, g - 1))
                            dve.wait_ge(counted, after(counted, g - 1))
                            hot_all(g + 2, ring(b, 2))
                        dve.wait_ge(landed[b], use * 16 * TPG)
                        dve.wait_ge(expanded, after(expanded, g))
                        nc.vector.tensor_tensor(terms[b], rows[b], p_q[b][:, :, :], ALU.mult).then_inc(products, 1)
                        dve.wait_ge(counted, after(counted, g))
                        dve.wait_ge(added, after(added, g - 1))
                        here = count[:, bass.ds(v, WIN)]
                        nc.vector.tensor_tensor(here, here, p_c[:, 0:WIN], ALU.add).then_inc(added, 1)
                        dve.wait_ge(products, after(products, g))
                        dest = score[:, bass.ds(g, 1), :, :].rearrange("p g q h -> p (g q h)")
                        by_head = terms[b].rearrange("p q (h d) -> p (q h) d", d=DK)
                        if first:
                            nc.vector.tensor_reduce(dest, by_head, AX.X, ALU.add).then_inc(scored, 1)
                        else:
                            dve.wait_ge(scored, after(scored, g - 1))
                            nc.vector.tensor_reduce(again, by_head, AX.X, ALU.add).then_inc(summed, 1)
                            dve.wait_ge(summed, after(summed, g))
                            nc.vector.tensor_tensor(dest, dest, again, ALU.add).then_inc(scored, 1)
                    groups(dve, body)

                @block.tensor
                def _(pe):
                    start(pe, turned, expanded, counted)

                    def turn(b):
                        for q in range(TPG):
                            ins = nc.tensor.transpose(p_t[:, q, :], hot_q[b][:, q, :], ident[:, :])
                        ins.then_inc(turned, 1)

                    pe.wait_ge(hots, 1)
                    turn(0)

                    def body(g, b, use):
                        pe.wait_ge(copied, after(copied, g))
                        if exists(g, 1):
                            pe.wait_ge(hots, after(hots, g + 1))
                            turn(ring(b, 1))
                        pe.wait_ge(q_in[b], use * 16)
                        pe.wait_ge(products, after(products, g - NB))
                        for q in range(TPG):
                            ins = nc.tensor.matmul(p_q[b][:, q, :], hot_t[b][:, q, :], q_win[b],
                                                   start=True, stop=True)
                        ins.then_inc(expanded, 1)
                        pe.wait_ge(added, after(added, g - 1))
                        for q in range(TPG):
                            ins = nc.tensor.matmul(p_c[:, 0:WIN], hot_r[b][:, q, :], hot_n[b][:, q, :],
                                                   start=(q == 0), stop=(q == TPG - 1))
                        ins.then_inc(counted, 1)
                    groups(pe, body)
            st.close()

        def softmax():
            st = Stage("soft")
            vec, asked, served, expd = (st.sem(n) for n in ("vec", "asked", "served", "expd"))
            cut = Carve(area, AREA)
            msk = cut(NG * TPG)
            of_type = cut.tiles(ET, NG * TPG, H)
            s = score[:, :, :, :].rearrange("p g q h -> p (g q) h")
            ty = type3[:, :, :].rearrange("p g q -> p (g q)")
            TH = ET * H
            with ExitStack() as ps, nc.Block() as block:
                p_m = bank(ps, "p_m", [P, 512])
                p_b = bank(ps, "p_b", [P, 512])
                p_z = bank(ps, "p_z", [P, 512])
                part, least, diag, top, z = (small[:, k * 64:k * 64 + TH] for k in range(5))

                @block.vector
                def _(dve):
                    link = linker(dve, vec)
                    for t in range(ET):
                        link(nc.vector.tensor_scalar(msk, ty, float(t), -3.0e38, ALU.not_equal, ALU.mult))
                        link(nc.vector.tensor_tensor(of_type[t], s, bc(msk.unsqueeze(2), [P, NG * TPG, H]), ALU.add))
                        link(nc.vector.tensor_reduce(part[:, t * H:(t + 1) * H], of_type[t].rearrange("p e h -> p h e"),
                                                     AX.X, ALU.max))
                    nc.vector.tensor_scalar(count[:, :], count[:, :], 1.0, None, ALU.max).then_inc(asked, 1)
                    dve.wait_ge(served, 1)
                    link(nc.vector.tensor_reduce(least[0:TH, 0:1], p_m[0:TH, 0:P], AX.X, ALU.max))
                    nc.vector.tensor_scalar(diag[0:TH, :], ident[0:TH, 0:TH], least[0:TH, 0:1], None, ALU.mult)\
                        .then_inc(asked, 1)
                    dve.wait_ge(served, 2)
                    nc.vector.tensor_scalar(top, p_b[:, 0:TH], -1.0e37, -1.0, ALU.max, ALU.mult).then_inc(asked, 1)
                    link(nc.vector.reciprocal(count[:, :], count[:, :]))
                    dve.wait_ge(expd, 2)
                    link(nc.vector.tensor_tensor(s, of_type[0], of_type[1], ALU.add))
                    dve.wait_ge(expd, 3)
                    link(nc.vector.tensor_tensor(s, s, of_type[2], ALU.add))
                    dve.wait_ge(served, 3)
                    link(nc.vector.tensor_scalar(z, p_z[:, 0:TH], 1e-30, None, ALU.max))
                    link(nc.vector.reciprocal(z, z))
                    for f in range(FC):
                        for t in range(ET):
                            for j in range(HC):
                                js = slice(j * DK, (j + 1) * DK)
                                c = t * H + f * HC + j
                                ins = nc.vector.tensor_scalar(bd_m[js, f, t, :], bd_m[js, f, t, :], z[js, c:c + 1], None, ALU.mult)
                    link(ins)

                @block.tensor
                def _(pe):
                    pe.wait_ge(asked, 1)
                    nc.tensor.transpose(p_m[0:TH, 0:P], part, ident[:, :]).then_inc(served, 1)
                    pe.wait_ge(asked, 2)
                    nc.tensor.matmul(p_b[:, 0:TH], ones[0:TH, :], diag[0:TH, :], start=True, stop=True).then_inc(served, 1)
                    pe.wait_ge(expd, 3)
                    nc.tensor.matmul(p_z[:, 0:TH], ones[:, :], z, start=True, stop=True).then_inc(served, 1)

                @block.scalar
                def _(act):
                    act.wait_ge(asked, 3)
                    for t in range(ET):
                        for h in range(H):
                            ins = nc.scalar.activation(of_type[t][:, :, h], of_type[t][:, :, h], ACT.Exp,
                                                       bias=top[:, t * H + h:t * H + h + 1],
                                                       accum_out=z[:, t * H + h:t * H + h + 1])
                        ins.then_inc(expd, 1)
            st.close()

        def values(first):
            st = Stage("val")
            idx_ready, weighted, hots, turned, copied, summed = (st.sem(n, a) for n, a in (
                ("idx_ready", 0), ("weighted", NB), ("hots", 0), ("turned", 1), ("copied", 0), ("summed", NB)))
            found, added, picked, shared, coefs, asked, rated = (st.sem(n, a) for n, a in (
                ("found", NB), ("added", NB), ("picked", 0), ("shared", 0), ("coefs", NB), ("asked", 0), ("rated", 0)))
            landed = [st.pool_dma_sem(f"landed{b}") for b in range(NB)]
            cut = Carve(area, AREA)
            rows = cut.tiles(NB, TPG, D)
            work = cut.tiles(NB, TPG, D)
            idx = [cut(TPG).bitcast(I32) for _ in range(NB)]
            hot_q, hot_n, hot_r = cut.tiles(NB, TPG, QR), cut.tiles(NB, TPG, WIN), cut.tiles(NB, TPG, R)
            hot_t = [a[0:R] for a in cut.tiles(NB, TPG, P)]
            pick = cut.tiles(NB, TPG, WIN)
            share = [cut(TPG) for _ in range(NB)]
            tables = [a[0:R] for a in cut.tiles(NB, WIN + 2 * B)]
            again, = cut.tiles(1, TPG, 2 * B)
            with ExitStack() as ps, nc.Block() as block:
                p_t = bank(ps, "p_rt", [R, TPG, P])
                p_f = [bank(ps, f"p_f{b}", [P, TPG, WIN + 2 * B]) for b in range(NB)]
                p_u = [bank(ps, f"p_u{b}", [P, FC, 256]) for b in range(NB)]

                @block.gpsimd
                def _(pool):
                    gathers(pool, vtab, rows, idx, idx_ready, weighted, asked, landed)

                @block.scalar
                def _(act):
                    copy_indices(act, 0, 0, idx, idx_ready)
                    copy_indices(act, 1, 1, idx, idx_ready)
                    for b in range(NB):
                        nc.scalar.copy(tables[b][:, WIN:], comp_sb[:, :])

                    def prepare(g, b):
                        v = act.value_load(base[0:1, bass.ds(g, 1)], min_val=0, max_val=N)
                        act.wait_ge(found, after(found, g - NB))
                        nc.scalar.copy(tables[b][:, 0:WIN], count[:, bass.ds(v, WIN)])
                        act.wait_ge(turned, after(turned, g))
                        nc.scalar.copy(hot_t[b], p_t[:, :, :]).then_inc(copied, 1)

                    prepare(0, 0)

                    def body(g, b, use):
                        if exists(g, 1):
                            prepare(g + 1, ring(b, 1))
                        if exists(g, 2):
                            act.wait_ge(weighted, after(weighted, g - 1))
                            copy_indices(act, g + 2, ring(b, 2), idx, idx_ready)
                    groups(act, body)

                @block.vector
                def _(dve):
                    start(dve, weighted, added, coefs)

                    def hot_all(g, b):
                        hot(hot_q[b], cell, g, QR)
                        hot(hot_n[b], local, g, WIN)
                        hot(hot_r[b], type8, g, R).then_inc(hots, 1)

                    def weigh(g, b, use):
                        dve.wait_ge(landed[b], use * 16 * TPG)
                        dve.wait_ge(summed, after(summed, g - NB))
                        wt = score[:, bass.ds(g, 1), :, :].rearrange("p g q h -> p (g q h)").unsqueeze(2)
                        nc.vector.tensor_tensor(work[b].rearrange("p q (h d) -> p (q h) d", d=DK),
                                                rows[b].rearrange("p q (h d) -> p (q h) d", d=DK),
                                                bc(wt, [P, TPG * H, DK]), ALU.mult).then_inc(weighted, 1)

                    hot_all(0, 0)
                    hot_all(1, 1)
                    weigh(0, 0, 1)

                    def body(g, b, use):
                        v = dve.value_load(base[0:1, bass.ds(g, 1)], min_val=0, max_val=N)
                        if exists(g, 2):
                            dve.wait_ge(turned, after(turned, g - 1))
                            hot_all(g + 2, ring(b, 2))
                        dve.wait_ge(found, after(found, g))
                        nc.vector.tensor_tensor(pick[b], p_f[b][:, :, 0:WIN], hot_n[b], ALU.mult).then_inc(picked, 1)
                        if exists(g, 1):
                            weigh(g + 1, ring(b, 1), use if b < NB - 1 else use + 1)
                        dve.wait_ge(picked, after(picked, g))
                        nc.vector.tensor_reduce(share[b], pick[b], AX.X, ALU.add).then_inc(shared, 1)
                        dve.wait_ge(shared, after(shared, g))
                        cf = coef[:, bass.ds(g, 1), :, :].rearrange("p g q c -> p (g q) c")
                        rate = bc(share[b].unsqueeze(2), [P, TPG, 2 * B])
                        if first:
                            nc.vector.tensor_tensor(cf, p_f[b][:, :, WIN:], rate, ALU.mult).then_inc(coefs, 1)
                        else:
                            dve.wait_ge(coefs, after(coefs, g - 1))
                            nc.vector.tensor_tensor(again, p_f[b][:, :, WIN:], rate, ALU.mult).then_inc(rated, 1)
                            dve.wait_ge(rated, after(rated, g))
                            nc.vector.tensor_tensor(cf, cf, again, ALU.add).then_inc(coefs, 1)
                        dve.wait_ge(summed, after(summed, g))
                        dve.wait_ge(added, after(added, g - 1))
                        here = acc_u[:, :, bass.ds(v * ET, QR)]
                        nc.vector.tensor_tensor(here, here, p_u[b][:, :, 0:QR], ALU.add).then_inc(added, 1)
                    groups(dve, body)

                @block.tensor
                def _(pe):
                    start(pe, summed, found, turned)

                    def turn(b):
                        for q in range(TPG):
                            ins = nc.tensor.transpose(p_t[:, q, :], hot_r[b][:, q, :], ident[:, :])
                        ins.then_inc(turned, 1)

                    def find(g, b):
                        pe.wait_ge(copied, after(copied, g))
                        pe.wait_ge(coefs, after(coefs, g - NB))
                        for q in range(TPG):
                            ins = nc.tensor.matmul(p_f[b][:, q, :], hot_t[b][:, q, :], tables[b], start=True, stop=True)
                        ins.then_inc(found, 1)

                    pe.wait_ge(hots, 1)
                    turn(0)
                    find(0, 0)
                    pe.wait_ge(hots, 2)
                    turn(1)

                    def body(g, b, use):
                        pe.wait_ge(weighted, after(weighted, g))
                        pe.wait_ge(added, after(added, g - NB))
                        for f in range(FC):
                            for q in range(TPG):
                                ins = nc.tensor.matmul(p_u[b][:, f, 0:QR], work[b][:, q, f * P:(f + 1) * P],
                                                       hot_q[b][:, q, :], start=(q == 0), stop=(q == TPG - 1))
                        ins.then_inc(summed, 1)
                        if exists(g, 1):
                            find(g + 1, ring(b, 1))
                        if exists(g, 2):
                            pe.wait_ge(hots, after(hots, g + 2))
                            turn(ring(b, 2))
                    groups(pe, body)
            st.close()

        def convolve(c, table, first):
            st = Stage(f"conv{c}")
            idx_ready, hots, weights, summed, added, cleared, asked = (st.sem(n, a) for n, a in (
                ("idx_ready", 0), ("hots", 0), ("weights", 0), ("summed", NB), ("added", NB), ("cleared", 0), ("asked", 0)))
            landed = [st.pool_dma_sem(f"landed{b}") for b in range(NB)]
            half = FC * NW * B // 2
            cut = Carve(area, AREA)
            rows = cut.tiles(NB, TPG, D)
            idx = [cut(TPG).bitcast(I32) for _ in range(NB)]
            hot_n, woh = cut.tiles(NB, TPG, WIN), cut.tiles(NB, TPG, WIN, B)
            with ExitStack() as ps, nc.Block() as block:
                p_s = [bank(ps, f"p_s{b}", [P, FC, 256]) for b in range(NB)]

                @block.gpsimd
                def _(pool):
                    gathers(pool, table, rows, idx, idx_ready, summed, asked, landed)

                @block.scalar
                def _(act):
                    copy_indices(act, 0, 0, idx, idx_ready)
                    copy_indices(act, 1, 1, idx, idx_ready)
                    if first:
                        nc.scalar.activation(acc[:, half:], bc(zero1[:, 0:1], [P, half]), ACT.Copy).then_inc(cleared, 1)

                    def body(g, b, use):
                        if exists(g, 2):
                            act.wait_ge(summed, after(summed, g - 1))
                            copy_indices(act, g + 2, ring(b, 2), idx, idx_ready)
                    groups(act, body)

                @block.vector
                def _(dve):
                    start(dve, added)

                    def weigh(g, b):
                        hot(hot_n[b], local, g, WIN).then_inc(hots, 1)
                        dve.wait_ge(hots, after(hots, g))
                        cf = coef[:, bass.ds(g, 1), :, c * B:(c + 1) * B].rearrange("p g q c -> p (g q) c").unsqueeze(2)
                        nc.vector.tensor_tensor(woh[b], bc(hot_n[b].unsqueeze(3), [P, TPG, WIN, B]),
                                                bc(cf, [P, TPG, WIN, B]), ALU.mult).then_inc(weights, 1)

                    weigh(0, 0)
                    weigh(1, 1)
                    if first:
                        nc.vector.memset(acc[:, 0:half], 0.0).then_inc(cleared, 1)
                        dve.wait_ge(cleared, 2)

                    def body(g, b, use):
                        v = dve.value_load(base[0:1, bass.ds(g, 1)], min_val=0, max_val=N)
                        if exists(g, 2):
                            dve.wait_ge(summed, after(summed, g - 1))
                            weigh(g + 2, ring(b, 2))
                        dve.wait_ge(summed, after(summed, g))
                        dve.wait_ge(added, after(added, g - 1))
                        here = acc_s[:, :, bass.ds(v * B, WB)]
                        nc.vector.tensor_tensor(here, here, p_s[b][:, :, 0:WB], ALU.add).then_inc(added, 1)
                    groups(dve, body)

                @block.tensor
                def _(pe):
                    start(pe, summed)

                    def body(g, b, use):
                        pe.wait_ge(landed[b], use * 16 * TPG)
                        pe.wait_ge(weights, after(weights, g))
                        pe.wait_ge(added, after(added, g - NB))
                        for f in range(FC):
                            for q in range(TPG):
                                ins = nc.tensor.matmul(p_s[b][:, f, 0:WB], rows[b][:, q, f * P:(f + 1) * P],
                                                       woh[b][:, q, :, :].rearrange("p n c -> p (n c)"),
                                                       start=(q == 0), stop=(q == TPG - 1))
                        ins.then_inc(summed, 1)
                    groups(pe, body)
            st.close()

        def next_window():
            with nc.Block() as block:
                @block.vector
                def _(dve):
                    nc.vector.tensor_scalar(cell[:, :, :], cell[:, :, :], float(-QR), None, ALU.add)
                    nc.vector.tensor_scalar(local[:, :, :], local[:, :, :], float(-WIN), None, ALU.add)
                    nc.vector.tensor_scalar(base[:, :], base[:, :], WIN, N, ALU.add, ALU.min)

        def first_window():
            with nc.Block() as block:
                @block.vector
                def _(dve):
                    nc.vector.tensor_copy(cell[:, :, :], cell0[:, :, :])
                    nc.vector.tensor_copy(local[:, :, :], local0[:, :, :])
                    nc.vector.tensor_copy(base[:, :], base0[:, :])

        def over_windows(stage):
            stage(True)
            with nc.If(passes > 1):
                with nc.Fori(1, passes):
                    next_window()
                    stage(False)
                first_window()

        def post(kind):
            st = Stage(f"post{kind}")
            NORMS = (2, 0, 1)[kind]
            loads = 2 if kind == 2 else 1
            w_in = st.sem("w_in")
            x_in = [st.sem(f"x_in{p}") for p in range(2)]
            laid, xt_made, xt_copied, made, used, vec, done, kept, own_ready = (st.sem(n, a) for n, a in (
                ("laid", 0), ("xt_made", 0), ("xt_copied", 2), ("made", 2), ("used", 2), ("vec", 0), ("done", 2),
                ("kept", 2), ("own_ready", 0)))
            var, dev, ready, chunk = (st.sem(n) for n in ("var", "dev", "ready", "chunk"))
            stored = st.pool_dma_sem("stored")
            C = ET if kind == 0 else B
            table = (x, x1tab, htab)[kind]
            dest = (x1tab, htab, out)[kind]
            src_acc = acc_u if kind == 0 else acc_s
            cut = Carve(area, AREA)
            rows = [a[0:NP] for a in cut.tiles(2, NK, D)]
            fin = [a[0:NP] for a in cut.tiles(2, NK, D)]
            laid_sb = cut.tiles(2, FC, C, NP)
            y = cut.tiles(1, NK, D)[0][0:NP] if kind != 1 else None
            if kind == 0:
                own_b = [a[0:NP] for a in cut.tiles(2, NK, D)]
                g_bc, b_bc = (a[0:NP] for a in cut.tiles(2, D))
            if kind:
                xt_sb = cut.tiles(2, FC, NP)
                bs = cut(D)[0:1]
            res = [a[0:NP] for a in cut.tiles(2, NK, D)] if kind == 2 else rows
            stat, = (a[0:NP] for a in cut.tiles(1, NK, 6))
            mv, = (a[0:NP] for a in cut.tiles(1, NK, 2))
            rstd, shift = cut(NK)[0:NP], [cut(NK)[0:NP] for _ in range(2)]
            rs2 = [cut(NK)[0:NP] for _ in range(2)]

            def steps(eng, body):
                body(0, 0, 1)
                with eng.Fori(0, NS // 2) as i:
                    body(i * 2 + 1, 1, i + 1)
                    body(i * 2 + 2, 0, i + 2)

            def tile(s, p, k):
                return s * NK + k, (p * NK + k) % 2

            def rows_of(ap, s):
                return ap[bass.ds(s * NK * NP, NK * NP), :].rearrange("(k p) d -> p k d", p=NP)

            with ExitStack() as ps, nc.Block() as block:
                p_xt = [bank(ps, f"p_pxt{p}", [P, FC, P]) for p in range(2)]
                p_o = [bank(ps, f"p_o{p}", [P, NK + 1, D]) for p in range(2)]

                @block.sync
                def _(sp):
                    if kind == 0:
                        sp.dma_start(g_bc, ln_g.unsqueeze(0).broadcast_to([NP, D])).then_inc(w_in, 16)
                        sp.dma_start(b_bc, ln_b.unsqueeze(0).broadcast_to([NP, D])).then_inc(w_in, 16)
                    else:
                        basis, root, bias = ((basis1, root1, bias1), (basis2, root2, bias2))[kind - 1]
                        for f in range(FC):
                            sp.dma_start(bas[:, f, 0:B, :], basis[:, f * P:(f + 1) * P, :].rearrange("b k o -> k b o"))\
                                .then_inc(w_in, 16)
                            sp.dma_start(bas[:, f, B, :], root[f * P:(f + 1) * P, :]).then_inc(w_in, 16)
                        sp.dma_start(bs, bias.unsqueeze(0)).then_inc(w_in, 16)

                    def body(s, p, use):
                        sp.wait_ge(used, after(used, s - 2))
                        sp.dma_start(rows[p], rows_of(table, s)).then_inc(x_in[p], 16)
                        if kind == 2:
                            sp.dma_start(res[p], rows_of(x1tab, s)).then_inc(x_in[p], 16)
                    steps(sp, body)

                @block.scalar
                def _(act):
                    if kind:
                        start(act, xt_copied)
                    start(act, done)
                    if kind == 1:
                        start(act, used)

                    def finish(s, p):
                        act.wait_ge(kept, after(kept, s - 2))
                        if kind == 1:
                            act.wait_ge(made, after(made, s * NK + NK - 1))
                            nc.scalar.activation(fin[p], p_o[p][0:NP, 0:NK, :], ACT.Relu).then_inc(done, 1)
                            act.sem_inc(used, 1)
                        else:
                            act.wait_ge(ready, after(ready, s))
                            for k in range(NK):
                                ins = nc.scalar.activation(fin[p][:, k, :], y[:, k, :], ACT.Identity,
                                                           bias=shift[p][:, k:k + 1], scale=rs2[p][:, k:k + 1])
                            ins.then_inc(done, 1)

                    def body(s, p, use):
                        for k in range(NK):
                            n, q = tile(s, p, k)
                            act.wait_ge(made, after(made, n - 2))
                            for f in range(FC):
                                sums = src_acc[:, f, bass.ds(n * NP * C, NP * C)].rearrange("p (n c) -> p c n", c=C)
                                ins = nc.scalar.copy(laid_sb[q][:, f, :, :], sums)
                            ins.then_inc(laid, 1)
                            if kind:
                                act.wait_ge(xt_made, after(xt_made, n))
                                nc.scalar.copy(xt_sb[q], p_xt[q][:, :, 0:NP]).then_inc(xt_copied, 1)
                        for r in range(NORMS):
                            act.wait_ge(var, s * NORMS + r + 1)
                            nc.scalar.activation(mv[:, :, 1], mv[:, :, 1], ACT.Sqrt, bias=eps1[0:NP, :]).then_inc(dev, 1)
                        finish(s, p)
                    steps(act, body)

                @block.tensor
                def _(pe):
                    start(pe, made)
                    pe.wait_ge(w_in, 16 * (2 if kind == 0 else 2 * FC + 1))

                    def body(s, p, use):
                        if kind:
                            pe.wait_ge(x_in[p], use * 16 * loads)
                            pe.wait_ge(done, after(done, s - 2))
                        else:
                            pe.wait_ge(used, after(used, s - 2))
                        for k in range(NK):
                            n, q = tile(s, p, k)
                            if kind:
                                pe.wait_ge(xt_copied, after(xt_copied, n - 2))
                                for f in range(FC):
                                    ins = nc.tensor.transpose(p_xt[q][:, f, 0:NP], rows[p][:, k, f * P:(f + 1) * P],
                                                              ident[0:NP, 0:NP])
                                ins.then_inc(xt_made, 1)
                            pe.wait_ge(laid, after(laid, n))
                            to = p_o[p][0:NP, k, :]
                            if kind == 0:
                                for f in range(FC):
                                    for t in range(ET):
                                        ins = nc.tensor.matmul(to[:, f * P:(f + 1) * P], laid_sb[q][:, f, t, :],
                                                               bd_m[:, f, t, :], start=(t == 0), stop=(t == ET - 1))
                                ins.then_inc(made, 1)
                            else:
                                for f in range(FC):
                                    for c in range(B):
                                        nc.tensor.matmul(to, laid_sb[q][:, f, c, :], bas[:, f, c, :],
                                                         start=(f == 0 and c == 0), stop=False)
                                pe.wait_ge(xt_copied, after(xt_copied, n))
                                for f in range(FC):
                                    nc.tensor.matmul(to, xt_sb[q][:, f, :], bas[:, f, B, :], start=False, stop=False)
                                nc.tensor.matmul(to, ones[0:1, 0:NP], bs, start=False, stop=True).then_inc(made, 1)
                    steps(pe, body)

                if kind != 1:
                    @block.vector
                    def _(dve):
                        start(dve, used)
                        STEPS = 8 if kind == 0 else 3

                        def body(s, p, use):
                            k, r = [0], [0]

                            def link(ins):
                                k[0] += 1
                                ins.then_inc(vec, 1)
                                dve.wait_ge(vec, s * STEPS + k[0])

                            def moments():
                                for j in range(NK):
                                    ins = nc.vector.bn_stats(stat[:, j, :], y[:, j, :])
                                ins.then_inc(vec, 1)
                                k[0] += 1
                                dve.wait_ge(vec, s * STEPS + k[0])
                                dve.sem_inc(chunk, 1)
                                for j in range(NK):
                                    ins = nc.vector.bn_aggr(mv[:, j, :], stat[:, j, :])
                                ins.then_inc(var, 1)
                                r[0] += 1
                                dve.wait_ge(dev, s * NORMS + r[0])

                            dve.wait_ge(x_in[p], use * 16 * loads)
                            dve.wait_ge(made, after(made, s * NK + NK - 1))
                            dve.wait_ge(done, after(done, s - 1))
                            ins = nc.vector.tensor_tensor(y, p_o[p][0:NP, 0:NK, :], res[p], ALU.add)
                            link(ins)
                            if kind == 2:
                                dve.sem_inc(used, 1)
                            moments()
                            if kind == 0:
                                link(nc.vector.reciprocal(rstd, mv[:, :, 1]))
                                for j in range(NK):
                                    ins = nc.vector.tensor_scalar(y[:, j, :], y[:, j, :], mv[:, j, 0:1], rstd[:, j:j + 1],
                                                                  ALU.subtract, ALU.mult)
                                link(ins)
                                link(nc.vector.tensor_tensor(y, y, bc(g_bc.unsqueeze(1), [NP, NK, D]), ALU.mult))
                                dve.wait_ge(own_ready, after(own_ready, s))
                                ins = nc.vector.tensor_tensor(y, y, own_b[p], ALU.add)
                                link(ins)
                                dve.sem_inc(used, 1)
                                moments()
                            link(nc.vector.reciprocal(rs2[p], mv[:, :, 1]))
                            nc.vector.scalar_tensor_tensor(shift[p], mv[:, :, 0], -1.0, rs2[p], ALU.mult, ALU.mult)\
                                .then_inc(ready, 1)
                            dve.wait_ge(ready, after(ready, s))
                            assert k[0] == STEPS, k
                        steps(dve, body)

                @block.gpsimd
                def _(pool):
                    start(pool, kept)
                    if kind == 0:
                        pool.wait_ge(w_in, 32)

                    def store(s, p):
                        pool.wait_ge(done, after(done, s))
                        pool.dma_start(rows_of(dest, s), fin[p]).then_inc(stored, 16)
                        pool.wait_ge(stored, (s + 1) * 16)
                        pool.sem_inc(kept, 1)

                    def body(s, p, use):
                        if kind == 0:
                            pool.wait_ge(x_in[p], use * 16)
                            pool.wait_ge(used, after(used, s - 2))
                            nc.gpsimd.tensor_tensor(own_b[p], rows[p], bc(b_bc.unsqueeze(1), [NP, NK, D]), ALU.add)\
                                .then_inc(own_ready, 1)
                        store(s, p)
                    steps(pool, body)
            st.close()

        bas = score[:, :, :, :].rearrange("p g q h -> p (g q h)")[:, 0:FC * (B + 1) * D]\
            .rearrange("p (f c o) -> p f c o", f=FC, c=B + 1)
        passes = nc.values_load(n_pass[0:1, 0:1], min_val=1, max_val=PASSES)
        over_windows(scores)
        softmax()
        over_windows(values)
        post(0)
        over_windows(lambda first: convolve(0, x1tab, first))
        post(1)
        over_windows(lambda first: convolve(1, htab, first))
        post(2)


_INS = ["x", "src", "dst", "edge_type_3", "edge_type_8", "node_type_6",
        "L0_gnn_Wk", "L0_gnn_bk", "L0_gnn_Wq", "L0_gnn_bq", "L0_gnn_Wv", "L0_gnn_bv",
        "L0_gnn_relation_pri", "L0_gnn_Wa", "L0_gnn_Wm", "L0_gnn_ln_g", "L0_gnn_ln_b",
        "L1_gnn_basis1", "L1_gnn_comp1", "L1_gnn_root1", "L1_gnn_bias1",
        "L1_gnn_basis2", "L1_gnn_comp2", "L1_gnn_root2", "L1_gnn_bias2"]


def kernel(**inputs):
    import numpy as _np
    import concourse.bacc as _bacc
    from concourse import mybir as _mybir
    from concourse.bass_utils import run_bass_kernel_spmd as _run

    nc = _bacc.Bacc("TRN2", target_bir_lowering=False, num_devices=1)
    arrays, args = {}, []
    for name in _INS:
        a = _np.ascontiguousarray(inputs[name])
        arrays[f"in_{name}"] = a
        args.append(nc.dram_tensor(f"in_{name}", a.shape, _mybir.dt.from_np(a.dtype), kind="ExternalInput").ap())
    args.append(nc.dram_tensor("out_0", inputs["x"].shape, _mybir.dt.float32, kind="ExternalOutput").ap())
    gnn_kernel(nc, *args)
    r = _run(nc, [arrays], core_ids=[0])
    return r.results[0]["out_0"]
```

```python
import concourse.bass as bass
from concourse import mybir
from contextlib import ExitStack

F32 = mybir.dt.float32
BF16 = mybir.dt.bfloat16
I32 = mybir.dt.int32
ALU = mybir.AluOpType
ACT = mybir.ActivationFunctionType
AX = mybir.AxisListType

P = 128
LN_EPS = 1e-5
NB = 3
TPG = 4
WIN = 40
NP = 125
NK = 5
UNIT = 4
SEM0 = 120
SEM0_POOL = 160
FAR = 20000


def gnn_kernel(nc, x, src, dst, edge_type_3, edge_type_8, node_type_6, Wk, bk, Wq, bq, Wv, bv,
               relation_pri, Wa, Wm, ln_g, ln_b, basis1, comp1, root1, bias1,
               basis2, comp2, root2, bias2, out):
    N, D = x.shape
    E = src.shape[0]
    NT = Wk.shape[0]
    ET, H = relation_pri.shape
    DK = D // H
    R, B = comp1.shape
    FC = D // P
    HC = H // FC
    EG = P * TPG
    NG = -(-E // EG)
    NTILE = N // NP
    NS = NTILE // NK
    SLOTS = (N + NT * (P - 1)) // P
    XR = D + 1
    NW = N + WIN
    QR = WIN * ET
    WB = WIN * B
    PASSES = -(-N // WIN)
    UNITS = NG // UNIT
    assert NG > UNITS * UNIT >= NG - 3 and UNITS < NTILE
    assert NG <= P and NTILE * NP == N and NS * NK == NTILE and NS % 2 == 1 and QR <= P and SLOTS % 2 == 0

    def scratch(name, shape):
        return nc.dram_tensor(name, shape, F32, kind="Internal").ap()

    xs = scratch("xs", [SLOTS * P, XR])
    ktab, vtab = scratch("ktab", [N, D]), scratch("vtab", [N, D])
    qtab = scratch("qtab", [NW, ET * D])
    x1tab, htab = scratch("x1tab", [N, D]), scratch("htab", [N, D])

    ctx = ExitStack()

    def sb(name, shape, dt=F32):
        return ctx.enter_context(nc.sbuf_tensor(name, shape, dt))

    def flat(ap):
        return ap.rearrange("p a b -> p (a b)")

    with ctx:
        ident = sb("ident", [P, P])
        iota_i = sb("iota_i", [P, P], I32)
        iota_f = sb("iota_f", [P, P])
        part_i = sb("part_i", [P, 1], I32)
        part_f = sb("part_f", [P, 1])
        ones = sb("ones", [P, P])
        zero1 = sb("zero1", [P, 1])
        eps1 = sb("eps1", [P, 1])
        src_i = sb("src_i", [P, NG, TPG], I32)
        cell0 = sb("cell0", [P, NG, TPG])
        local0 = sb("local0", [P, NG, TPG])
        cell = sb("cell", [P, NG, TPG])
        local = sb("local", [P, NG, TPG])
        type3 = sb("type3", [P, NG, TPG])
        type8 = sb("type8", [P, NG, TPG])
        base0 = sb("base0", [1, NG], I32)
        base = sb("base", [1, NG], I32)
        slot_type = sb("slot_type", [1, SLOTS], I32)
        n_pass = sb("n_pass", [1, 1], I32)
        in_order = sb("in_order", [1, 1], I32)
        score = sb("score", [P, NG, TPG, H])
        coef = sb("coef", [P, NG, TPG, 2 * B])
        count = sb("count", [R, NW])
        comp_sb = sb("comp_sb", [R, 2 * B])
        bd_a = sb("bd_a", [P, FC, ET, P])
        bd_m = sb("bd_m", [P, FC, ET, P])
        small = sb("small", [P, 512])
        acc = sb("acc", [P, FC * NW * B])
        acc_u = acc[:, 0:FC * NW * ET].rearrange("p (f c) -> p f c", f=FC)
        acc_s = acc[:, :].rearrange("p (f c) -> p f c", f=FC)
        AREA = 12000
        area = sb("area", [P, AREA])

        class Carve:

            def __init__(self, of, size):
                self.of, self.at, self.size = of, 0, size

            def __call__(self, n):
                self.at += n
                assert self.at <= self.size, (self.at, self.size)
                return self.of[:, self.at - n:self.at]

            def tiles(self, count, *shape):
                n = 1
                for d in shape:
                    n *= d
                letters = "abcd"[:len(shape)]
                sizes = dict(zip(letters, shape))
                return [self(n).rearrange(f"p ({' '.join(letters)}) -> p {' '.join(letters)}", **sizes)
                        for _ in range(count)]

        iota_c = iota_f[:, :].unsqueeze(1)

        def bc(ap, shape):
            return ap.broadcast_to(shape)

        drawn = [0]

        def fresh(name):
            drawn[0] += 1
            return f"{name}_{drawn[0]}"

        def bank(held, name, shape):
            return held.enter_context(nc.psum_tensor(fresh(name), shape, F32))

        lead = {}

        class Stage:

            def __init__(self, name):
                self.name, self.ctx, self.made, self.of_pool = name, ExitStack(), 0, 0

            def sem(self, name, ahead=0):
                self.made += 1
                assert SEM0 + self.made <= SEM0_POOL
                s = self.ctx.enter_context(nc.semaphore(fresh(f"{self.name}_{name}"), SEM0 + self.made - 1))
                lead[s.name] = ahead
                return s

            def pool_dma_sem(self, name):
                self.of_pool += 1
                return self.ctx.enter_context(nc.semaphore(fresh(f"{self.name}_{name}"), SEM0_POOL + self.of_pool - 1))

            def close(self):
                nc.all_engine_barrier(sems_to_clear=range(SEM0, SEM0 + self.made))
                if self.of_pool:
                    nc.gpsimd.dma_reset(range(SEM0_POOL, SEM0_POOL + self.of_pool))
                    nc.all_engine_barrier(sems_to_clear=range(SEM0_POOL, SEM0_POOL + self.of_pool))
                self.ctx.close()

        def after(sem, n):
            return n + 1 + lead[sem.name]

        def start(eng, *sems):
            for s in sems:
                eng.sem_inc(s, lead[s.name])

        def linker(eng, sem):
            n = [0]

            def link(ins):
                n[0] += 1
                ins.then_inc(sem, 1)
                eng.wait_ge(sem, n[0])
            return link

        st = Stage("setup")
        const_ready, rows_set, rows_in, small_in, w_in, types_in, x_in, fill_out, pad_out = (st.sem(n) for n in (
            "const_ready", "rows_set", "rows_in", "small_in", "w_in", "types_in", "x_in", "fill_out", "pad_out"))
        rows_made, turned, vec, ranked, offset, slotted, filled, zeroed, numbered = (st.sem(n) for n in (
            "rows_made", "turned", "vec", "ranked", "offset", "slotted", "filled", "zeroed", "numbered"))
        sorted_out = st.pool_dma_sem("sorted_out")
        cut = Carve(acc, FC * NW * B)
        w_all, = cut.tiles(1, FC, NT, 3 * D)
        b_all, = cut.tiles(1, NT, 3 * D)
        a_r = cut(4 * EG).bitcast(I32).rearrange("p (a e) -> p a e", a=4)
        a_f, = cut.tiles(1, 6, EG)
        wa_rows, = cut.tiles(1, ET, DK)
        pri_col, = cut.tiles(1, FC, ET)
        cut = Carve(area, AREA)
        JN = N // NP
        x_rows, = cut.tiles(1, JN, XR)
        filler = cut(XR)
        nt_i = cut(JN).bitcast(I32)
        hot6, = cut.tiles(1, NT, JN)
        rank6, = cut.tiles(1, NT, JN)
        slot_f, slot_i = cut(JN), cut(JN).bitcast(I32)
        before_p = cut(P)
        zrow = cut(ET * D)
        finished = cut((UNITS + 1) * UNIT).bitcast(I32)
        lead_f, behind = cut(NG), cut(4)
        tri = cut(SLOTS * NT).rearrange("p (s t) -> p s t", t=NT)
        full = E // EG
        rest = E - full * EG
        FILL = (0, FAR, ET + 2, 0)
        n_small = 16 * (HC * (1 + FC * (1 + ET)) + 2)
        with ExitStack() as ps, nc.Block() as block:
            pt = [bank(ps, f"pt{a}", [P, 512]) for a in range(7)]
            p_n = bank(ps, "p_n", [P, 512])

            @block.gpsimd
            def _(pool):
                nc.gpsimd.iota(iota_i[:, :], pattern=[[1, P]], base=0, channel_multiplier=0).then_inc(const_ready, 1)
                nc.gpsimd.iota(part_i[:, :], pattern=[[0, 1]], base=0, channel_multiplier=1).then_inc(const_ready, 1)
                nc.gpsimd.iota(x_rows[0:NP, :, D:XR].bitcast(I32), pattern=[[1, JN], [0, 1]], base=0,
                               channel_multiplier=JN).then_inc(numbered, 1)
                nc.gpsimd.iota(finished.rearrange("p (u g) -> p u g", g=UNIT), pattern=[[NP, UNITS + 1], [0, UNIT]],
                               base=0, channel_multiplier=0).then_inc(const_ready, 1)
                pool.wait_ge(numbered, 1)
                pool.wait_ge(x_in, 16)
                pool.wait_ge(fill_out, 16)
                pool.wait_ge(slotted, 1)
                for j in range(JN):
                    nc.gpsimd.indirect_dma_start(
                        out=xs, out_offset=bass.IndirectOffsetOnAxis(ap=slot_i[0:NP, j:j + 1], axis=0),
                        in_=x_rows[0:NP, j, :], in_offset=None).then_inc(sorted_out, 16)
                pool.wait_ge(sorted_out, 16 * JN)

            @block.sync
            def _(sp):
                sp.dma_start(nt_i[0:NP, :], node_type_6.rearrange("(p j) -> p j", j=JN)).then_inc(types_in, 16)
                sp.dma_start(x_rows[0:NP, :, 0:D], x.rearrange("(p j) d -> p j d", j=JN)).then_inc(x_in, 16)
                sp.wait_ge(filled, 1)
                sp.dma_start(xs.rearrange("(s p) c -> p s c", p=P), bc(filler.unsqueeze(1), [P, SLOTS, XR]))\
                    .then_inc(fill_out, 16)
                sp.wait_ge(rows_set, 1)
                for a, e in enumerate((src, dst, edge_type_3, edge_type_8)):
                    sp.dma_start(a_r[0:full, a, :], e[0:full * EG].rearrange("(g c) -> g c", c=EG)).then_inc(rows_in, 16)
                    if rest:
                        sp.dma_start(a_r[full:full + 1, a, 0:rest], e[full * EG:E].unsqueeze(0)).then_inc(rows_in, 16)
                for f in range(FC):
                    for k, w in enumerate((Wk, Wv, Wq)):
                        sp.dma_start(w_all[:, f, :, k * D:(k + 1) * D],
                                     w[:, f * P:(f + 1) * P, :].rearrange("t k o -> k t o")).then_inc(w_in, 16)
                for k, b in enumerate((bk, bv, bq)):
                    sp.dma_start(b_all[:, :, k * D:(k + 1) * D], b.unsqueeze(0).broadcast_to([P, NT, D])).then_inc(w_in, 16)
                for j in range(HC):
                    js = slice(j * DK, (j + 1) * DK)
                    sp.dma_start(wa_rows[js], Wa.rearrange("t d k -> d t k")).then_inc(small_in, 16)
                    for f in range(FC):
                        h = f * HC + j
                        sp.dma_start(pri_col[js, f, :], relation_pri[:, h:h + 1].rearrange("t o -> o t").broadcast_to([DK, ET]),
                                     allow_slow_non_contiguous=True).then_inc(small_in, 16)
                        for t in range(ET):
                            sp.dma_start(bd_m[js, f, t, js], Wm[t]).then_inc(small_in, 16)
                sp.dma_start(comp_sb[:, 0:B], comp1).then_inc(small_in, 16)
                sp.dma_start(comp_sb[:, B:2 * B], comp2).then_inc(small_in, 16)
                sp.wait_ge(zeroed, 1)
                sp.dma_start(qtab[N:NW, :], zrow[0:WIN, :]).then_inc(pad_out, 16)
                sp.wait_ge(small_in, n_small)
                sp.wait_ge(w_in, 16 * 3 * (FC + 1))
                sp.wait_ge(pad_out, 16)

            @block.vector
            def _(dve):
                nc.vector.memset(filler[:, 0:D], 0.0)
                nc.vector.memset(filler[:, D:XR].bitcast(I32), FAR).then_inc(filled, 1)
                for a in range(4):
                    nc.vector.memset(a_r[:, a, :], FILL[a])
                nc.vector.memset(bd_a[:, :, :, :], 0.0)
                nc.vector.memset(bd_m[:, :, :, :], 0.0).then_inc(rows_set, 1)
                link = linker(dve, vec)
                nc.vector.memset(zrow, 0.0).then_inc(zeroed, 1)
                nc.vector.memset(eps1[:, :], LN_EPS)
                nc.vector.memset(zero1[:, :], 0.0)
                nc.vector.memset(ones[:, :], 1.0)
                dve.wait_ge(const_ready, 2)
                nc.vector.tensor_copy(iota_f[:, :], iota_i[:, :])
                link(nc.vector.tensor_copy(part_f[:, :], part_i[:, :]))
                nc.vector.tensor_scalar(ident[:, :], iota_f[:, :], part_f[:, 0:1], None, ALU.is_equal)
                link(nc.vector.tensor_scalar(before_p, iota_f[:, :], part_f[:, 0:1], None, ALU.is_gt))

                dve.wait_ge(types_in, 16)
                link(nc.vector.tensor_copy(slot_f[0:NP, :], nt_i[0:NP, :]))
                link(nc.vector.tensor_tensor(hot6[0:NP], bc(slot_f[0:NP, :].unsqueeze(1), [NP, NT, JN]),
                                             bc(iota_f[0:NP, 0:NT].unsqueeze(2), [NP, NT, JN]), ALU.is_equal))
                for t in range(NT):
                    ins = nc.vector.tensor_tensor_scan(rank6[0:NP, t, :], ones[0:NP, 0:JN], hot6[0:NP, t, :], 0.0,
                                                       ALU.mult, ALU.add)
                ins.then_inc(ranked, 1)
                dve.wait_ge(offset, 1)
                tiles_f, upto, off = small[:, 16:16 + NT], small[:, 32:32 + NT], small[:, 48:48 + NT]
                tiles_i = small[:, 64:64 + NT].bitcast(I32)
                link(nc.vector.tensor_scalar(tiles_f, p_n[:, 64:64 + NT], 1.0 / P, (P - 1) / (2.0 * P), ALU.mult, ALU.add))
                link(nc.vector.tensor_copy(tiles_i, tiles_f))
                link(nc.vector.tensor_copy(tiles_f, tiles_i))
                link(nc.vector.tensor_tensor_scan(upto, ones[:, 0:NT], tiles_f, 0.0, ALU.mult, ALU.add))
                link(nc.vector.tensor_tensor(off, upto, tiles_f, ALU.subtract))
                link(nc.vector.tensor_scalar(off, off, float(P), -1.0, ALU.mult, ALU.add))
                link(nc.vector.tensor_tensor(off[0:NP], off[0:NP], p_n[0:NP, 0:NT], ALU.add))
                link(nc.vector.tensor_tensor(rank6[0:NP], rank6[0:NP], bc(off[0:NP].unsqueeze(2), [NP, NT, JN]), ALU.add))
                link(nc.vector.tensor_tensor(rank6[0:NP], rank6[0:NP], hot6[0:NP], ALU.mult))
                link(nc.vector.tensor_reduce(slot_f[0:NP, :], rank6[0:NP].rearrange("p t j -> p j t"), AX.X, ALU.add))
                nc.vector.tensor_copy(slot_i[0:NP, :], slot_f[0:NP, :]).then_inc(slotted, 1)
                link(nc.vector.tensor_tensor(tri[0:1], bc(iota_f[0:1, 0:SLOTS].unsqueeze(2), [1, SLOTS, NT]),
                                             bc(upto[0:1].unsqueeze(1), [1, SLOTS, NT]), ALU.is_ge))
                link(nc.vector.tensor_reduce(small[0:1, 80:80 + SLOTS], tri[0:1], AX.X, ALU.add))
                link(nc.vector.tensor_scalar(small[0:1, 80:80 + SLOTS], small[0:1, 80:80 + SLOTS], float(NT - 1), None, ALU.min))
                nc.vector.tensor_copy(slot_type[:, :], small[0:1, 80:80 + SLOTS])

                dve.wait_ge(rows_in, 16 * (8 if rest else 4))
                link(nc.vector.tensor_copy(a_f[0:NG, 0:4, :], a_r[0:NG, :, :]))
                lo, hi, up = small[0:NG, 0:1], small[0:NG, 1:2], small[0:NG, 2:3]
                link(nc.vector.tensor_reduce(lo, a_f[0:NG, 1, :], AX.X, ALU.min))
                link(nc.vector.tensor_scalar(a_f[0:NG, 5, :], a_f[0:NG, 1, :], float(FAR), None, ALU.is_lt))
                link(nc.vector.tensor_tensor(a_f[0:NG, 5, :], a_f[0:NG, 5, :], a_f[0:NG, 1, :], ALU.mult))
                link(nc.vector.tensor_reduce(hi, a_f[0:NG, 5, :], AX.X, ALU.max))
                link(nc.vector.tensor_tensor(up, hi, lo, ALU.subtract))
                link(nc.vector.tensor_scalar(a_f[0:NG, 5, :], a_f[0:NG, 1, :], lo, None, ALU.subtract))
                nc.vector.scalar_tensor_tensor(a_f[0:NG, 4, :], a_f[0:NG, 5, :], float(ET), a_f[0:NG, 2, :],
                                               ALU.mult, ALU.add).then_inc(rows_made, 1)
                nc.vector.memset(count[:, :], 0.0)
                dve.wait_ge(small_in, n_small)
                for j in range(HC):
                    js = slice(j * DK, (j + 1) * DK)
                    for f in range(FC):
                        for t in range(ET):
                            ins = nc.vector.transpose(bd_a[js, f, t, js], wa_rows[js, t, :])
                link(ins)
                for f in range(FC):
                    for t in range(ET):
                        ins = nc.vector.tensor_scalar(bd_a[:, f, t, :], bd_a[:, f, t, :], pri_col[:, f, t:t + 1],
                                                      float(DK) ** -0.5, ALU.mult, ALU.mult)
                link(ins)
                dve.wait_ge(turned, 1)
                for k, to in enumerate((src_i, type3, type8, cell0, local0)):
                    ins = nc.vector.tensor_copy(to[:, :, :].rearrange("p g q -> p q g"),
                                                pt[k][:, 0:TPG * NG].rearrange("p (q g) -> p q g", q=TPG))
                link(ins)
                nc.vector.tensor_copy(base0[0:1, :], pt[5][0:1, 0:NG])
                nc.vector.tensor_copy(cell[:, :, :], cell0[:, :, :])
                nc.vector.tensor_copy(local[:, :, :], local0[:, :, :])
                link(nc.vector.tensor_reduce(small[0:1, 4:5], pt[6][0:1, 0:NG], AX.X, ALU.max))
                nc.vector.tensor_copy(base[:, :], base0[:, :])
                link(nc.vector.tensor_scalar(small[0:1, 5:6], small[0:1, 4:5], 1.0 / WIN,
                                             1.0 - (WIN - 1) / (2.0 * WIN), ALU.mult, ALU.add))
                link(nc.vector.tensor_copy(n_pass[:, :], small[0:1, 5:6]))
                dve.wait_ge(const_ready, 3)
                link(nc.vector.tensor_copy(lead_f[0:1, 1:NG], finished[0:1, 0:NG - 1]))
                nc.vector.memset(lead_f[0:1, 0:1], 0.0)
                link(nc.vector.tensor_scalar(behind[0:1, 1:2], small[0:1, 4:5], float(WIN), None, ALU.is_lt))
                link(nc.vector.tensor_tensor(lead_f[0:1, 0:NG], pt[5][0:1, 0:NG], lead_f[0:1, 0:NG], ALU.subtract))
                link(nc.vector.tensor_reduce(behind[0:1, 0:1], lead_f[0:1, 0:NG], AX.X, ALU.min))
                link(nc.vector.tensor_scalar(behind[0:1, 0:1], behind[0:1, 0:1], 0.0, None, ALU.is_ge))
                link(nc.vector.tensor_tensor(behind[0:1, 2:3], behind[0:1, 0:1], behind[0:1, 1:2], ALU.mult))
                link(nc.vector.tensor_copy(in_order[:, :], behind[0:1, 2:3]))

            @block.tensor
            def _(pe):
                pe.wait_ge(ranked, 1)
                totals = rank6[0:NP, :, JN - 1]
                nc.tensor.matmul(p_n[0:NP, 0:NT], before_p[0:NP, 0:NP], totals, start=True, stop=True)
                nc.tensor.matmul(p_n[:, 64:64 + NT], ones[0:NP, :], totals, start=True, stop=True).then_inc(offset, 1)
                pe.wait_ge(rows_made, 1)
                for k, a in enumerate((0, 2, 3, 4, 5)):
                    for q in range(TPG):
                        nc.tensor.transpose(pt[k][:, q * NG:(q + 1) * NG], a_f[0:NG, a, q * P:(q + 1) * P],
                                            ident[0:NG, 0:NG])
                nc.tensor.transpose(pt[5][0:1, 0:NG], small[0:NG, 0:1], ident[0:NG, 0:NG])
                nc.tensor.transpose(pt[6][0:1, 0:NG], small[0:NG, 2:3], ident[0:NG, 0:NG]).then_inc(turned, 1)
        st.close()

        st = Stage("proj")
        NR = 3
        xs_in = [st.sem(f"xs_in{p}") for p in range(NR)]
        xt_made, xt_copied, made, biased, qt_made, qt_copied, typed, typed_copied = (st.sem(n, a) for n, a in (
            ("xt_made", NR), ("xt_copied", 0), ("made", NR), ("biased", 1), ("qt_made", NR), ("qt_copied", 1),
            ("typed", NR), ("typed_copied", 1)))
        stored = [st.pool_dma_sem(f"stored{p}") for p in range(NR)]
        kept, asked = st.sem("kept", NR), st.sem("asked")
        cut = Carve(area, AREA)
        x_sb = cut.tiles(NR, XR)
        xt = cut.tiles(NR, FC, P)
        kv = cut.tiles(NR, 3, D)
        qt = cut.tiles(NR, FC, P)
        qs = cut.tiles(NR, ET * D)

        def slots(eng, body):
            loops = (SLOTS - 1) // NR
            with eng.Fori(0, loops) as i:
                for p in range(NR):
                    body(i * NR + p, p, i + 1)
            for n in range(loops * NR, SLOTS):
                body(n, n % NR, n // NR + 1)

        def more(n):
            return not isinstance(n, int) or n + 1 < SLOTS

        with ExitStack() as ps, nc.Block() as block:
            p_xt = bank(ps, "p_xt", [P, FC, P])
            p_kv = [bank(ps, f"p_kv{p}", [P, 2, D]) for p in range(NR)]
            p_q = bank(ps, "p_q", [P, 512])
            p_qt = bank(ps, "p_qt", [P, FC, P])
            p_ty = bank(ps, "p_ty", [P, 4, D])

            @block.sync
            def _(sp):
                def body(n, p, use):
                    sp.wait_ge(xt_made, after(xt_made, n - NR))
                    sp.wait_ge(kept, after(kept, n - NR))
                    sp.dma_start(x_sb[p], xs[bass.ds(n * P, P), :]).then_inc(xs_in[p], 16)
                slots(sp, body)

            @block.tensor
            def _(pe):
                start(pe, xt_made, made, qt_made, typed)

                def turn(p, use):
                    pe.wait_ge(xs_in[p], use * 16)
                    for f in range(FC):
                        ins = nc.tensor.transpose(p_xt[:, f, :], x_sb[p][:, f * P:(f + 1) * P], ident[:, :])
                    ins.then_inc(xt_made, 1)

                def project(n, p):
                    v = pe.value_load(slot_type[0:1, bass.ds(n, 1)], min_val=0, max_val=NT - 1)
                    pe.wait_ge(biased, after(biased, n - 1))
                    for k, to in ((0, p_kv[p][:, :, :].rearrange("p a d -> p (a d)")), (2, p_q[:, 0:D])):
                        n_col = 2 * D if k == 0 else D
                        for f in range(FC):
                            rhs = w_all[:, f, bass.ds(v, 1), k * D:k * D + n_col].rearrange("p t o -> p (t o)")
                            ins = nc.tensor.matmul(to, xt[p][:, f, :], rhs, start=(f == 0), stop=(f == FC - 1))
                    ins.then_inc(made, 1)

                def turn_queries(n, p):
                    pe.wait_ge(biased, after(biased, n))
                    pe.wait_ge(qt_copied, after(qt_copied, n - 1))
                    for f in range(FC):
                        ins = nc.tensor.transpose(p_qt[:, f, :], kv[p][:, 2, f * P:(f + 1) * P], ident[:, :])
                    ins.then_inc(qt_made, 1)

                def typed_queries(n, p):
                    pe.wait_ge(qt_copied, after(qt_copied, n))
                    pe.wait_ge(typed_copied, after(typed_copied, n - 1))
                    for t in range(ET):
                        for c in range(FC):
                            ins = nc.tensor.matmul(p_ty[:, t, c * P:(c + 1) * P], qt[p][:, c, :], bd_a[:, c, t, :],
                                                   start=True, stop=True)
                    ins.then_inc(typed, 1)

                turn(0, 1)
                pe.wait_ge(xt_copied, after(xt_copied, 0))
                project(0, 0)

                def body(n, p, use):
                    if more(n):
                        turn((p + 1) % NR, use if p < NR - 1 else use + 1)
                    turn_queries(n, p)
                    if more(n):
                        pe.wait_ge(xt_copied, after(xt_copied, n + 1))
                        project(n + 1, (p + 1) % NR)
                    typed_queries(n, p)
                slots(pe, body)

            @block.scalar
            def _(act):
                start(act, qt_copied, typed_copied)

                def copy_xt(n, p):
                    act.wait_ge(xt_made, after(xt_made, n))
                    act.wait_ge(made, after(made, n - NR))
                    nc.scalar.copy(xt[p], p_xt[:, :, :]).then_inc(xt_copied, 1)

                copy_xt(0, 0)

                def body(n, p, use):
                    if more(n):
                        copy_xt(n + 1, (p + 1) % NR)
                    act.wait_ge(qt_made, after(qt_made, n))
                    act.wait_ge(typed, after(typed, n - NR))
                    nc.scalar.copy(qt[p], p_qt[:, :, :]).then_inc(qt_copied, 1)
                    act.wait_ge(typed, after(typed, n))
                    act.wait_ge(kept, after(kept, n - NR))
                    nc.scalar.copy(qs[p].rearrange("p (t d) -> p t d", t=ET), p_ty[:, 0:ET, :]).then_inc(typed_copied, 1)
                slots(act, body)

            @block.vector
            def _(dve):
                start(dve, biased)

                def body(n, p, use):
                    v = dve.value_load(slot_type[0:1, bass.ds(n, 1)], min_val=0, max_val=NT - 1)
                    dve.wait_ge(made, after(made, n))
                    dve.wait_ge(kept, after(kept, n - NR))
                    dve.wait_ge(qt_made, after(qt_made, n - NR))
                    own = b_all[:, bass.ds(v, 1), :].rearrange("p t (a d) -> p (t a) d", d=D)
                    nc.vector.tensor_tensor(kv[p][:, 2, :], p_q[:, 0:D], own[:, 2, :], ALU.add)
                    nc.vector.tensor_tensor(kv[p][:, 0:2, :], p_kv[p][:, :, :], own[:, 0:2, :], ALU.add).then_inc(biased, 1)
                slots(dve, body)

            @block.gpsimd
            def _(pool):
                start(pool, kept)

                def body(n, p, use):
                    where = x_sb[p][:, D:XR].bitcast(I32)
                    to = bass.IndirectOffsetOnAxis(ap=where, axis=0)
                    pool.wait_ge(biased, after(biased, n))
                    pool.wait_ge(typed_copied, after(typed_copied, n))
                    pool.wait_ge(xs_in[p], use * 16)
                    pool.sem_inc(asked, 1)
                    for table, rows in ((ktab, kv[p][:, 0, :]), (vtab, kv[p][:, 1, :]), (qtab, qs[p])):
                        nc.gpsimd.indirect_dma_start(out=table, out_offset=to, in_=rows, in_offset=None,
                                                     bounds_check=N - 1, oob_is_err=False).then_inc(stored[p], 16)
                    pool.wait_ge(stored[p], use * 48)
                    pool.sem_inc(kept, 1)
                slots(pool, body)
        st.close()

        def groups(eng, body):
            with eng.Fori(0, NG // NB) as i:
                for b in range(NB):
                    body(i * NB + b, b, i + 1)
            for g in range(NG // NB * NB, NG):
                body(g, g % NB, g // NB + 1)

        def exists(g, k):
            return not isinstance(g, int) or g + k < NG

        def ring(b, k):
            return (b + k) % NB

        def units(eng, body, piece=None):
            def unit(i, first):
                for j in range(UNIT):
                    body(i * UNIT + j, j, i)
                    if piece and not first:
                        piece(i - 1, j)
            unit(0, True)
            with eng.Fori(1, UNITS) as i:
                unit(i, False)
            for g in range(UNITS * UNIT, NG):
                body(g, g % UNIT, UNITS)
            if piece:
                for n in range(UNITS - 1, NTILE):
                    for j in range(UNIT):
                        piece(n, j)

        def gathers(pool, walk, ring_size, table, rows, idx, idx_ready, free, asked, landed):
            def body(g, b, use):
                pool.wait_ge(idx_ready, after(idx_ready, g))
                pool.wait_ge(free, after(free, g - ring_size))
                pool.sem_inc(asked, 1)
                for q in range(TPG):
                    nc.gpsimd.indirect_dma_start(
                        out=rows[b][:, q, :], out_offset=None, in_=table,
                        in_offset=bass.IndirectOffsetOnAxis(ap=idx[b][:, q:q + 1], axis=0),
                    ).then_inc(landed[b], 16)
            walk(pool, body)
            for b in range(ring_size):
                pool.wait_ge(landed[b], len(range(b, NG, ring_size)) * 16 * TPG)

        def group(a, g):
            return a[:, bass.ds(g, 1), :].rearrange("p g q -> p (g q)")

        def copy_indices(act, g, b, idx, idx_ready):
            nc.scalar.copy(idx[b], group(src_i, g)).then_inc(idx_ready, 1)

        def hot(to, which, g, width):
            return nc.vector.tensor_tensor(to, bc(group(which, g).unsqueeze(2), [P, TPG, width]),
                                           bc(iota_c[:, :, 0:width], [P, TPG, width]), ALU.is_equal)

        def scores(first):
            st = Stage("score")
            idx_ready, products, hots, turned, copied, expanded = (st.sem(n, a) for n, a in (
                ("idx_ready", 0), ("products", NB), ("hots", 0), ("turned", 1), ("copied", 0), ("expanded", NB)))
            scored, counted, added, summed, asked = (st.sem(n, a) for n, a in (
                ("scored", 1), ("counted", 1), ("added", 1), ("summed", 0), ("asked", 0)))
            landed = [st.pool_dma_sem(f"landed{b}") for b in range(NB)]
            q_in = [st.sem(f"q_in{b}") for b in range(NB)]
            cut = Carve(area, AREA)
            rows = cut.tiles(NB, TPG, D)
            terms = cut.tiles(NB, TPG, D)
            idx = [cut(TPG).bitcast(I32) for _ in range(NB)]
            hot_q, hot_n, hot_r = cut.tiles(NB, TPG, QR), cut.tiles(NB, TPG, WIN), cut.tiles(NB, TPG, R)
            q_win = [a[0:QR] for a in cut.tiles(NB, D)]
            hot_t = [a[0:QR] for a in cut.tiles(NB, TPG, P)]
            again = cut(TPG * H)
            with ExitStack() as ps, nc.Block() as block:
                p_t = bank(ps, "p_t", [QR, TPG, P])
                p_q = [bank(ps, f"p_qe{b}", [P, TPG, D]) for b in range(NB)]
                p_c = bank(ps, "p_c", [R, 512])

                @block.gpsimd
                def _(pool):
                    gathers(pool, groups, NB, ktab, rows, idx, idx_ready, products, asked, landed)

                @block.sync
                def _(sp):
                    def body(g, b, use):
                        v = sp.value_load(base[0:1, bass.ds(g, 1)], min_val=0, max_val=N)
                        sp.wait_ge(expanded, after(expanded, g - NB))
                        sp.dma_start(q_win[b], qtab.rearrange("n (t d) -> (n t) d", t=ET)[bass.ds(v * ET, QR), :])\
                            .then_inc(q_in[b], 16)
                    groups(sp, body)

                @block.scalar
                def _(act):
                    copy_indices(act, 0, 0, idx, idx_ready)
                    copy_indices(act, 1, 1, idx, idx_ready)
                    if first:
                        nc.scalar.activation(acc_u[:, :, :], bc(zero1[:, 0:1].unsqueeze(2), [P, FC, NW * ET]), ACT.Copy)

                    def body(g, b, use):
                        act.wait_ge(turned, after(turned, g))
                        act.wait_ge(expanded, after(expanded, g - NB))
                        nc.scalar.copy(hot_t[b], p_t[:, :, :]).then_inc(copied, 1)
                        if exists(g, 2):
                            act.wait_ge(products, after(products, g - 1))
                            copy_indices(act, g + 2, ring(b, 2), idx, idx_ready)
                    groups(act, body)

                @block.vector
                def _(dve):
                    start(dve, products, scored, added)

                    def hot_all(g, b):
                        hot(hot_q[b], cell, g, QR)
                        hot(hot_n[b], local, g, WIN)
                        hot(hot_r[b], type8, g, R).then_inc(hots, 1)

                    hot_all(0, 0)
                    hot_all(1, 1)

                    def body(g, b, use):
                        v = dve.value_load(base[0:1, bass.ds(g, 1)], min_val=0, max_val=N)
                        if exists(g, 2):
                            dve.wait_ge(turned, after(turned, g - 1))
                            dve.wait_ge(counted, after(counted, g - 1))
                            hot_all(g + 2, ring(b, 2))
                        dve.wait_ge(landed[b], use * 16 * TPG)
                        dve.wait_ge(expanded, after(expanded, g))
                        nc.vector.tensor_tensor(terms[b], rows[b], p_q[b][:, :, :], ALU.mult).then_inc(products, 1)
                        dve.wait_ge(counted, after(counted, g))
                        dve.wait_ge(added, after(added, g - 1))
                        here = count[:, bass.ds(v, WIN)]
                        nc.vector.tensor_tensor(here, here, p_c[:, 0:WIN], ALU.add).then_inc(added, 1)
                        dve.wait_ge(products, after(products, g))
                        dest = score[:, bass.ds(g, 1), :, :].rearrange("p g q h -> p (g q h)")
                        by_head = terms[b].rearrange("p q (h d) -> p (q h) d", d=DK)
                        if first:
                            nc.vector.tensor_reduce(dest, by_head, AX.X, ALU.add).then_inc(scored, 1)
                        else:
                            dve.wait_ge(scored, after(scored, g - 1))
                            nc.vector.tensor_reduce(again, by_head, AX.X, ALU.add).then_inc(summed, 1)
                            dve.wait_ge(summed, after(summed, g))
                            nc.vector.tensor_tensor(dest, dest, again, ALU.add).then_inc(scored, 1)
                    groups(dve, body)

                @block.tensor
                def _(pe):
                    start(pe, turned, expanded, counted)

                    def turn(b):
                        for q in range(TPG):
                            ins = nc.tensor.transpose(p_t[:, q, :], hot_q[b][:, q, :], ident[:, :])
                        ins.then_inc(turned, 1)

                    pe.wait_ge(hots, 1)
                    turn(0)

                    def body(g, b, use):
                        pe.wait_ge(copied, after(copied, g))
                        if exists(g, 1):
                            pe.wait_ge(hots, after(hots, g + 1))
                            turn(ring(b, 1))
                        pe.wait_ge(q_in[b], use * 16)
                        pe.wait_ge(products, after(products, g - NB))
                        for q in range(TPG):
                            ins = nc.tensor.matmul(p_q[b][:, q, :], hot_t[b][:, q, :], q_win[b],
                                                   start=True, stop=True)
                        ins.then_inc(expanded, 1)
                        pe.wait_ge(added, after(added, g - 1))
                        for q in range(TPG):
                            ins = nc.tensor.matmul(p_c[:, 0:WIN], hot_r[b][:, q, :], hot_n[b][:, q, :],
                                                   start=(q == 0), stop=(q == TPG - 1))
                        ins.then_inc(counted, 1)
                    groups(pe, body)
            st.close()

        def softmax():
            st = Stage("soft")
            vec, asked, served, expd = (st.sem(n) for n in ("vec", "asked", "served", "expd"))
            cut = Carve(area, AREA)
            msk = cut(NG * TPG)
            of_type = cut.tiles(ET, NG * TPG, H)
            s = score[:, :, :, :].rearrange("p g q h -> p (g q) h")
            ty = type3[:, :, :].rearrange("p g q -> p (g q)")
            TH = ET * H
            with ExitStack() as ps, nc.Block() as block:
                p_m = bank(ps, "p_m", [P, 512])
                p_b = bank(ps, "p_b", [P, 512])
                p_z = bank(ps, "p_z", [P, 512])
                part, least, diag, top, z = (small[:, k * 64:k * 64 + TH] for k in range(5))

                @block.vector
                def _(dve):
                    link = linker(dve, vec)
                    for t in range(ET):
                        link(nc.vector.tensor_scalar(msk, ty, float(t), -3.0e38, ALU.not_equal, ALU.mult))
                        link(nc.vector.tensor_tensor(of_type[t], s, bc(msk.unsqueeze(2), [P, NG * TPG, H]), ALU.add))
                        link(nc.vector.tensor_reduce(part[:, t * H:(t + 1) * H], of_type[t].rearrange("p e h -> p h e"),
                                                     AX.X, ALU.max))
                    nc.vector.tensor_scalar(count[:, :], count[:, :], 1.0, None, ALU.max).then_inc(asked, 1)
                    dve.wait_ge(served, 1)
                    link(nc.vector.tensor_reduce(least[0:TH, 0:1], p_m[0:TH, 0:P], AX.X, ALU.max))
                    nc.vector.tensor_scalar(diag[0:TH, :], ident[0:TH, 0:TH], least[0:TH, 0:1], None, ALU.mult)\
                        .then_inc(asked, 1)
                    dve.wait_ge(served, 2)
                    nc.vector.tensor_scalar(top, p_b[:, 0:TH], -1.0e37, -1.0, ALU.max, ALU.mult).then_inc(asked, 1)
                    link(nc.vector.reciprocal(count[:, :], count[:, :]))
                    dve.wait_ge(expd, 2)
                    link(nc.vector.tensor_tensor(s, of_type[0], of_type[1], ALU.add))
                    dve.wait_ge(expd, 3)
                    link(nc.vector.tensor_tensor(s, s, of_type[2], ALU.add))
                    dve.wait_ge(served, 3)
                    link(nc.vector.tensor_scalar(z, p_z[:, 0:TH], 1e-30, None, ALU.max))
                    link(nc.vector.reciprocal(z, z))
                    for f in range(FC):
                        for t in range(ET):
                            for j in range(HC):
                                js = slice(j * DK, (j + 1) * DK)
                                c = t * H + f * HC + j
                                ins = nc.vector.tensor_scalar(bd_m[js, f, t, :], bd_m[js, f, t, :], z[js, c:c + 1], None, ALU.mult)
                    link(ins)

                @block.tensor
                def _(pe):
                    pe.wait_ge(asked, 1)
                    nc.tensor.transpose(p_m[0:TH, 0:P], part, ident[:, :]).then_inc(served, 1)
                    pe.wait_ge(asked, 2)
                    nc.tensor.matmul(p_b[:, 0:TH], ones[0:TH, :], diag[0:TH, :], start=True, stop=True).then_inc(served, 1)
                    pe.wait_ge(expd, 3)
                    nc.tensor.matmul(p_z[:, 0:TH], ones[:, :], z, start=True, stop=True).then_inc(served, 1)

                @block.scalar
                def _(act):
                    act.wait_ge(asked, 3)
                    for t in range(ET):
                        for h in range(H):
                            ins = nc.scalar.activation(of_type[t][:, :, h], of_type[t][:, :, h], ACT.Exp,
                                                       bias=top[:, t * H + h:t * H + h + 1],
                                                       accum_out=z[:, t * H + h:t * H + h + 1])
                        ins.then_inc(expd, 1)
            st.close()

        class Finish:

            def __init__(self, st, ps, cut, kind):
                self.kind = kind
                self.table, self.dest = (x, x1tab, htab)[kind], (x1tab, htab, out)[kind]
                self.C = ET if kind == 0 else B
                self.rows, self.fin, self.y = (cut(D)[0:NP] for _ in range(3))
                self.res = cut(D)[0:NP] if kind == 2 else self.rows
                self.laid_sb, = cut.tiles(1, FC, self.C, NP)
                self.stat, self.mv = cut(6)[0:NP], cut(2)[0:NP]
                self.rstd, self.shift, self.rs2 = (cut(1)[0:NP] for _ in range(3))
                if kind == 0:
                    self.g_bc, self.b_bc = cut(D)[0:NP], cut(D)[0:NP]
                else:
                    self.xt_sb, = cut.tiles(1, FC, NP)
                    self.bs = cut(D)[0:1]
                    self.p_xt = bank(ps, "p_fx", [P, FC, P])
                self.p_o = bank(ps, "p_fo", [P, 2, D])
                self.w_in, self.x_in, self.stored = st.sem("w_in"), st.sem("x_in"), st.sem("stored")
                self.laid, self.xt_made, self.xt_copied, self.made, self.used, self.done = (st.sem(n, a) for n, a in (
                    ("laid", 0), ("xt_made", 1), ("xt_copied", 0), ("made", 1), ("used", 1), ("done", 1)))
                self.vec, self.chunk, self.var, self.dev, self.ready = (st.sem(n) for n in (
                    "vec", "chunk", "var", "dev", "ready"))

            def load_weights(self, sp):
                if self.kind == 0:
                    sp.dma_start(self.g_bc, ln_g.unsqueeze(0).broadcast_to([NP, D])).then_inc(self.w_in, 16)
                    sp.dma_start(self.b_bc, ln_b.unsqueeze(0).broadcast_to([NP, D])).then_inc(self.w_in, 16)
                    return
                basis, root, bias = ((basis1, root1, bias1), (basis2, root2, bias2))[self.kind - 1]
                for f in range(FC):
                    sp.dma_start(bas[:, f, 0:B, :], basis[:, f * P:(f + 1) * P, :].rearrange("b k o -> k b o"))\
                        .then_inc(self.w_in, 16)
                    sp.dma_start(bas[:, f, B, :], root[f * P:(f + 1) * P, :]).then_inc(self.w_in, 16)
                sp.dma_start(self.bs, bias.unsqueeze(0)).then_inc(self.w_in, 16)

            def sync(self, sp):
                self.load_weights(sp)

                def load(n):
                    sp.wait_ge(self.used, after(self.used, n - 1))
                    at = bass.ds(n * NP, NP)
                    sp.dma_start(self.rows, self.table[at, :]).then_inc(self.x_in, 16)
                    if self.kind == 2:
                        sp.dma_start(self.res, x1tab[at, :]).then_inc(self.x_in, 16)

                def store(n):
                    sp.wait_ge(self.done, after(self.done, n))
                    sp.dma_start(self.dest[bass.ds(n * NP, NP), :], self.fin).then_inc(self.stored, 16)

                load(0)
                with sp.Fori(1, NTILE) as n:
                    load(n)
                    store(n - 1)
                store(NTILE - 1)
                sp.wait_ge(self.stored, NTILE * 16)

            def rows_landed(self, eng, n):
                eng.wait_ge(self.x_in, (n + 1) * 16 * (2 if self.kind == 2 else 1))

            def start_scalar(self, act):
                start(act, self.done)
                if self.kind == 1:
                    start(act, self.used)

            def scalar(self, act, n, j, added):
                if j == 0:
                    act.wait_ge(added, after(added, min((n + 1) * UNIT, NG - 1) if isinstance(n, int) else (n + 1) * UNIT))
                    act.wait_ge(self.made, after(self.made, n - 1))
                    of = (acc_u if self.kind == 0 else acc_s)
                    for f in range(FC):
                        sums = of[:, f, bass.ds(n * NP * self.C, NP * self.C)].rearrange("p (n c) -> p c n", c=self.C)
                        ins = nc.scalar.copy(self.laid_sb[:, f, :, :], sums)
                    ins.then_inc(self.laid, 1)
                    if self.kind:
                        act.wait_ge(self.xt_made, after(self.xt_made, n))
                        nc.scalar.copy(self.xt_sb, self.p_xt[:, :, 0:NP]).then_inc(self.xt_copied, 1)
                if j == 3:
                    for r in range((2, 0, 1)[self.kind]):
                        act.wait_ge(self.var, n * (2, 0, 1)[self.kind] + r + 1)
                        nc.scalar.activation(self.mv[:, 1:2], self.mv[:, 1:2], ACT.Sqrt, bias=eps1[0:NP, :])\
                            .then_inc(self.dev, 1)
                    if isinstance(n, int):
                        if n:
                            act.wait_ge(self.stored, n * 16)
                    else:
                        act.wait_ge(self.stored, n * 16)
                    if self.kind == 1:
                        act.wait_ge(self.made, after(self.made, n))
                        nc.scalar.activation(self.fin, self.p_o[0:NP, 0, :], ACT.Relu).then_inc(self.done, 1)
                        act.sem_inc(self.used, 1)
                    else:
                        act.wait_ge(self.ready, n + 1)
                        nc.scalar.activation(self.fin, self.y, ACT.Identity, bias=self.shift, scale=self.rs2)\
                            .then_inc(self.done, 1)

            def start_tensor(self, pe):
                start(pe, self.made)
                if self.kind:
                    start(pe, self.xt_made)
                pe.wait_ge(self.w_in, 16 * (2 if self.kind == 0 else 2 * FC + 1))

            def tensor(self, pe, n, j):
                if self.kind and j == 0:
                    self.rows_landed(pe, n)
                    pe.wait_ge(self.made, after(self.made, n - 1))
                    for f in range(FC):
                        ins = nc.tensor.transpose(self.p_xt[:, f, 0:NP], self.rows[:, f * P:(f + 1) * P],
                                                  ident[0:NP, 0:NP])
                    ins.then_inc(self.xt_made, 1)
                if j == 1:
                    pe.wait_ge(self.laid, after(self.laid, n))
                    pe.wait_ge(self.done, after(self.done, n - 1))
                    to = self.p_o[0:NP, 0, :]
                    if self.kind == 0:
                        for f in range(FC):
                            for t in range(ET):
                                ins = nc.tensor.matmul(to[:, f * P:(f + 1) * P], self.laid_sb[:, f, t, :], bd_m[:, f, t, :],
                                                       start=(t == 0), stop=(t == ET - 1))
                        ins.then_inc(self.made, 1)
                    else:
                        for f in range(FC):
                            for c in range(B):
                                nc.tensor.matmul(to, self.laid_sb[:, f, c, :], bas[:, f, c, :],
                                                 start=(f == 0 and c == 0), stop=False)
                        pe.wait_ge(self.xt_copied, after(self.xt_copied, n))
                        for f in range(FC):
                            nc.tensor.matmul(to, self.xt_sb[:, f, :], bas[:, f, B, :], start=False, stop=False)
                        nc.tensor.matmul(to, ones[0:1, 0:NP], self.bs, start=False, stop=True).then_inc(self.made, 1)

            def start_vector(self, dve):
                if self.kind != 1:
                    start(dve, self.used)

            def vector(self, dve, n, j):
                if self.kind == 1 or j < 2:
                    return
                NORMS, STEPS = (2, 0, 1)[self.kind], (8, 0, 3)[self.kind]
                if j == 2:
                    self.k, self.r = 0, 0

                def link(ins):
                    self.k += 1
                    ins.then_inc(self.vec, 1)
                    dve.wait_ge(self.vec, n * STEPS + self.k)

                def moments():
                    link(nc.vector.bn_stats(self.stat, self.y))
                    dve.sem_inc(self.chunk, 1)
                    nc.vector.bn_aggr(self.mv, self.stat).then_inc(self.var, 1)

                def deviation():
                    self.r += 1
                    dve.wait_ge(self.dev, n * NORMS + self.r)

                if j == 2:
                    self.rows_landed(dve, n)
                    dve.wait_ge(self.made, after(self.made, n))
                    dve.wait_ge(self.done, after(self.done, n - 1))
                    link(nc.vector.tensor_tensor(self.y, self.p_o[0:NP, 0, :], self.res, ALU.add))
                    if self.kind == 2:
                        dve.sem_inc(self.used, 1)
                    moments()
                if j == 3:
                    if self.kind == 0:
                        deviation()
                        link(nc.vector.reciprocal(self.rstd, self.mv[:, 1:2]))
                        link(nc.vector.scalar_tensor_tensor(self.y, self.y, self.mv[:, 0:1], self.g_bc, ALU.subtract, ALU.mult))
                        link(nc.vector.scalar_tensor_tensor(self.y, self.y, self.rstd, self.rows, ALU.mult, ALU.add))
                        dve.sem_inc(self.used, 1)
                        link(nc.vector.tensor_tensor(self.y, self.y, self.b_bc, ALU.add))
                        moments()
                    deviation()
                    link(nc.vector.reciprocal(self.rs2, self.mv[:, 1:2]))
                    ins = nc.vector.scalar_tensor_tensor(self.shift, self.mv[:, 0:1], -1.0, self.rs2, ALU.mult, ALU.mult)
                    ins.then_inc(self.ready, 1)
                    dve.wait_ge(self.ready, n + 1)
                    assert self.k == STEPS, self.k

        def values(first, finish=False):
            st = Stage("val")
            idx_ready, weighted, hots, turned, copied, summed = (st.sem(n, a) for n, a in (
                ("idx_ready", 0), ("weighted", UNIT), ("hots", 0), ("turned", 1), ("copied", 0), ("summed", 2)))
            found, added, picked, shared, coefs, asked, rated = (st.sem(n, a) for n, a in (
                ("found", 2), ("added", 2), ("picked", 0), ("shared", 0), ("coefs", 2), ("asked", 0), ("rated", 0)))
            landed = [st.pool_dma_sem(f"landed{b}") for b in range(UNIT)]
            cut = Carve(area, AREA)
            rows = cut.tiles(UNIT, TPG, D)
            work = cut.tiles(2, TPG, D)
            idx = [cut(TPG).bitcast(I32) for _ in range(UNIT)]
            hot_q, hot_n, hot_r = cut.tiles(UNIT, TPG, QR), cut.tiles(UNIT, TPG, WIN), cut.tiles(UNIT, TPG, R)
            pick = cut.tiles(2, TPG, WIN)
            share = [cut(TPG) for _ in range(2)]
            again, = cut.tiles(1, TPG, 2 * B)
            tables = [a[0:R] for a in cut.tiles(2, WIN + 2 * B)]
            cut = Carve(acc[:, FC * NW * ET:], FC * NW * (B - ET))
            hot_t = [a[0:R] for a in cut.tiles(2, TPG, P)]
            with ExitStack() as ps, nc.Block() as block:
                p_t = bank(ps, "p_rt", [R, TPG, P])
                p_f = [bank(ps, f"p_f{b}", [P, TPG, WIN + 2 * B]) for b in range(2)]
                p_u = [bank(ps, f"p_u{b}", [P, FC, 256]) for b in range(2)]
                tile = Finish(st, ps, cut, 0) if finish else None

                def pieces(of):
                    return of if finish else None

                if finish:
                    block.sync(tile.sync)

                @block.gpsimd
                def _(pool):
                    gathers(pool, lambda eng, body: units(eng, lambda g, j, i: body(g, j, i + 1)), UNIT, vtab, rows, idx, idx_ready, weighted, asked, landed)

                @block.scalar
                def _(act):
                    copy_indices(act, 0, 0, idx, idx_ready)
                    copy_indices(act, 1, 1, idx, idx_ready)
                    if finish:
                        tile.start_scalar(act)
                    for b in range(2):
                        nc.scalar.copy(tables[b][:, WIN:], comp_sb[:, :])

                    def prepare(g, b):
                        v = act.value_load(base[0:1, bass.ds(g, 1)], min_val=0, max_val=N)
                        act.wait_ge(found, after(found, g - 2))
                        nc.scalar.copy(tables[b % 2][:, 0:WIN], count[:, bass.ds(v, WIN)])
                        act.wait_ge(turned, after(turned, g))
                        nc.scalar.copy(hot_t[b % 2], p_t[:, :, :]).then_inc(copied, 1)

                    prepare(0, 0)

                    def body(g, b, i):
                        if exists(g, 1):
                            prepare(g + 1, (b + 1) % UNIT)
                        if exists(g, 2):
                            act.wait_ge(weighted, after(weighted, g - 2))
                            copy_indices(act, g + 2, (b + 2) % UNIT, idx, idx_ready)
                    units(act, body, pieces(lambda n, j: tile.scalar(act, n, j, added)))

                @block.vector
                def _(dve):
                    start(dve, weighted, added, coefs)
                    if finish:
                        tile.start_vector(dve)

                    def hot_all(g, b):
                        hot(hot_q[b], cell, g, QR)
                        hot(hot_n[b], local, g, WIN)
                        hot(hot_r[b], type8, g, R).then_inc(hots, 1)

                    def weigh(g, b, i):
                        dve.wait_ge(landed[b], (i + 1) * 16 * TPG)
                        dve.wait_ge(summed, after(summed, g - 2))
                        wt = score[:, bass.ds(g, 1), :, :].rearrange("p g q h -> p (g q h)").unsqueeze(2)
                        nc.vector.tensor_tensor(work[b % 2].rearrange("p q (h d) -> p (q h) d", d=DK),
                                                rows[b].rearrange("p q (h d) -> p (q h) d", d=DK),
                                                bc(wt, [P, TPG * H, DK]), ALU.mult).then_inc(weighted, 1)

                    hot_all(0, 0)
                    hot_all(1, 1)
                    weigh(0, 0, 0)

                    def body(g, b, i):
                        v = dve.value_load(base[0:1, bass.ds(g, 1)], min_val=0, max_val=N)
                        c = b % 2
                        if exists(g, 2):
                            hot_all(g + 2, (b + 2) % UNIT)
                        dve.wait_ge(found, after(found, g))
                        nc.vector.tensor_tensor(pick[c], p_f[c][:, :, 0:WIN], hot_n[b], ALU.mult).then_inc(picked, 1)
                        if exists(g, 1):
                            weigh(g + 1, (b + 1) % UNIT, i if b < UNIT - 1 else i + 1)
                        dve.wait_ge(picked, after(picked, g))
                        nc.vector.tensor_reduce(share[c], pick[c], AX.X, ALU.add).then_inc(shared, 1)
                        dve.wait_ge(shared, after(shared, g))
                        cf = coef[:, bass.ds(g, 1), :, :].rearrange("p g q c -> p (g q) c")
                        rate = bc(share[c].unsqueeze(2), [P, TPG, 2 * B])
                        if first:
                            nc.vector.tensor_tensor(cf, p_f[c][:, :, WIN:], rate, ALU.mult).then_inc(coefs, 1)
                        else:
                            dve.wait_ge(coefs, after(coefs, g - 1))
                            nc.vector.tensor_tensor(again, p_f[c][:, :, WIN:], rate, ALU.mult).then_inc(rated, 1)
                            dve.wait_ge(rated, after(rated, g))
                            nc.vector.tensor_tensor(cf, cf, again, ALU.add).then_inc(coefs, 1)
                        dve.wait_ge(summed, after(summed, g))
                        dve.wait_ge(added, after(added, g - 1))
                        here = acc_u[:, :, bass.ds(v * ET, QR)]
                        nc.vector.tensor_tensor(here, here, p_u[c][:, :, 0:QR], ALU.add).then_inc(added, 1)
                    units(dve, body, pieces(lambda n, j: tile.vector(dve, n, j)))

                @block.tensor
                def _(pe):
                    start(pe, summed, found, turned)
                    if finish:
                        tile.start_tensor(pe)

                    def turn(b):
                        for q in range(TPG):
                            ins = nc.tensor.transpose(p_t[:, q, :], hot_r[b][:, q, :], ident[:, :])
                        ins.then_inc(turned, 1)

                    def find(g, b):
                        pe.wait_ge(copied, after(copied, g))
                        pe.wait_ge(coefs, after(coefs, g - 2))
                        for q in range(TPG):
                            ins = nc.tensor.matmul(p_f[b % 2][:, q, :], hot_t[b % 2][:, q, :], tables[b % 2],
                                                   start=True, stop=True)
                        ins.then_inc(found, 1)

                    pe.wait_ge(hots, 1)
                    turn(0)
                    find(0, 0)
                    pe.wait_ge(hots, 2)
                    turn(1)

                    def body(g, b, i):
                        pe.wait_ge(weighted, after(weighted, g))
                        pe.wait_ge(added, after(added, g - 2))
                        for f in range(FC):
                            for q in range(TPG):
                                ins = nc.tensor.matmul(p_u[b % 2][:, f, 0:QR], work[b % 2][:, q, f * P:(f + 1) * P],
                                                       hot_q[b][:, q, :], start=(q == 0), stop=(q == TPG - 1))
                        ins.then_inc(summed, 1)
                        if exists(g, 1):
                            find(g + 1, (b + 1) % UNIT)
                        if exists(g, 2):
                            pe.wait_ge(hots, after(hots, g + 2))
                            turn((b + 2) % UNIT)
                    units(pe, body, pieces(lambda n, j: tile.tensor(pe, n, j)))
            st.close()

        def convolve(c, table, first, finish=False):
            st = Stage(f"conv{c}")
            idx_ready, hots, weights, summed, added, cleared, asked = (st.sem(n, a) for n, a in (
                ("idx_ready", 0), ("hots", 0), ("weights", 0), ("summed", UNIT), ("added", UNIT), ("cleared", 0), ("asked", 0)))
            landed = [st.pool_dma_sem(f"landed{b}") for b in range(UNIT)]
            half = FC * NW * B // 2
            cut = Carve(area, AREA)
            rows = cut.tiles(UNIT, TPG, D)
            idx = [cut(TPG).bitcast(I32) for _ in range(UNIT)]
            hot_n, woh = cut.tiles(UNIT, TPG, WIN), cut.tiles(UNIT, TPG, WIN, B)
            with ExitStack() as ps, nc.Block() as block:
                p_s = [bank(ps, f"p_s{b}", [P, FC, 256]) for b in range(UNIT)]

                tile = Finish(st, ps, cut, c + 1) if finish else None

                def pieces(of):
                    return of if finish else None

                if finish:
                    block.sync(tile.sync)

                @block.gpsimd
                def _(pool):
                    gathers(pool, lambda eng, body: units(eng, lambda g, j, i: body(g, j, i + 1)), UNIT, table, rows, idx, idx_ready, summed, asked, landed)

                @block.scalar
                def _(act):
                    copy_indices(act, 0, 0, idx, idx_ready)
                    copy_indices(act, 1, 1, idx, idx_ready)
                    if first:
                        nc.scalar.activation(acc[:, half:], bc(zero1[:, 0:1], [P, half]), ACT.Copy).then_inc(cleared, 1)

                    if finish:
                        tile.start_scalar(act)

                    def body(g, b, i):
                        if exists(g, 2):
                            act.wait_ge(summed, after(summed, g - 2))
                            copy_indices(act, g + 2, (b + 2) % UNIT, idx, idx_ready)
                    units(act, body, pieces(lambda n, j: tile.scalar(act, n, j, added)))

                @block.vector
                def _(dve):
                    start(dve, added)
                    if finish:
                        tile.start_vector(dve)

                    def weigh(g, b):
                        hot(hot_n[b], local, g, WIN).then_inc(hots, 1)
                        dve.wait_ge(hots, after(hots, g))
                        cf = coef[:, bass.ds(g, 1), :, c * B:(c + 1) * B].rearrange("p g q c -> p (g q) c").unsqueeze(2)
                        nc.vector.tensor_tensor(woh[b], bc(hot_n[b].unsqueeze(3), [P, TPG, WIN, B]),
                                                bc(cf, [P, TPG, WIN, B]), ALU.mult).then_inc(weights, 1)

                    weigh(0, 0)
                    weigh(1, 1)
                    if first:
                        nc.vector.memset(acc[:, 0:half], 0.0).then_inc(cleared, 1)
                        dve.wait_ge(cleared, 2)

                    def body(g, b, i):
                        v = dve.value_load(base[0:1, bass.ds(g, 1)], min_val=0, max_val=N)
                        if exists(g, 2):
                            weigh(g + 2, (b + 2) % UNIT)
                        dve.wait_ge(summed, after(summed, g))
                        dve.wait_ge(added, after(added, g - 1))
                        here = acc_s[:, :, bass.ds(v * B, WB)]
                        nc.vector.tensor_tensor(here, here, p_s[b][:, :, 0:WB], ALU.add).then_inc(added, 1)
                    units(dve, body, pieces(lambda n, j: tile.vector(dve, n, j)))

                @block.tensor
                def _(pe):
                    start(pe, summed)
                    if finish:
                        tile.start_tensor(pe)

                    def body(g, b, i):
                        pe.wait_ge(landed[b], (i + 1) * 16 * TPG)
                        pe.wait_ge(weights, after(weights, g))
                        pe.wait_ge(added, after(added, g - UNIT))
                        for f in range(FC):
                            for q in range(TPG):
                                ins = nc.tensor.matmul(p_s[b][:, f, 0:WB], rows[b][:, q, f * P:(f + 1) * P],
                                                       woh[b][:, q, :, :].rearrange("p n c -> p (n c)"),
                                                       start=(q == 0), stop=(q == TPG - 1))
                        ins.then_inc(summed, 1)
                    units(pe, body, pieces(lambda n, j: tile.tensor(pe, n, j)))
            st.close()

        def next_window():
            with nc.Block() as block:
                @block.vector
                def _(dve):
                    nc.vector.tensor_scalar(cell[:, :, :], cell[:, :, :], float(-QR), None, ALU.add)
                    nc.vector.tensor_scalar(local[:, :, :], local[:, :, :], float(-WIN), None, ALU.add)
                    nc.vector.tensor_scalar(base[:, :], base[:, :], WIN, N, ALU.add, ALU.min)

        def first_window():
            with nc.Block() as block:
                @block.vector
                def _(dve):
                    nc.vector.tensor_copy(cell[:, :, :], cell0[:, :, :])
                    nc.vector.tensor_copy(local[:, :, :], local0[:, :, :])
                    nc.vector.tensor_copy(base[:, :], base0[:, :])

        def over_windows(stage):
            stage(True)
            with nc.If(passes > 1):
                with nc.Fori(1, passes):
                    next_window()
                    stage(False)
                first_window()

        def clear(sums):
            with nc.Block() as block:
                @block.vector
                def _(dve):
                    nc.vector.memset(sums, 0.0)

        def all_windows(stage):
            with nc.Fori(0, passes):
                stage(False)
                next_window()
            first_window()

        def post(kind):
            st = Stage(f"post{kind}")
            NORMS = (2, 0, 1)[kind]
            loads = 2 if kind == 2 else 1
            w_in = st.sem("w_in")
            x_in = [st.sem(f"x_in{p}") for p in range(2)]
            laid, xt_made, xt_copied, made, used, vec, done, kept, own_ready = (st.sem(n, a) for n, a in (
                ("laid", 0), ("xt_made", 0), ("xt_copied", 2), ("made", 2), ("used", 2), ("vec", 0), ("done", 2),
                ("kept", 2), ("own_ready", 0)))
            var, dev, ready, chunk = (st.sem(n) for n in ("var", "dev", "ready", "chunk"))
            stored = st.pool_dma_sem("stored")
            C = ET if kind == 0 else B
            table = (x, x1tab, htab)[kind]
            dest = (x1tab, htab, out)[kind]
            src_acc = acc_u if kind == 0 else acc_s
            cut = Carve(area, AREA)
            rows = [a[0:NP] for a in cut.tiles(2, NK, D)]
            fin = [a[0:NP] for a in cut.tiles(2, NK, D)]
            laid_sb = cut.tiles(2, FC, C, NP)
            y = cut.tiles(1, NK, D)[0][0:NP] if kind != 1 else None
            if kind == 0:
                own_b = [a[0:NP] for a in cut.tiles(2, NK, D)]
                g_bc, b_bc = (a[0:NP] for a in cut.tiles(2, D))
            if kind:
                xt_sb = cut.tiles(2, FC, NP)
                bs = cut(D)[0:1]
            res = [a[0:NP] for a in cut.tiles(2, NK, D)] if kind == 2 else rows
            stat, = (a[0:NP] for a in cut.tiles(1, NK, 6))
            mv, = (a[0:NP] for a in cut.tiles(1, NK, 2))
            rstd, shift = cut(NK)[0:NP], [cut(NK)[0:NP] for _ in range(2)]
            rs2 = [cut(NK)[0:NP] for _ in range(2)]

            def steps(eng, body):
                body(0, 0, 1)
                with eng.Fori(0, NS // 2) as i:
                    body(i * 2 + 1, 1, i + 1)
                    body(i * 2 + 2, 0, i + 2)

            def tile(s, p, k):
                return s * NK + k, (p * NK + k) % 2

            def rows_of(ap, s):
                return ap[bass.ds(s * NK * NP, NK * NP), :].rearrange("(k p) d -> p k d", p=NP)

            with ExitStack() as ps, nc.Block() as block:
                p_xt = [bank(ps, f"p_pxt{p}", [P, FC, P]) for p in range(2)]
                p_o = [bank(ps, f"p_o{p}", [P, NK + 1, D]) for p in range(2)]

                @block.sync
                def _(sp):
                    if kind == 0:
                        sp.dma_start(g_bc, ln_g.unsqueeze(0).broadcast_to([NP, D])).then_inc(w_in, 16)
                        sp.dma_start(b_bc, ln_b.unsqueeze(0).broadcast_to([NP, D])).then_inc(w_in, 16)
                    else:
                        basis, root, bias = ((basis1, root1, bias1), (basis2, root2, bias2))[kind - 1]
                        for f in range(FC):
                            sp.dma_start(bas[:, f, 0:B, :], basis[:, f * P:(f + 1) * P, :].rearrange("b k o -> k b o"))\
                                .then_inc(w_in, 16)
                            sp.dma_start(bas[:, f, B, :], root[f * P:(f + 1) * P, :]).then_inc(w_in, 16)
                        sp.dma_start(bs, bias.unsqueeze(0)).then_inc(w_in, 16)

                    def body(s, p, use):
                        sp.wait_ge(used, after(used, s - 2))
                        sp.dma_start(rows[p], rows_of(table, s)).then_inc(x_in[p], 16)
                        if kind == 2:
                            sp.dma_start(res[p], rows_of(x1tab, s)).then_inc(x_in[p], 16)
                    steps(sp, body)

                @block.scalar
                def _(act):
                    if kind:
                        start(act, xt_copied)
                    start(act, done)
                    if kind == 1:
                        start(act, used)

                    def finish(s, p):
                        act.wait_ge(kept, after(kept, s - 2))
                        if kind == 1:
                            act.wait_ge(made, after(made, s * NK + NK - 1))
                            nc.scalar.activation(fin[p], p_o[p][0:NP, 0:NK, :], ACT.Relu).then_inc(done, 1)
                            act.sem_inc(used, 1)
                        else:
                            act.wait_ge(ready, after(ready, s))
                            for k in range(NK):
                                ins = nc.scalar.activation(fin[p][:, k, :], y[:, k, :], ACT.Identity,
                                                           bias=shift[p][:, k:k + 1], scale=rs2[p][:, k:k + 1])
                            ins.then_inc(done, 1)

                    def body(s, p, use):
                        for k in range(NK):
                            n, q = tile(s, p, k)
                            act.wait_ge(made, after(made, n - 2))
                            for f in range(FC):
                                sums = src_acc[:, f, bass.ds(n * NP * C, NP * C)].rearrange("p (n c) -> p c n", c=C)
                                ins = nc.scalar.copy(laid_sb[q][:, f, :, :], sums)
                            ins.then_inc(laid, 1)
                            if kind:
                                act.wait_ge(xt_made, after(xt_made, n))
                                nc.scalar.copy(xt_sb[q], p_xt[q][:, :, 0:NP]).then_inc(xt_copied, 1)
                        for r in range(NORMS):
                            act.wait_ge(var, s * NORMS + r + 1)
                            nc.scalar.activation(mv[:, :, 1], mv[:, :, 1], ACT.Sqrt, bias=eps1[0:NP, :]).then_inc(dev, 1)
                        finish(s, p)
                    steps(act, body)

                @block.tensor
                def _(pe):
                    start(pe, made)
                    pe.wait_ge(w_in, 16 * (2 if kind == 0 else 2 * FC + 1))

                    def body(s, p, use):
                        if kind:
                            pe.wait_ge(x_in[p], use * 16 * loads)
                            pe.wait_ge(done, after(done, s - 2))
                        else:
                            pe.wait_ge(used, after(used, s - 2))
                        for k in range(NK):
                            n, q = tile(s, p, k)
                            if kind:
                                pe.wait_ge(xt_copied, after(xt_copied, n - 2))
                                for f in range(FC):
                                    ins = nc.tensor.transpose(p_xt[q][:, f, 0:NP], rows[p][:, k, f * P:(f + 1) * P],
                                                              ident[0:NP, 0:NP])
                                ins.then_inc(xt_made, 1)
                            pe.wait_ge(laid, after(laid, n))
                            to = p_o[p][0:NP, k, :]
                            if kind == 0:
                                for f in range(FC):
                                    for t in range(ET):
                                        ins = nc.tensor.matmul(to[:, f * P:(f + 1) * P], laid_sb[q][:, f, t, :],
                                                               bd_m[:, f, t, :], start=(t == 0), stop=(t == ET - 1))
                                ins.then_inc(made, 1)
                            else:
                                for f in range(FC):
                                    for c in range(B):
                                        nc.tensor.matmul(to, laid_sb[q][:, f, c, :], bas[:, f, c, :],
                                                         start=(f == 0 and c == 0), stop=False)
                                pe.wait_ge(xt_copied, after(xt_copied, n))
                                for f in range(FC):
                                    nc.tensor.matmul(to, xt_sb[q][:, f, :], bas[:, f, B, :], start=False, stop=False)
                                nc.tensor.matmul(to, ones[0:1, 0:NP], bs, start=False, stop=True).then_inc(made, 1)
                    steps(pe, body)

                if kind != 1:
                    @block.vector
                    def _(dve):
                        start(dve, used)
                        STEPS = 8 if kind == 0 else 3

                        def body(s, p, use):
                            k, r = [0], [0]

                            def link(ins):
                                k[0] += 1
                                ins.then_inc(vec, 1)
                                dve.wait_ge(vec, s * STEPS + k[0])

                            def moments():
                                for j in range(NK):
                                    ins = nc.vector.bn_stats(stat[:, j, :], y[:, j, :])
                                ins.then_inc(vec, 1)
                                k[0] += 1
                                dve.wait_ge(vec, s * STEPS + k[0])
                                dve.sem_inc(chunk, 1)
                                for j in range(NK):
                                    ins = nc.vector.bn_aggr(mv[:, j, :], stat[:, j, :])
                                ins.then_inc(var, 1)
                                r[0] += 1
                                dve.wait_ge(dev, s * NORMS + r[0])

                            dve.wait_ge(x_in[p], use * 16 * loads)
                            dve.wait_ge(made, after(made, s * NK + NK - 1))
                            dve.wait_ge(done, after(done, s - 1))
                            ins = nc.vector.tensor_tensor(y, p_o[p][0:NP, 0:NK, :], res[p], ALU.add)
                            link(ins)
                            if kind == 2:
                                dve.sem_inc(used, 1)
                            moments()
                            if kind == 0:
                                link(nc.vector.reciprocal(rstd, mv[:, :, 1]))
                                for j in range(NK):
                                    ins = nc.vector.tensor_scalar(y[:, j, :], y[:, j, :], mv[:, j, 0:1], rstd[:, j:j + 1],
                                                                  ALU.subtract, ALU.mult)
                                link(ins)
                                link(nc.vector.tensor_tensor(y, y, bc(g_bc.unsqueeze(1), [NP, NK, D]), ALU.mult))
                                dve.wait_ge(own_ready, after(own_ready, s))
                                ins = nc.vector.tensor_tensor(y, y, own_b[p], ALU.add)
                                link(ins)
                                dve.sem_inc(used, 1)
                                moments()
                            link(nc.vector.reciprocal(rs2[p], mv[:, :, 1]))
                            nc.vector.scalar_tensor_tensor(shift[p], mv[:, :, 0], -1.0, rs2[p], ALU.mult, ALU.mult)\
                                .then_inc(ready, 1)
                            dve.wait_ge(ready, after(ready, s))
                            assert k[0] == STEPS, k
                        steps(dve, body)

                @block.gpsimd
                def _(pool):
                    start(pool, kept)
                    if kind == 0:
                        pool.wait_ge(w_in, 32)

                    def store(s, p):
                        pool.wait_ge(done, after(done, s))
                        pool.dma_start(rows_of(dest, s), fin[p]).then_inc(stored, 16)
                        pool.wait_ge(stored, (s + 1) * 16)
                        pool.sem_inc(kept, 1)

                    def body(s, p, use):
                        if kind == 0:
                            pool.wait_ge(x_in[p], use * 16)
                            pool.wait_ge(used, after(used, s - 2))
                            nc.gpsimd.tensor_tensor(own_b[p], rows[p], bc(b_bc.unsqueeze(1), [NP, NK, D]), ALU.add)\
                                .then_inc(own_ready, 1)
                        store(s, p)
                    steps(pool, body)
            st.close()

        bas = score[:, :, :, :].rearrange("p g q h -> p (g q h)")[:, 0:FC * (B + 1) * D]\
            .rearrange("p (f c o) -> p f c o", f=FC, c=B + 1)
        passes = nc.values_load(n_pass[0:1, 0:1], min_val=1, max_val=PASSES)
        ordered = nc.values_load(in_order[0:1, 0:1], min_val=0, max_val=1)
        over_windows(scores)
        softmax()
        with nc.If(ordered > 0):
            values(True, finish=True)
            convolve(0, x1tab, True, finish=True)
            convolve(1, htab, True, finish=True)
        with nc.Else():
            clear(coef[:, :, :, :].rearrange("p g q c -> p (g q c)"))
            all_windows(values)
            post(0)
            clear(acc[:, :])
            all_windows(lambda first: convolve(0, x1tab, first))
            post(1)
            clear(acc[:, :])
            all_windows(lambda first: convolve(1, htab, first))
            post(2)


_INS = ["x", "src", "dst", "edge_type_3", "edge_type_8", "node_type_6",
        "L0_gnn_Wk", "L0_gnn_bk", "L0_gnn_Wq", "L0_gnn_bq", "L0_gnn_Wv", "L0_gnn_bv",
        "L0_gnn_relation_pri", "L0_gnn_Wa", "L0_gnn_Wm", "L0_gnn_ln_g", "L0_gnn_ln_b",
        "L1_gnn_basis1", "L1_gnn_comp1", "L1_gnn_root1", "L1_gnn_bias1",
        "L1_gnn_basis2", "L1_gnn_comp2", "L1_gnn_root2", "L1_gnn_bias2"]


def kernel(**inputs):
    import numpy as _np
    import concourse.bacc as _bacc
    from concourse import mybir as _mybir
    from concourse.bass_utils import run_bass_kernel_spmd as _run

    nc = _bacc.Bacc("TRN2", target_bir_lowering=False, num_devices=1)
    arrays, args = {}, []
    for name in _INS:
        a = _np.ascontiguousarray(inputs[name])
        arrays[f"in_{name}"] = a
        args.append(nc.dram_tensor(f"in_{name}", a.shape, _mybir.dt.from_np(a.dtype), kind="ExternalInput").ap())
    args.append(nc.dram_tensor("out_0", inputs["x"].shape, _mybir.dt.float32, kind="ExternalOutput").ap())
    gnn_kernel(nc, *args)
    r = _run(nc, [arrays], core_ids=[0])
    return r.results[0]["out_0"]
```

```python
import concourse.bass as bass
from concourse import mybir
from contextlib import ExitStack

F32 = mybir.dt.float32
BF16 = mybir.dt.bfloat16
I32 = mybir.dt.int32
ALU = mybir.AluOpType
ACT = mybir.ActivationFunctionType
AX = mybir.AxisListType

P = 128
LN_EPS = 1e-5
NB = 3
TPG = 4
WIN = 40
NP = 125
NK = 5
UNIT = 4
SEM0 = 120
SEM0_POOL = 160
FAR = 20000


def gnn_kernel(nc, x, src, dst, edge_type_3, edge_type_8, node_type_6, Wk, bk, Wq, bq, Wv, bv,
               relation_pri, Wa, Wm, ln_g, ln_b, basis1, comp1, root1, bias1,
               basis2, comp2, root2, bias2, out):
    N, D = x.shape
    E = src.shape[0]
    NT = Wk.shape[0]
    ET, H = relation_pri.shape
    DK = D // H
    R, B = comp1.shape
    FC = D // P
    HC = H // FC
    EG = P * TPG
    NG = -(-E // EG)
    NTILE = N // NP
    NS = NTILE // NK
    SLOTS = (N + NT * (P - 1)) // P
    XR = D + 1
    NW = N + WIN
    QK = TPG * R
    QR = WIN * ET
    WB = WIN * B
    PASSES = -(-N // WIN)
    UNITS = NG // UNIT
    assert NG > UNITS * UNIT >= NG - 3 and UNITS < NTILE
    assert NG <= P and NTILE * NP == N and NS * NK == NTILE and NS % 2 == 1 and QR <= P and SLOTS % 2 == 0

    def scratch(name, shape):
        return nc.dram_tensor(name, shape, F32, kind="Internal").ap()

    xs = scratch("xs", [SLOTS * P, XR])
    ktab, vtab = scratch("ktab", [N, D]), scratch("vtab", [N, D])
    qtab = scratch("qtab", [NW, ET * D])
    x1tab, htab = scratch("x1tab", [N, D]), scratch("htab", [N, D])

    ctx = ExitStack()

    def sb(name, shape, dt=F32):
        return ctx.enter_context(nc.sbuf_tensor(name, shape, dt))

    def flat(ap):
        return ap.rearrange("p a b -> p (a b)")

    with ctx:
        ident = sb("ident", [P, P])
        iota_i = sb("iota_i", [P, P], I32)
        iota_f = sb("iota_f", [P, P])
        part_i = sb("part_i", [P, 1], I32)
        part_f = sb("part_f", [P, 1])
        ones = sb("ones", [P, P])
        zero1 = sb("zero1", [P, 1])
        eps1 = sb("eps1", [P, 1])
        src_i = sb("src_i", [P, NG + 1, TPG], I32)
        cell0 = sb("cell0", [P, NG, TPG])
        local0 = sb("local0", [P, NG, TPG])
        cell = sb("cell", [P, NG, TPG])
        local = sb("local", [P, NG, TPG])
        type3 = sb("type3", [P, NG, TPG])
        type8 = sb("type8", [P, NG, TPG])
        base0 = sb("base0", [1, NG], I32)
        base = sb("base", [1, NG], I32)
        slot_type = sb("slot_type", [1, SLOTS], I32)
        n_pass = sb("n_pass", [1, 1], I32)
        in_order = sb("in_order", [1, 1], I32)
        score = sb("score", [P, NG, TPG, H])
        coef = sb("coef", [P, NG, TPG, 2 * B])
        count = sb("count", [QK, NW])
        comp_sb = sb("comp_sb", [QK, 2 * B])
        of_tile = sb("of_tile", [QK, TPG])
        relations = sb("relations", [P, TPG, R])
        bd_a = sb("bd_a", [P, FC, ET, P])
        bd_m = sb("bd_m", [P, FC, ET, P])
        small = sb("small", [P, 512])
        acc = sb("acc", [P, FC * NW * B])
        acc_u = acc[:, 0:FC * NW * ET].rearrange("p (f c) -> p f c", f=FC)
        acc_s = acc[:, :].rearrange("p (f c) -> p f c", f=FC)
        AREA = 12000
        area = sb("area", [P, AREA])

        class Carve:

            def __init__(self, of, size):
                self.of, self.at, self.size = of, 0, size

            def __call__(self, n):
                self.at += n
                assert self.at <= self.size, (self.at, self.size)
                return self.of[:, self.at - n:self.at]

            def tiles(self, count, *shape):
                n = 1
                for d in shape:
                    n *= d
                letters = "abcd"[:len(shape)]
                sizes = dict(zip(letters, shape))
                return [self(n).rearrange(f"p ({' '.join(letters)}) -> p {' '.join(letters)}", **sizes)
                        for _ in range(count)]

        iota_c = iota_f[:, :].unsqueeze(1)

        def bc(ap, shape):
            return ap.broadcast_to(shape)

        drawn = [0]

        def fresh(name):
            drawn[0] += 1
            return f"{name}_{drawn[0]}"

        def bank(held, name, shape):
            return held.enter_context(nc.psum_tensor(fresh(name), shape, F32))

        lead = {}

        class Stage:

            def __init__(self, name):
                self.name, self.ctx, self.made, self.of_pool = name, ExitStack(), 0, 0

            def sem(self, name, ahead=0):
                self.made += 1
                assert SEM0 + self.made <= SEM0_POOL
                s = self.ctx.enter_context(nc.semaphore(fresh(f"{self.name}_{name}"), SEM0 + self.made - 1))
                lead[s.name] = ahead
                return s

            def pool_dma_sem(self, name):
                self.of_pool += 1
                return self.ctx.enter_context(nc.semaphore(fresh(f"{self.name}_{name}"), SEM0_POOL + self.of_pool - 1))

            def close(self):
                nc.all_engine_barrier(sems_to_clear=range(SEM0, SEM0 + self.made))
                if self.of_pool:
                    nc.gpsimd.dma_reset(range(SEM0_POOL, SEM0_POOL + self.of_pool))
                    nc.all_engine_barrier(sems_to_clear=range(SEM0_POOL, SEM0_POOL + self.of_pool))
                self.ctx.close()

        def after(sem, n):
            return n + 1 + lead[sem.name]

        def start(eng, *sems):
            for s in sems:
                eng.sem_inc(s, lead[s.name])

        def linker(eng, sem):
            n = [0]

            def link(ins):
                n[0] += 1
                ins.then_inc(sem, 1)
                eng.wait_ge(sem, n[0])
            return link

        st = Stage("setup")
        const_ready, rows_set, rows_in, small_in, w_in, types_in, x_in, fill_out, pad_out = (st.sem(n) for n in (
            "const_ready", "rows_set", "rows_in", "small_in", "w_in", "types_in", "x_in", "fill_out", "pad_out"))
        rows_made, turned, vec, ranked, offset, slotted, filled, zeroed, numbered = (st.sem(n) for n in (
            "rows_made", "turned", "vec", "ranked", "offset", "slotted", "filled", "zeroed", "numbered"))
        sorted_out = st.pool_dma_sem("sorted_out")
        cut = Carve(acc, FC * NW * B)
        w_all, = cut.tiles(1, FC, NT, 3 * D)
        b_all, = cut.tiles(1, NT, 3 * D)
        a_r = cut(4 * EG).bitcast(I32).rearrange("p (a e) -> p a e", a=4)
        a_f, = cut.tiles(1, 6, EG)
        wa_rows, = cut.tiles(1, ET, DK)
        pri_col, = cut.tiles(1, FC, ET)
        cut = Carve(area, AREA)
        JN = N // NP
        x_rows, = cut.tiles(1, JN, XR)
        filler = cut(XR)
        nt_i = cut(JN).bitcast(I32)
        hot6, = cut.tiles(1, NT, JN)
        rank6, = cut.tiles(1, NT, JN)
        slot_f, slot_i = cut(JN), cut(JN).bitcast(I32)
        before_p = cut(P)
        zrow = cut(ET * D)
        finished = cut((UNITS + 1) * UNIT).bitcast(I32)
        lead_f, behind = cut(NG), cut(4)
        tri = cut(SLOTS * NT).rearrange("p (s t) -> p s t", t=NT)
        full = E // EG
        rest = E - full * EG
        FILL = (0, FAR, ET + 2, 0)
        n_small = 16 * (HC * (1 + FC * (1 + ET)) + 2 * TPG)
        with ExitStack() as ps, nc.Block() as block:
            pt = [bank(ps, f"pt{a}", [P, 512]) for a in range(7)]
            p_n = bank(ps, "p_n", [P, 512])

            @block.gpsimd
            def _(pool):
                nc.gpsimd.iota(iota_i[:, :], pattern=[[1, P]], base=0, channel_multiplier=0).then_inc(const_ready, 1)
                nc.gpsimd.iota(part_i[:, :], pattern=[[0, 1]], base=0, channel_multiplier=1).then_inc(const_ready, 1)
                nc.gpsimd.iota(x_rows[0:NP, :, D:XR].bitcast(I32), pattern=[[1, JN], [0, 1]], base=0,
                               channel_multiplier=JN).then_inc(numbered, 1)
                nc.gpsimd.iota(finished.rearrange("p (u g) -> p u g", g=UNIT), pattern=[[NP, UNITS + 1], [0, UNIT]],
                               base=0, channel_multiplier=0).then_inc(const_ready, 1)
                pool.wait_ge(numbered, 1)
                pool.wait_ge(x_in, 16)
                pool.wait_ge(fill_out, 16)
                pool.wait_ge(slotted, 1)
                for j in range(JN):
                    nc.gpsimd.indirect_dma_start(
                        out=xs, out_offset=bass.IndirectOffsetOnAxis(ap=slot_i[0:NP, j:j + 1], axis=0),
                        in_=x_rows[0:NP, j, :], in_offset=None).then_inc(sorted_out, 16)
                pool.wait_ge(sorted_out, 16 * JN)

            @block.sync
            def _(sp):
                sp.dma_start(nt_i[0:NP, :], node_type_6.rearrange("(p j) -> p j", j=JN)).then_inc(types_in, 16)
                sp.dma_start(x_rows[0:NP, :, 0:D], x.rearrange("(p j) d -> p j d", j=JN)).then_inc(x_in, 16)
                sp.wait_ge(filled, 1)
                sp.dma_start(xs.rearrange("(s p) c -> p s c", p=P), bc(filler.unsqueeze(1), [P, SLOTS, XR]))\
                    .then_inc(fill_out, 16)
                sp.wait_ge(rows_set, 1)
                for a, e in enumerate((src, dst, edge_type_3, edge_type_8)):
                    sp.dma_start(a_r[0:full, a, :], e[0:full * EG].rearrange("(g c) -> g c", c=EG)).then_inc(rows_in, 16)
                    if rest:
                        sp.dma_start(a_r[full:full + 1, a, 0:rest], e[full * EG:E].unsqueeze(0)).then_inc(rows_in, 16)
                for j in range(HC):
                    js = slice(j * DK, (j + 1) * DK)
                    sp.dma_start(wa_rows[js], Wa.rearrange("t d k -> d t k")).then_inc(small_in, 16)
                    for f in range(FC):
                        h = f * HC + j
                        sp.dma_start(pri_col[js, f, :], relation_pri[:, h:h + 1].rearrange("t o -> o t").broadcast_to([DK, ET]),
                                     allow_slow_non_contiguous=True).then_inc(small_in, 16)
                        for t in range(ET):
                            sp.dma_start(bd_m[js, f, t, js], Wm[t]).then_inc(small_in, 16)
                for q in range(TPG):
                    sp.dma_start(comp_sb[q * R:(q + 1) * R, 0:B], comp1).then_inc(small_in, 16)
                    sp.dma_start(comp_sb[q * R:(q + 1) * R, B:2 * B], comp2).then_inc(small_in, 16)
                for f in range(FC):
                    for k, w in enumerate((Wk, Wv, Wq)):
                        sp.dma_start(w_all[:, f, :, k * D:(k + 1) * D],
                                     w[:, f * P:(f + 1) * P, :].rearrange("t k o -> k t o")).then_inc(w_in, 16)
                for k, b in enumerate((bk, bv, bq)):
                    sp.dma_start(b_all[:, :, k * D:(k + 1) * D], b.unsqueeze(0).broadcast_to([P, NT, D])).then_inc(w_in, 16)
                sp.wait_ge(zeroed, 1)
                sp.dma_start(qtab[N:NW, :], zrow[0:WIN, :]).then_inc(pad_out, 16)
                sp.wait_ge(small_in, n_small)
                sp.wait_ge(w_in, 16 * 3 * (FC + 1))
                sp.wait_ge(pad_out, 16)

            @block.vector
            def _(dve):
                nc.vector.memset(filler[:, 0:D], 0.0)
                nc.vector.memset(filler[:, D:XR].bitcast(I32), FAR).then_inc(filled, 1)
                for a in range(4):
                    nc.vector.memset(a_r[:, a, :], FILL[a])
                nc.vector.memset(bd_a[:, :, :, :], 0.0)
                nc.vector.memset(bd_m[:, :, :, :], 0.0).then_inc(rows_set, 1)
                link = linker(dve, vec)
                nc.vector.memset(zrow, 0.0).then_inc(zeroed, 1)
                nc.vector.memset(eps1[:, :], LN_EPS)
                nc.vector.memset(zero1[:, :], 0.0)
                nc.vector.memset(ones[:, :], 1.0)
                dve.wait_ge(const_ready, 2)
                nc.vector.tensor_copy(iota_f[:, :], iota_i[:, :])
                link(nc.vector.tensor_copy(part_f[:, :], part_i[:, :]))
                nc.vector.tensor_scalar(ident[:, :], iota_f[:, :], part_f[:, 0:1], None, ALU.is_equal)
                link(nc.vector.tensor_scalar(before_p, iota_f[:, :], part_f[:, 0:1], None, ALU.is_gt))

                link(nc.vector.tensor_copy(relations[:, :, :], bc(iota_f[:, 0:R].unsqueeze(1), [P, TPG, R])))
                row0 = iota_f[0:QK, 0:QK].rearrange("p (q r) -> p q r", r=R)[:, :, 0]
                link(nc.vector.tensor_scalar(of_tile[:, :], row0, part_f[0:QK, 0:1], None, ALU.is_le))
                link(nc.vector.tensor_scalar(small[0:QK, 0:TPG], row0, float(R - 1), part_f[0:QK, 0:1], ALU.add, ALU.is_ge))
                link(nc.vector.tensor_tensor(of_tile[:, :], of_tile[:, :], small[0:QK, 0:TPG], ALU.mult))

                dve.wait_ge(types_in, 16)
                link(nc.vector.tensor_copy(slot_f[0:NP, :], nt_i[0:NP, :]))
                link(nc.vector.tensor_tensor(hot6[0:NP], bc(slot_f[0:NP, :].unsqueeze(1), [NP, NT, JN]),
                                             bc(iota_f[0:NP, 0:NT].unsqueeze(2), [NP, NT, JN]), ALU.is_equal))
                for t in range(NT):
                    ins = nc.vector.tensor_tensor_scan(rank6[0:NP, t, :], ones[0:NP, 0:JN], hot6[0:NP, t, :], 0.0,
                                                       ALU.mult, ALU.add)
                ins.then_inc(ranked, 1)
                dve.wait_ge(offset, 1)
                tiles_f, upto, off = small[:, 16:16 + NT], small[:, 32:32 + NT], small[:, 48:48 + NT]
                tiles_i = small[:, 64:64 + NT].bitcast(I32)
                link(nc.vector.tensor_scalar(tiles_f, p_n[:, 64:64 + NT], 1.0 / P, (P - 1) / (2.0 * P), ALU.mult, ALU.add))
                link(nc.vector.tensor_copy(tiles_i, tiles_f))
                link(nc.vector.tensor_copy(tiles_f, tiles_i))
                link(nc.vector.tensor_tensor_scan(upto, ones[:, 0:NT], tiles_f, 0.0, ALU.mult, ALU.add))
                link(nc.vector.tensor_tensor(off, upto, tiles_f, ALU.subtract))
                link(nc.vector.tensor_scalar(off, off, float(P), -1.0, ALU.mult, ALU.add))
                link(nc.vector.tensor_tensor(off[0:NP], off[0:NP], p_n[0:NP, 0:NT], ALU.add))
                link(nc.vector.tensor_tensor(rank6[0:NP], rank6[0:NP], bc(off[0:NP].unsqueeze(2), [NP, NT, JN]), ALU.add))
                link(nc.vector.tensor_tensor(rank6[0:NP], rank6[0:NP], hot6[0:NP], ALU.mult))
                link(nc.vector.tensor_reduce(slot_f[0:NP, :], rank6[0:NP].rearrange("p t j -> p j t"), AX.X, ALU.add))
                nc.vector.tensor_copy(slot_i[0:NP, :], slot_f[0:NP, :]).then_inc(slotted, 1)
                link(nc.vector.tensor_tensor(tri[0:1], bc(iota_f[0:1, 0:SLOTS].unsqueeze(2), [1, SLOTS, NT]),
                                             bc(upto[0:1].unsqueeze(1), [1, SLOTS, NT]), ALU.is_ge))
                link(nc.vector.tensor_reduce(small[0:1, 80:80 + SLOTS], tri[0:1], AX.X, ALU.add))
                link(nc.vector.tensor_scalar(small[0:1, 80:80 + SLOTS], small[0:1, 80:80 + SLOTS], float(NT - 1), None, ALU.min))
                nc.vector.tensor_copy(slot_type[:, :], small[0:1, 80:80 + SLOTS])

                dve.wait_ge(rows_in, 16 * (8 if rest else 4))
                link(nc.vector.tensor_copy(a_f[0:NG, 0:4, :], a_r[0:NG, :, :]))
                lo, hi, up = small[0:NG, 0:1], small[0:NG, 1:2], small[0:NG, 2:3]
                link(nc.vector.tensor_reduce(lo, a_f[0:NG, 1, :], AX.X, ALU.min))
                link(nc.vector.tensor_scalar(a_f[0:NG, 5, :], a_f[0:NG, 1, :], float(FAR), None, ALU.is_lt))
                link(nc.vector.tensor_tensor(a_f[0:NG, 5, :], a_f[0:NG, 5, :], a_f[0:NG, 1, :], ALU.mult))
                link(nc.vector.tensor_reduce(hi, a_f[0:NG, 5, :], AX.X, ALU.max))
                link(nc.vector.tensor_tensor(up, hi, lo, ALU.subtract))
                link(nc.vector.tensor_scalar(a_f[0:NG, 5, :], a_f[0:NG, 1, :], lo, None, ALU.subtract))
                nc.vector.scalar_tensor_tensor(a_f[0:NG, 4, :], a_f[0:NG, 5, :], float(ET), a_f[0:NG, 2, :],
                                               ALU.mult, ALU.add).then_inc(rows_made, 1)
                nc.vector.memset(src_i[:, NG, :], 0)
                nc.vector.memset(count[:, :], 0.0)
                dve.wait_ge(small_in, n_small)
                for j in range(HC):
                    js = slice(j * DK, (j + 1) * DK)
                    for f in range(FC):
                        for t in range(ET):
                            ins = nc.vector.transpose(bd_a[js, f, t, js], wa_rows[js, t, :])
                link(ins)
                for f in range(FC):
                    for t in range(ET):
                        ins = nc.vector.tensor_scalar(bd_a[:, f, t, :], bd_a[:, f, t, :], pri_col[:, f, t:t + 1],
                                                      float(DK) ** -0.5, ALU.mult, ALU.mult)
                link(ins)
                dve.wait_ge(turned, 1)
                for k, to in enumerate((src_i, type3, type8, cell0, local0)):
                    ins = nc.vector.tensor_copy(to[:, 0:NG, :].rearrange("p g q -> p q g"),
                                                pt[k][:, 0:TPG * NG].rearrange("p (q g) -> p q g", q=TPG))
                link(ins)
                nc.vector.tensor_copy(base0[0:1, :], pt[5][0:1, 0:NG])
                nc.vector.tensor_copy(cell[:, :, :], cell0[:, :, :])
                nc.vector.tensor_copy(local[:, :, :], local0[:, :, :])
                link(nc.vector.tensor_reduce(small[0:1, 4:5], pt[6][0:1, 0:NG], AX.X, ALU.max))
                nc.vector.tensor_copy(base[:, :], base0[:, :])
                link(nc.vector.tensor_scalar(small[0:1, 5:6], small[0:1, 4:5], 1.0 / WIN,
                                             1.0 - (WIN - 1) / (2.0 * WIN), ALU.mult, ALU.add))
                link(nc.vector.tensor_copy(n_pass[:, :], small[0:1, 5:6]))
                dve.wait_ge(const_ready, 3)
                link(nc.vector.tensor_copy(lead_f[0:1, 1:NG], finished[0:1, 0:NG - 1]))
                nc.vector.memset(lead_f[0:1, 0:1], 0.0)
                link(nc.vector.tensor_scalar(behind[0:1, 1:2], small[0:1, 4:5], float(WIN), None, ALU.is_lt))
                link(nc.vector.tensor_tensor(lead_f[0:1, 0:NG], pt[5][0:1, 0:NG], lead_f[0:1, 0:NG], ALU.subtract))
                link(nc.vector.tensor_reduce(behind[0:1, 0:1], lead_f[0:1, 0:NG], AX.X, ALU.min))
                link(nc.vector.tensor_scalar(behind[0:1, 0:1], behind[0:1, 0:1], 0.0, None, ALU.is_ge))
                link(nc.vector.tensor_tensor(behind[0:1, 2:3], behind[0:1, 0:1], behind[0:1, 1:2], ALU.mult))
                link(nc.vector.tensor_copy(in_order[:, :], behind[0:1, 2:3]))

            @block.tensor
            def _(pe):
                pe.wait_ge(ranked, 1)
                totals = rank6[0:NP, :, JN - 1]
                nc.tensor.matmul(p_n[0:NP, 0:NT], before_p[0:NP, 0:NP], totals, start=True, stop=True)
                nc.tensor.matmul(p_n[:, 64:64 + NT], ones[0:NP, :], totals, start=True, stop=True).then_inc(offset, 1)
                pe.wait_ge(rows_made, 1)
                for k, a in enumerate((0, 2, 3, 4, 5)):
                    for q in range(TPG):
                        nc.tensor.transpose(pt[k][:, q * NG:(q + 1) * NG], a_f[0:NG, a, q * P:(q + 1) * P],
                                            ident[0:NG, 0:NG])
                nc.tensor.transpose(pt[5][0:1, 0:NG], small[0:NG, 0:1], ident[0:NG, 0:NG])
                nc.tensor.transpose(pt[6][0:1, 0:NG], small[0:NG, 2:3], ident[0:NG, 0:NG]).then_inc(turned, 1)
        st.close()

        st = Stage("proj")
        NR = 3
        xs_in = [st.sem(f"xs_in{p}") for p in range(NR)]
        xt_made, xt_copied, made, biased, qt_made, qt_copied, typed, typed_copied = (st.sem(n, a) for n, a in (
            ("xt_made", NR), ("xt_copied", 0), ("made", NR), ("biased", NR), ("qt_made", NR), ("qt_copied", 1),
            ("typed", NR), ("typed_copied", 1)))
        stored = [st.pool_dma_sem(f"stored{p}") for p in range(NR)]
        asked = st.sem("asked")
        cut = Carve(area, AREA)
        x_sb = cut.tiles(NR, XR)
        number = [cut(1).bitcast(I32) for _ in range(NR)]
        xt = cut.tiles(NR, FC, P)
        kv = cut.tiles(NR, 3, D)
        qt = cut.tiles(NR, FC, P)
        qs = cut.tiles(NR, ET * D)

        def slots(eng, body):
            loops = (SLOTS - 1) // NR
            for n in range(NR):
                body(n, n, 1)
            with eng.Fori(1, loops) as i:
                for p in range(NR):
                    body(i * NR + p, p, i + 1)
            for n in range(loops * NR, SLOTS):
                body(n, n % NR, n // NR + 1)

        def before_stored(eng, p, use):
            if not isinstance(use, int) or use > 1:
                eng.wait_ge(stored[p], (use - 1) * 48)

        def more(n, k):
            return not isinstance(n, int) or n + k < SLOTS

        def use_of(p, use, k):
            return use if p + k < NR else use + 1

        with ExitStack() as ps, nc.Block() as block:
            p_xt = bank(ps, "p_xt", [P, FC, P])
            p_kv = [bank(ps, f"p_kv{p}", [P, 2, D]) for p in range(NR)]
            p_q = bank(ps, "p_q", [P, 512])
            p_qt = bank(ps, "p_qt", [P, FC, P])
            p_ty = bank(ps, "p_ty", [P, 4, D])

            @block.sync
            def _(sp):
                def body(n, p, use):
                    sp.wait_ge(xt_made, after(xt_made, n - NR))
                    sp.wait_ge(biased, after(biased, n - NR))
                    sp.dma_start(x_sb[p], xs[bass.ds(n * P, P), :]).then_inc(xs_in[p], 16)
                slots(sp, body)

            @block.tensor
            def _(pe):
                start(pe, xt_made, made, qt_made, typed)

                def turn(n, p, use):
                    pe.wait_ge(xs_in[p], use * 16)
                    if not isinstance(n, int) or n:
                        pe.wait_ge(xt_copied, after(xt_copied, n - 1))
                    for f in range(FC):
                        ins = nc.tensor.transpose(p_xt[:, f, :], x_sb[p][:, f * P:(f + 1) * P], ident[:, :])
                    ins.then_inc(xt_made, 1)

                def project(n, p):
                    v = pe.value_load(slot_type[0:1, bass.ds(n, 1)], min_val=0, max_val=NT - 1)
                    pe.wait_ge(biased, after(biased, n - 1))
                    for k, to in ((0, p_kv[p][:, :, :].rearrange("p a d -> p (a d)")), (2, p_q[:, 0:D])):
                        n_col = 2 * D if k == 0 else D
                        for f in range(FC):
                            rhs = w_all[:, f, bass.ds(v, 1), k * D:k * D + n_col].rearrange("p t o -> p (t o)")
                            ins = nc.tensor.matmul(to, xt[p][:, f, :], rhs, start=(f == 0), stop=(f == FC - 1))
                    ins.then_inc(made, 1)

                def turn_queries(n, p):
                    pe.wait_ge(biased, after(biased, n))
                    pe.wait_ge(qt_copied, after(qt_copied, n - 1))
                    for f in range(FC):
                        ins = nc.tensor.transpose(p_qt[:, f, :], kv[p][:, 2, f * P:(f + 1) * P], ident[:, :])
                    ins.then_inc(qt_made, 1)

                def typed_queries(n, p):
                    pe.wait_ge(qt_copied, after(qt_copied, n))
                    pe.wait_ge(typed_copied, after(typed_copied, n - 1))
                    for t in range(ET):
                        for c in range(FC):
                            ins = nc.tensor.matmul(p_ty[:, t, c * P:(c + 1) * P], qt[p][:, c, :], bd_a[:, c, t, :],
                                                   start=True, stop=True)
                    ins.then_inc(typed, 1)

                turn(0, 0, 1)
                turn(1, 1, 1)
                project(0, 0)

                def body(n, p, use):
                    turn_queries(n, p)
                    if more(n, 1):
                        pe.wait_ge(xt_copied, after(xt_copied, n + 1))
                        project(n + 1, (p + 1) % NR)
                    if more(n, 2):
                        turn(n + 2, (p + 2) % NR, use_of(p, use, 2))
                    typed_queries(n, p)
                slots(pe, body)

            @block.scalar
            def _(act):
                start(act, qt_copied, typed_copied)

                def copy_xt(n, p):
                    act.wait_ge(xt_made, after(xt_made, n))
                    act.wait_ge(made, after(made, n - NR))
                    nc.scalar.copy(xt[p], p_xt[:, :, :]).then_inc(xt_copied, 1)

                copy_xt(0, 0)
                copy_xt(1, 1)

                def body(n, p, use):
                    act.wait_ge(qt_made, after(qt_made, n))
                    act.wait_ge(typed, after(typed, n - NR))
                    nc.scalar.copy(qt[p], p_qt[:, :, :]).then_inc(qt_copied, 1)
                    if more(n, 2):
                        copy_xt(n + 2, (p + 2) % NR)
                    act.wait_ge(typed, after(typed, n))
                    before_stored(act, p, use)
                    nc.scalar.copy(qs[p].rearrange("p (t d) -> p t d", t=ET), p_ty[:, 0:ET, :]).then_inc(typed_copied, 1)
                slots(act, body)

            @block.vector
            def _(dve):
                start(dve, biased)

                def body(n, p, use):
                    v = dve.value_load(slot_type[0:1, bass.ds(n, 1)], min_val=0, max_val=NT - 1)
                    dve.wait_ge(xs_in[p], use * 16)
                    dve.wait_ge(made, after(made, n))
                    before_stored(dve, p, use)
                    dve.wait_ge(qt_made, after(qt_made, n - NR))
                    own = b_all[:, bass.ds(v, 1), :].rearrange("p t (a d) -> p (t a) d", d=D)
                    nc.vector.tensor_copy(number[p], x_sb[p][:, D:XR].bitcast(I32))
                    nc.vector.tensor_tensor(kv[p][:, 2, :], p_q[:, 0:D], own[:, 2, :], ALU.add)
                    nc.vector.tensor_tensor(kv[p][:, 0:2, :], p_kv[p][:, :, :], own[:, 0:2, :], ALU.add).then_inc(biased, 1)
                slots(dve, body)

            @block.gpsimd
            def _(pool):
                def body(n, p, use):
                    to = bass.IndirectOffsetOnAxis(ap=number[p], axis=0)
                    pool.wait_ge(biased, after(biased, n))
                    pool.wait_ge(typed_copied, after(typed_copied, n))
                    pool.sem_inc(asked, 1)
                    for table, rows in ((ktab, kv[p][:, 0, :]), (vtab, kv[p][:, 1, :]), (qtab, qs[p])):
                        nc.gpsimd.indirect_dma_start(out=table, out_offset=to, in_=rows, in_offset=None,
                                                     bounds_check=N - 1, oob_is_err=False).then_inc(stored[p], 16)
                slots(pool, body)
                for p in range(NR):
                    pool.wait_ge(stored[p], len(range(p, SLOTS, NR)) * 48)
        st.close()

        def groups(eng, body):
            with eng.Fori(0, NG // NB) as i:
                for b in range(NB):
                    body(i * NB + b, b, i + 1)
            for g in range(NG // NB * NB, NG):
                body(g, g % NB, g // NB + 1)

        def exists(g, k):
            return not isinstance(g, int) or g + k < NG

        def ring(b, k):
            return (b + k) % NB

        def units(eng, body, piece=None):
            def unit(i, first):
                for j in range(UNIT):
                    body(i * UNIT + j, j, i)
                    if piece and not first:
                        piece(i - 1, j)
            unit(0, True)
            with eng.Fori(1, UNITS) as i:
                unit(i, False)
            for g in range(UNITS * UNIT, NG):
                body(g, g % UNIT, UNITS)
            if piece:
                for n in range(UNITS - 1, NTILE):
                    for j in range(UNIT):
                        piece(n, j)

        def gathers(pool, walk, ring_size, table, rows, idx, idx_ready, free, asked, landed):
            def body(g, b, use):
                pool.wait_ge(idx_ready, after(idx_ready, g))
                pool.wait_ge(free, after(free, g - ring_size))
                pool.sem_inc(asked, 1)
                for q in range(TPG):
                    nc.gpsimd.indirect_dma_start(
                        out=rows[b][:, q, :], out_offset=None, in_=table,
                        in_offset=bass.IndirectOffsetOnAxis(ap=idx[b][:, q:q + 1], axis=0),
                    ).then_inc(landed[b], 16)
            walk(pool, body)
            for b in range(ring_size):
                pool.wait_ge(landed[b], len(range(b, NG, ring_size)) * 16 * TPG)

        def group(a, g):
            return a[:, bass.ds(g, 1), :].rearrange("p g q -> p (g q)")

        def copy_indices(act, g, b, idx, idx_ready):
            nc.scalar.copy(idx[b], group(src_i, g)).then_inc(idx_ready, 1)

        def hot(to, which, g, width):
            return nc.vector.tensor_tensor(to, bc(group(which, g).unsqueeze(2), [P, TPG, width]),
                                           bc(iota_c[:, :, 0:width], [P, TPG, width]), ALU.is_equal)

        def scores(first):
            st = Stage("score")
            idx_ready, products, hots, turned, copied, expanded = (st.sem(n, a) for n, a in (
                ("idx_ready", 0), ("products", NB), ("hots", 0), ("turned", 1), ("copied", 0), ("expanded", NB)))
            scored, counted, added, summed, asked = (st.sem(n, a) for n, a in (
                ("scored", 1), ("counted", 1), ("added", 1), ("summed", 0), ("asked", 0)))
            landed = [st.pool_dma_sem(f"landed{b}") for b in range(NB)]
            q_in = [st.sem(f"q_in{b}") for b in range(NB)]
            cut = Carve(area, AREA)
            rows = cut.tiles(NB, TPG, D)
            terms = cut.tiles(NB, TPG, D)
            idx = [cut(TPG).bitcast(I32) for _ in range(NB)]
            hot_q, hot_n, hot_r = cut.tiles(NB, TPG, QR), cut.tiles(NB, TPG, WIN), cut.tiles(NB, TPG, QK)
            q_win = [a[0:QR] for a in cut.tiles(NB, D)]
            hot_t = [a[0:QR] for a in cut.tiles(NB, TPG, P)]
            again = cut(TPG * H)
            with ExitStack() as ps, nc.Block() as block:
                p_t = bank(ps, "p_t", [QR, TPG, P])
                p_q = [bank(ps, f"p_qe{b}", [P, TPG, D]) for b in range(NB)]
                p_c = bank(ps, "p_c", [QK, 512])

                @block.gpsimd
                def _(pool):
                    gathers(pool, groups, NB, ktab, rows, idx, idx_ready, products, asked, landed)

                @block.sync
                def _(sp):
                    def body(g, b, use):
                        v = sp.value_load(base[0:1, bass.ds(g, 1)], min_val=0, max_val=N)
                        sp.wait_ge(expanded, after(expanded, g - NB))
                        sp.dma_start(q_win[b], qtab.rearrange("n (t d) -> (n t) d", t=ET)[bass.ds(v * ET, QR), :])\
                            .then_inc(q_in[b], 16)
                    groups(sp, body)

                @block.scalar
                def _(act):
                    copy_indices(act, 0, 0, idx, idx_ready)
                    copy_indices(act, 1, 1, idx, idx_ready)
                    if first:
                        nc.scalar.activation(acc_u[:, :, :], bc(zero1[:, 0:1].unsqueeze(2), [P, FC, NW * ET]), ACT.Copy)

                    def body(g, b, use):
                        act.wait_ge(turned, after(turned, g))
                        act.wait_ge(expanded, after(expanded, g - NB))
                        nc.scalar.copy(hot_t[b], p_t[:, :, :]).then_inc(copied, 1)
                        if exists(g, 2):
                            act.wait_ge(products, after(products, g - 1))
                            copy_indices(act, g + 2, ring(b, 2), idx, idx_ready)
                    groups(act, body)

                @block.vector
                def _(dve):
                    start(dve, products, scored, added)

                    def hot_all(g, b):
                        hot(hot_q[b], cell, g, QR)
                        hot(hot_n[b], local, g, WIN)
                        nc.vector.tensor_tensor(hot_r[b], bc(group(type8, g).unsqueeze(2), [P, TPG, QK]),
                                                bc(relations[:, :, :].rearrange("p q r -> p (q r)").unsqueeze(1), [P, TPG, QK]),
                                                ALU.is_equal).then_inc(hots, 1)

                    hot_all(0, 0)
                    hot_all(1, 1)

                    def body(g, b, use):
                        v = dve.value_load(base[0:1, bass.ds(g, 1)], min_val=0, max_val=N)
                        if exists(g, 2):
                            dve.wait_ge(turned, after(turned, g - 1))
                            dve.wait_ge(counted, after(counted, g - 1))
                            hot_all(g + 2, ring(b, 2))
                        dve.wait_ge(landed[b], use * 16 * TPG)
                        dve.wait_ge(expanded, after(expanded, g))
                        nc.vector.tensor_tensor(terms[b], rows[b], p_q[b][:, :, :], ALU.mult).then_inc(products, 1)
                        dve.wait_ge(counted, after(counted, g))
                        dve.wait_ge(added, after(added, g - 1))
                        here = count[:, bass.ds(v, WIN)]
                        nc.vector.tensor_tensor(here, here, p_c[:, 0:WIN], ALU.add).then_inc(added, 1)
                        dve.wait_ge(products, after(products, g))
                        dest = score[:, bass.ds(g, 1), :, :].rearrange("p g q h -> p (g q h)")
                        by_head = terms[b].rearrange("p q (h d) -> p (q h) d", d=DK)
                        if first:
                            nc.vector.tensor_reduce(dest, by_head, AX.X, ALU.add).then_inc(scored, 1)
                        else:
                            dve.wait_ge(scored, after(scored, g - 1))
                            nc.vector.tensor_reduce(again, by_head, AX.X, ALU.add).then_inc(summed, 1)
                            dve.wait_ge(summed, after(summed, g))
                            nc.vector.tensor_tensor(dest, dest, again, ALU.add).then_inc(scored, 1)
                    groups(dve, body)

                @block.tensor
                def _(pe):
                    start(pe, turned, expanded, counted)

                    def turn(b):
                        for q in range(TPG):
                            ins = nc.tensor.transpose(p_t[:, q, :], hot_q[b][:, q, :], ident[:, :])
                        ins.then_inc(turned, 1)

                    pe.wait_ge(hots, 1)
                    turn(0)

                    def body(g, b, use):
                        pe.wait_ge(copied, after(copied, g))
                        if exists(g, 1):
                            pe.wait_ge(hots, after(hots, g + 1))
                            turn(ring(b, 1))
                        pe.wait_ge(q_in[b], use * 16)
                        pe.wait_ge(products, after(products, g - NB))
                        for q in range(TPG):
                            ins = nc.tensor.matmul(p_q[b][:, q, :], hot_t[b][:, q, :], q_win[b],
                                                   start=True, stop=True)
                        ins.then_inc(expanded, 1)
                        pe.wait_ge(added, after(added, g - 1))
                        for q in range(TPG):
                            ins = nc.tensor.matmul(p_c[:, 0:WIN], hot_r[b][:, q, :], hot_n[b][:, q, :],
                                                   start=(q == 0), stop=(q == TPG - 1))
                        ins.then_inc(counted, 1)
                    groups(pe, body)
            st.close()

        def softmax():
            st = Stage("soft")
            vec, asked, served, expd, joined = (st.sem(n) for n in ("vec", "asked", "served", "expd", "joined"))
            cut = Carve(area, AREA)
            msk = cut(NG * TPG)
            of_type = cut.tiles(ET, NG * TPG, H)
            s = score[:, :, :, :].rearrange("p g q h -> p (g q) h")
            ty = type3[:, :, :].rearrange("p g q -> p (g q)")
            TH = ET * H
            with ExitStack() as ps, nc.Block() as block:
                p_m = bank(ps, "p_m", [P, 512])
                p_b = bank(ps, "p_b", [P, 512])
                p_z = bank(ps, "p_z", [P, 512])
                part, least, diag, top, z = (small[:, k * 64:k * 64 + TH] for k in range(5))

                @block.vector
                def _(dve):
                    link = linker(dve, vec)
                    for t in range(ET):
                        link(nc.vector.tensor_scalar(msk, ty, float(t), -3.0e38, ALU.not_equal, ALU.mult))
                        link(nc.vector.tensor_tensor(of_type[t], s, bc(msk.unsqueeze(2), [P, NG * TPG, H]), ALU.add))
                        link(nc.vector.tensor_reduce(part[:, t * H:(t + 1) * H], of_type[t].rearrange("p e h -> p h e"),
                                                     AX.X, ALU.max))
                    nc.vector.tensor_scalar(count[:, :], count[:, :], 1.0, None, ALU.max).then_inc(asked, 1)
                    dve.wait_ge(served, 1)
                    link(nc.vector.tensor_reduce(least[0:TH, 0:1], p_m[0:TH, 0:P], AX.X, ALU.max))
                    nc.vector.tensor_scalar(diag[0:TH, :], ident[0:TH, 0:TH], least[0:TH, 0:1], None, ALU.mult)\
                        .then_inc(asked, 1)
                    dve.wait_ge(served, 2)
                    nc.vector.tensor_scalar(top, p_b[:, 0:TH], -1.0e37, -1.0, ALU.max, ALU.mult).then_inc(asked, 1)
                    link(nc.vector.reciprocal(count[:, :], count[:, :]))
                    dve.wait_ge(served, 3)
                    link(nc.vector.tensor_scalar(z, p_z[:, 0:TH], 1e-30, None, ALU.max))
                    link(nc.vector.reciprocal(z, z))
                    for f in range(FC):
                        for t in range(ET):
                            for j in range(HC):
                                js = slice(j * DK, (j + 1) * DK)
                                c = t * H + f * HC + j
                                ins = nc.vector.tensor_scalar(bd_m[js, f, t, :], bd_m[js, f, t, :], z[js, c:c + 1], None, ALU.mult)
                    link(ins)

                @block.gpsimd
                def _(pool):
                    pool.wait_ge(expd, 2)
                    nc.gpsimd.tensor_tensor(s, of_type[0], of_type[1], ALU.add).then_inc(joined, 1)
                    pool.wait_ge(joined, 1)
                    pool.wait_ge(expd, 3)
                    nc.gpsimd.tensor_tensor(s, s, of_type[2], ALU.add).then_inc(joined, 1)
                    pool.wait_ge(joined, 2)

                @block.tensor
                def _(pe):
                    pe.wait_ge(asked, 1)
                    nc.tensor.transpose(p_m[0:TH, 0:P], part, ident[:, :]).then_inc(served, 1)
                    pe.wait_ge(asked, 2)
                    nc.tensor.matmul(p_b[:, 0:TH], ones[0:TH, :], diag[0:TH, :], start=True, stop=True).then_inc(served, 1)
                    pe.wait_ge(expd, 3)
                    nc.tensor.matmul(p_z[:, 0:TH], ones[:, :], z, start=True, stop=True).then_inc(served, 1)

                @block.scalar
                def _(act):
                    act.wait_ge(asked, 3)
                    for t in range(ET):
                        for h in range(H):
                            ins = nc.scalar.activation(of_type[t][:, :, h], of_type[t][:, :, h], ACT.Exp,
                                                       bias=top[:, t * H + h:t * H + h + 1],
                                                       accum_out=z[:, t * H + h:t * H + h + 1])
                        ins.then_inc(expd, 1)
            st.close()

        class Finish:

            def __init__(self, st, ps, cut, kind):
                self.kind = kind
                self.table, self.dest = (x, x1tab, htab)[kind], (x1tab, htab, out)[kind]
                self.C = ET if kind == 0 else B
                self.rows, self.fin, self.y = (cut(D)[0:NP] for _ in range(3))
                self.res = cut(D)[0:NP] if kind == 2 else self.rows
                self.laid_sb, = cut.tiles(1, FC, self.C, NP)
                self.stat, self.mv = cut(6)[0:NP], cut(2)[0:NP]
                self.rstd, self.shift, self.rs2 = (cut(1)[0:NP] for _ in range(3))
                if kind == 0:
                    self.g_bc, self.b_bc = cut(D)[0:NP], cut(D)[0:NP]
                else:
                    self.xt_sb, = cut.tiles(1, FC, NP)
                    self.bs = cut(D)[0:1]
                    self.p_xt = bank(ps, "p_fx", [P, FC, P])
                self.p_o = bank(ps, "p_fo", [P, 2, D])
                self.w_in, self.x_in, self.stored = st.sem("w_in"), st.sem("x_in"), st.sem("stored")
                self.laid, self.xt_made, self.xt_copied, self.made, self.used, self.done = (st.sem(n, a) for n, a in (
                    ("laid", 0), ("xt_made", 1), ("xt_copied", 0), ("made", 1), ("used", 1), ("done", 1)))
                self.vec, self.chunk, self.var, self.dev, self.ready = (st.sem(n) for n in (
                    "vec", "chunk", "var", "dev", "ready"))

            def load_weights(self, sp):
                if self.kind == 0:
                    sp.dma_start(self.g_bc, ln_g.unsqueeze(0).broadcast_to([NP, D])).then_inc(self.w_in, 16)
                    sp.dma_start(self.b_bc, ln_b.unsqueeze(0).broadcast_to([NP, D])).then_inc(self.w_in, 16)
                    return
                basis, root, bias = ((basis1, root1, bias1), (basis2, root2, bias2))[self.kind - 1]
                for f in range(FC):
                    sp.dma_start(bas[:, f, 0:B, :], basis[:, f * P:(f + 1) * P, :].rearrange("b k o -> k b o"))\
                        .then_inc(self.w_in, 16)
                    sp.dma_start(bas[:, f, B, :], root[f * P:(f + 1) * P, :]).then_inc(self.w_in, 16)
                sp.dma_start(self.bs, bias.unsqueeze(0)).then_inc(self.w_in, 16)

            def sync(self, sp):
                self.load_weights(sp)

                def load(n):
                    sp.wait_ge(self.used, after(self.used, n - 1))
                    at = bass.ds(n * NP, NP)
                    sp.dma_start(self.rows, self.table[at, :]).then_inc(self.x_in, 16)
                    if self.kind == 2:
                        sp.dma_start(self.res, x1tab[at, :]).then_inc(self.x_in, 16)

                def store(n):
                    sp.wait_ge(self.done, after(self.done, n))
                    sp.dma_start(self.dest[bass.ds(n * NP, NP), :], self.fin).then_inc(self.stored, 16)

                load(0)
                with sp.Fori(1, NTILE) as n:
                    load(n)
                    store(n - 1)
                store(NTILE - 1)
                sp.wait_ge(self.stored, NTILE * 16)

            def rows_landed(self, eng, n):
                eng.wait_ge(self.x_in, (n + 1) * 16 * (2 if self.kind == 2 else 1))

            def start_scalar(self, act):
                start(act, self.done)
                if self.kind == 1:
                    start(act, self.used)
                else:
                    nc.scalar.activation(self.rstd, eps1[0:NP, :], ACT.Sqrt)

            def scalar(self, act, n, j, added):
                if j == 0:
                    act.wait_ge(added, after(added, min((n + 1) * UNIT, NG - 1) if isinstance(n, int) else (n + 1) * UNIT))
                    act.wait_ge(self.made, after(self.made, n - 1))
                    of = (acc_u if self.kind == 0 else acc_s)
                    for f in range(FC):
                        sums = of[:, f, bass.ds(n * NP * self.C, NP * self.C)].rearrange("p (n c) -> p c n", c=self.C)
                        ins = nc.scalar.copy(self.laid_sb[:, f, :, :], sums)
                    ins.then_inc(self.laid, 1)
                    if self.kind:
                        act.wait_ge(self.xt_made, after(self.xt_made, n))
                        nc.scalar.copy(self.xt_sb, self.p_xt[:, :, 0:NP]).then_inc(self.xt_copied, 1)
                norms = (2, 0, 1)[self.kind]
                if 2 <= j < 2 + norms:
                    act.wait_ge(self.var, n * norms + j - 1)
                    nc.scalar.activation(self.mv[:, 1:2], self.mv[:, 1:2], ACT.Sqrt, bias=eps1[0:NP, :])\
                        .then_inc(self.dev, 1)
                if j == 3:
                    if isinstance(n, int):
                        if n:
                            act.wait_ge(self.stored, n * 16)
                    else:
                        act.wait_ge(self.stored, n * 16)
                    if self.kind == 1:
                        act.wait_ge(self.made, after(self.made, n))
                        nc.scalar.activation(self.fin, self.p_o[0:NP, 0, :], ACT.Relu).then_inc(self.done, 1)
                        act.sem_inc(self.used, 1)
                    else:
                        act.wait_ge(self.ready, n + 1)
                        nc.scalar.activation(self.fin, self.y, ACT.Identity, bias=self.shift, scale=self.rs2)\
                            .then_inc(self.done, 1)

            def start_tensor(self, pe):
                start(pe, self.made)
                if self.kind:
                    start(pe, self.xt_made)
                pe.wait_ge(self.w_in, 16 * (2 if self.kind == 0 else 2 * FC + 1))

            def tensor(self, pe, n, j):
                if self.kind and j == 0:
                    self.rows_landed(pe, n)
                    pe.wait_ge(self.made, after(self.made, n - 1))
                    for f in range(FC):
                        ins = nc.tensor.transpose(self.p_xt[:, f, 0:NP], self.rows[:, f * P:(f + 1) * P],
                                                  ident[0:NP, 0:NP])
                    ins.then_inc(self.xt_made, 1)
                to = self.p_o[0:NP, 0, :]
                if j == 1:
                    pe.wait_ge(self.laid, after(self.laid, n))
                    pe.wait_ge(self.done, after(self.done, n - 1))
                if self.kind == 0 and j == 1:
                    for f in range(FC):
                        for t in range(ET):
                            ins = nc.tensor.matmul(to[:, f * P:(f + 1) * P], self.laid_sb[:, f, t, :], bd_m[:, f, t, :],
                                                   start=(t == 0), stop=(t == ET - 1))
                    ins.then_inc(self.made, 1)
                elif self.kind:
                    for f in range(FC):
                        if j == (1 + f if self.kind == 1 else 1):
                            for c in range(B):
                                nc.tensor.matmul(to, self.laid_sb[:, f, c, :], bas[:, f, c, :],
                                                 start=(f == 0 and c == 0), stop=False)
                    if j == (2 if self.kind == 1 else 1):
                        pe.wait_ge(self.xt_copied, after(self.xt_copied, n))
                        for f in range(FC):
                            nc.tensor.matmul(to, self.xt_sb[:, f, :], bas[:, f, B, :], start=False, stop=False)
                        nc.tensor.matmul(to, ones[0:1, 0:NP], self.bs, start=False, stop=True).then_inc(self.made, 1)

            def start_vector(self, dve):
                if self.kind != 1:
                    start(dve, self.used)

            def vector(self, dve, n, j):
                if self.kind == 1 or j < 2:
                    return
                NORMS, STEPS = (2, 0, 1)[self.kind], (8, 0, 3)[self.kind]
                if j == 2:
                    self.k, self.r = 0, 0

                def link(ins):
                    self.k += 1
                    ins.then_inc(self.vec, 1)
                    dve.wait_ge(self.vec, n * STEPS + self.k)

                def moments():
                    link(nc.vector.bn_stats(self.stat, self.y))
                    dve.sem_inc(self.chunk, 1)
                    nc.vector.bn_aggr(self.mv, self.stat).then_inc(self.var, 1)

                def deviation():
                    self.r += 1
                    dve.wait_ge(self.dev, n * NORMS + self.r)

                if j == 2:
                    self.rows_landed(dve, n)
                    dve.wait_ge(self.made, after(self.made, n))
                    dve.wait_ge(self.done, after(self.done, n - 1))
                    link(nc.vector.tensor_tensor(self.y, self.p_o[0:NP, 0, :], self.res, ALU.add))
                    if self.kind == 2:
                        dve.sem_inc(self.used, 1)
                    moments()
                if j == 3:
                    if self.kind == 0:
                        deviation()
                        link(nc.vector.reciprocal(self.rstd, self.mv[:, 1:2]))
                        link(nc.vector.scalar_tensor_tensor(self.y, self.y, self.mv[:, 0:1], self.g_bc, ALU.subtract, ALU.mult))
                        link(nc.vector.scalar_tensor_tensor(self.y, self.y, self.rstd, self.rows, ALU.mult, ALU.add))
                        dve.sem_inc(self.used, 1)
                        link(nc.vector.tensor_tensor(self.y, self.y, self.b_bc, ALU.add))
                        moments()
                    deviation()
                    link(nc.vector.reciprocal(self.rs2, self.mv[:, 1:2]))
                    ins = nc.vector.scalar_tensor_tensor(self.shift, self.mv[:, 0:1], -1.0, self.rs2, ALU.mult, ALU.mult)
                    ins.then_inc(self.ready, 1)
                    dve.wait_ge(self.ready, n + 1)
                    assert self.k == STEPS, self.k

        def in_units(eng, body):
            units(eng, lambda g, j, i: body(g, j, i + 1))

        def values(finish=False):
            st = Stage("val")
            idx_ready, weighted, summed, added, asked = (st.sem(n, a) for n, a in (
                ("idx_ready", 0), ("weighted", UNIT), ("summed", UNIT), ("added", 2), ("asked", 0)))
            landed = [st.pool_dma_sem(f"landed{b}") for b in range(UNIT)]
            cut = Carve(area, AREA)
            rows = cut.tiles(UNIT, TPG, D)
            past = Carve(acc[:, FC * NW * ET:], FC * NW * (B - ET))
            work = past.tiles(UNIT, TPG, D)
            idx = [cut(TPG).bitcast(I32) for _ in range(UNIT)]
            hot_q = cut.tiles(UNIT, TPG, QR)
            with ExitStack() as ps, nc.Block() as block:
                p_u = [bank(ps, f"p_u{b}", [P, FC, 256]) for b in range(2)]
                tile = Finish(st, ps, cut, 0) if finish else None

                def pieces(of):
                    return of if finish else None

                if finish:
                    block.sync(tile.sync)

                @block.gpsimd
                def _(pool):
                    gathers(pool, in_units, UNIT, vtab, rows, idx, idx_ready, weighted, asked, landed)

                @block.scalar
                def _(act):
                    for b in range(3):
                        copy_indices(act, b, b, idx, idx_ready)
                    if finish:
                        tile.start_scalar(act)

                    def body(g, b, i):
                        if exists(g, 3):
                            act.wait_ge(weighted, after(weighted, g - 1))
                            copy_indices(act, g + 3, (b + 3) % UNIT, idx, idx_ready)
                    units(act, body, pieces(lambda n, j: tile.scalar(act, n, j, added)))

                @block.vector
                def _(dve):
                    start(dve, weighted, added)
                    if finish:
                        tile.start_vector(dve)

                    def weigh(g, b, i):
                        dve.wait_ge(landed[b], (i + 1) * 16 * TPG)
                        dve.wait_ge(summed, after(summed, g - UNIT))
                        wt = score[:, bass.ds(g, 1), :, :].rearrange("p g q h -> p (g q h)").unsqueeze(2)
                        nc.vector.tensor_tensor(work[b].rearrange("p q (h d) -> p (q h) d", d=DK),
                                                rows[b].rearrange("p q (h d) -> p (q h) d", d=DK),
                                                bc(wt, [P, TPG * H, DK]), ALU.mult).then_inc(weighted, 1)

                    hot(hot_q[0], cell, 0, QR)
                    hot(hot_q[1], cell, 1, QR)
                    weigh(0, 0, 0)

                    def add(g, b):
                        v = dve.value_load(base[0:1, bass.ds(g, 1)], min_val=0, max_val=N)
                        dve.wait_ge(summed, after(summed, g))
                        dve.wait_ge(added, after(added, g - 1))
                        here = acc_u[:, :, bass.ds(v * ET, QR)]
                        nc.vector.tensor_tensor(here, here, p_u[b % 2][:, :, 0:QR], ALU.add).then_inc(added, 1)

                    def body(g, b, i):
                        if exists(g, 2):
                            dve.wait_ge(summed, after(summed, g - 2))
                            hot(hot_q[(b + 2) % UNIT], cell, g + 2, QR)
                        if exists(g, 1):
                            weigh(g + 1, (b + 1) % UNIT, i if b < UNIT - 1 else i + 1)
                        if not isinstance(g, int) or g:
                            add(g - 1, (b - 1) % UNIT)
                        if not exists(g, 1):
                            add(g, b)
                    units(dve, body, pieces(lambda n, j: tile.vector(dve, n, j)))

                @block.tensor
                def _(pe):
                    start(pe, summed)
                    if finish:
                        tile.start_tensor(pe)

                    def body(g, b, i):
                        pe.wait_ge(weighted, after(weighted, g))
                        pe.wait_ge(added, after(added, g - 2))
                        for f in range(FC):
                            for q in range(TPG):
                                ins = nc.tensor.matmul(p_u[b % 2][:, f, 0:QR], work[b][:, q, f * P:(f + 1) * P],
                                                       hot_q[b][:, q, :], start=(q == 0), stop=(q == TPG - 1))
                        ins.then_inc(summed, 1)
                    units(pe, body, pieces(lambda n, j: tile.tensor(pe, n, j)))
            st.close()

        def convolve(c, table, finish=False):
            st = Stage(f"conv{c}")
            first = finish
            idx_ready, hots, weights, summed, added, cleared, asked = (st.sem(n, a) for n, a in (
                ("idx_ready", 0), ("hots", 0), ("weights", 0), ("summed", UNIT), ("added", 2), ("cleared", 0), ("asked", 0)))
            turned, copied, found, picked, shared, rated, coefs = (st.sem(n, a) for n, a in (
                ("turned", 0), ("copied", 0), ("found", 2), ("picked", 0), ("shared", 0), ("rated", 0), ("coefs", 2)))
            landed = [st.pool_dma_sem(f"landed{b}") for b in range(UNIT)]
            half = FC * NW * B // 2
            cut = Carve(area, AREA)
            rows = cut.tiles(UNIT, TPG, D)
            idx = [cut(TPG).bitcast(I32) for _ in range(UNIT)]
            hot_n, woh = cut.tiles(UNIT, TPG, WIN), cut.tiles(UNIT, TPG, WIN, B)
            if c == 0:
                hot_r = cut.tiles(UNIT, TPG, R)
                hot_t = [a[0:QK] for a in cut.tiles(2, P)]
                tables = [a[0:QK] for a in cut.tiles(2, TPG, WIN + 2 * B)]
                pick = cut.tiles(2, TPG, WIN)
                share = [cut(TPG) for _ in range(2)]
                again, = cut.tiles(1, TPG, 2 * B)
            with ExitStack() as ps, nc.Block() as block:
                p_s = [bank(ps, f"p_s{b}", [P, FC, 256]) for b in range(2)]
                if c == 0:
                    p_t = bank(ps, "p_rt", [QK, P])
                    p_f = [bank(ps, f"p_f{b}", [P, TPG, WIN + 2 * B]) for b in range(2)]
                tile = Finish(st, ps, cut, c + 1) if finish else None

                def pieces(of):
                    return of if finish else None

                if finish:
                    block.sync(tile.sync)

                @block.gpsimd
                def _(pool):
                    gathers(pool, in_units, UNIT, table, rows, idx, idx_ready, summed, asked, landed)

                @block.scalar
                def _(act):
                    for b in range(3):
                        copy_indices(act, b, b, idx, idx_ready)
                    if c == 0:
                        for b in range(2):
                            for q in range(TPG):
                                nc.scalar.activation(tables[b][:, q, WIN:], comp_sb[:, :], ACT.Identity,
                                                     scale=of_tile[:, q:q + 1])
                    if first:
                        nc.scalar.activation(acc[:, half:], bc(zero1[:, 0:1], [P, half]), ACT.Copy).then_inc(cleared, 1)
                    if finish:
                        tile.start_scalar(act)

                    def prepare(g, b):
                        v = act.value_load(base[0:1, bass.ds(g, 1)], min_val=0, max_val=N)
                        act.wait_ge(found, after(found, g - 2))
                        for q in range(TPG):
                            nc.scalar.activation(tables[b % 2][:, q, 0:WIN], count[:, bass.ds(v, WIN)], ACT.Identity,
                                                 scale=of_tile[:, q:q + 1])
                        act.wait_ge(turned, after(turned, g))
                        nc.scalar.copy(hot_t[b % 2], p_t[:, :]).then_inc(copied, 1)

                    if c == 0:
                        prepare(0, 0)
                        prepare(1, 1)

                    def body(g, b, i):
                        if exists(g, 3):
                            act.wait_ge(summed, after(summed, g - 1))
                            copy_indices(act, g + 3, (b + 3) % UNIT, idx, idx_ready)
                        if c == 0 and exists(g, 2):
                            prepare(g + 2, (b + 2) % UNIT)
                    units(act, body, pieces(lambda n, j: tile.scalar(act, n, j, added)))

                @block.vector
                def _(dve):
                    start(dve, added)
                    if c == 0:
                        start(dve, coefs)
                    if finish:
                        tile.start_vector(dve)

                    def hot_all(g, b):
                        if c == 0:
                            hot(hot_r[b], type8, g, R)
                        hot(hot_n[b], local, g, WIN).then_inc(hots, 1)

                    def make_coefficients(g, b):
                        k = b % 2
                        dve.wait_ge(found, after(found, g))
                        dve.wait_ge(hots, after(hots, g))
                        nc.vector.tensor_tensor(pick[k], p_f[k][:, :, 0:WIN], hot_n[b], ALU.mult).then_inc(picked, 1)
                        dve.wait_ge(picked, after(picked, g))
                        nc.vector.tensor_reduce(share[k], pick[k], AX.X, ALU.add).then_inc(shared, 1)
                        dve.wait_ge(shared, after(shared, g))
                        cf = coef[:, bass.ds(g, 1), :, :].rearrange("p g q c -> p (g q) c")
                        rate = bc(share[k].unsqueeze(2), [P, TPG, 2 * B])
                        if first:
                            nc.vector.tensor_tensor(cf, p_f[k][:, :, WIN:], rate, ALU.mult).then_inc(coefs, 1)
                        else:
                            dve.wait_ge(coefs, after(coefs, g - 1))
                            nc.vector.tensor_tensor(again, p_f[k][:, :, WIN:], rate, ALU.mult).then_inc(rated, 1)
                            dve.wait_ge(rated, after(rated, g))
                            nc.vector.tensor_tensor(cf, cf, again, ALU.add).then_inc(coefs, 1)
                        dve.wait_ge(coefs, after(coefs, g))

                    def weigh(g, b):
                        if c == 0:
                            make_coefficients(g, b)
                        dve.wait_ge(hots, after(hots, g))
                        cf = coef[:, bass.ds(g, 1), :, c * B:(c + 1) * B].rearrange("p g q c -> p (g q) c").unsqueeze(2)
                        nc.vector.tensor_tensor(woh[b], bc(hot_n[b].unsqueeze(3), [P, TPG, WIN, B]),
                                                bc(cf, [P, TPG, WIN, B]), ALU.mult).then_inc(weights, 1)

                    hot_all(0, 0)
                    hot_all(1, 1)
                    weigh(0, 0)
                    if first:
                        nc.vector.memset(acc[:, 0:half], 0.0).then_inc(cleared, 1)
                        dve.wait_ge(cleared, 2)

                    def body(g, b, i):
                        v = dve.value_load(base[0:1, bass.ds(g, 1)], min_val=0, max_val=N)
                        if exists(g, 2):
                            hot_all(g + 2, (b + 2) % UNIT)
                        if exists(g, 1):
                            weigh(g + 1, (b + 1) % UNIT)
                        dve.wait_ge(summed, after(summed, g))
                        dve.wait_ge(added, after(added, g - 1))
                        here = acc_s[:, :, bass.ds(v * B, WB)]
                        nc.vector.tensor_tensor(here, here, p_s[b % 2][:, :, 0:WB], ALU.add).then_inc(added, 1)
                    units(dve, body, pieces(lambda n, j: tile.vector(dve, n, j)))

                @block.tensor
                def _(pe):
                    start(pe, summed)
                    if c == 0:
                        start(pe, found)

                    def turn(g, b):
                        pe.wait_ge(hots, after(hots, g))
                        if not isinstance(g, int) or g:
                            pe.wait_ge(copied, after(copied, g - 1))
                        nc.tensor.transpose(p_t[:, :], hot_r[b].rearrange("p q r -> p (q r)"), ident[:, :]).then_inc(turned, 1)

                    def find(g, b):
                        pe.wait_ge(copied, after(copied, g))
                        pe.wait_ge(coefs, after(coefs, g - 2))
                        nc.tensor.matmul(p_f[b % 2][:, :, :].rearrange("p q c -> p (q c)"), hot_t[b % 2],
                                         tables[b % 2].rearrange("p q c -> p (q c)"), start=True, stop=True)\
                            .then_inc(found, 1)

                    if c == 0:
                        turn(0, 0)
                        find(0, 0)
                        turn(1, 1)
                    if finish:
                        tile.start_tensor(pe)

                    def body(g, b, i):
                        if c == 0 and exists(g, 1):
                            find(g + 1, (b + 1) % UNIT)
                        pe.wait_ge(landed[b], (i + 1) * 16 * TPG)
                        pe.wait_ge(weights, after(weights, g))
                        pe.wait_ge(added, after(added, g - 2))
                        for f in range(FC):
                            for q in range(TPG):
                                ins = nc.tensor.matmul(p_s[b % 2][:, f, 0:WB], rows[b][:, q, f * P:(f + 1) * P],
                                                       woh[b][:, q, :, :].rearrange("p n c -> p (n c)"),
                                                       start=(q == 0), stop=(q == TPG - 1))
                            if f == 0 and c == 0 and exists(g, 2):
                                turn(g + 2, (b + 2) % UNIT)
                        ins.then_inc(summed, 1)
                    units(pe, body, pieces(lambda n, j: tile.tensor(pe, n, j)))
            st.close()

        def next_window():
            with nc.Block() as block:
                @block.vector
                def _(dve):
                    nc.vector.tensor_scalar(cell[:, :, :], cell[:, :, :], float(-QR), None, ALU.add)
                    nc.vector.tensor_scalar(local[:, :, :], local[:, :, :], float(-WIN), None, ALU.add)
                    nc.vector.tensor_scalar(base[:, :], base[:, :], WIN, N, ALU.add, ALU.min)

        def first_window():
            with nc.Block() as block:
                @block.vector
                def _(dve):
                    nc.vector.tensor_copy(cell[:, :, :], cell0[:, :, :])
                    nc.vector.tensor_copy(local[:, :, :], local0[:, :, :])
                    nc.vector.tensor_copy(base[:, :], base0[:, :])

        def over_windows(stage):
            stage(True)
            with nc.If(passes > 1):
                with nc.Fori(1, passes):
                    next_window()
                    stage(False)
                first_window()

        def clear(sums):
            with nc.Block() as block:
                @block.vector
                def _(dve):
                    nc.vector.memset(sums, 0.0)

        def all_windows(stage):
            with nc.Fori(0, passes):
                stage()
                next_window()
            first_window()

        def post(kind):
            st = Stage(f"post{kind}")
            NORMS = (2, 0, 1)[kind]
            loads = 2 if kind == 2 else 1
            w_in = st.sem("w_in")
            x_in = [st.sem(f"x_in{p}") for p in range(2)]
            laid, xt_made, xt_copied, made, used, vec, done, kept, own_ready = (st.sem(n, a) for n, a in (
                ("laid", 0), ("xt_made", 0), ("xt_copied", 2), ("made", 2), ("used", 2), ("vec", 0), ("done", 2),
                ("kept", 2), ("own_ready", 0)))
            var, dev, ready, chunk = (st.sem(n) for n in ("var", "dev", "ready", "chunk"))
            stored = st.pool_dma_sem("stored")
            C = ET if kind == 0 else B
            table = (x, x1tab, htab)[kind]
            dest = (x1tab, htab, out)[kind]
            src_acc = acc_u if kind == 0 else acc_s
            cut = Carve(area, AREA)
            rows = [a[0:NP] for a in cut.tiles(2, NK, D)]
            fin = [a[0:NP] for a in cut.tiles(2, NK, D)]
            laid_sb = cut.tiles(2, FC, C, NP)
            y = cut.tiles(1, NK, D)[0][0:NP] if kind != 1 else None
            if kind == 0:
                own_b = [a[0:NP] for a in cut.tiles(2, NK, D)]
                g_bc, b_bc = (a[0:NP] for a in cut.tiles(2, D))
            if kind:
                xt_sb = cut.tiles(2, FC, NP)
                bs = cut(D)[0:1]
            res = [a[0:NP] for a in cut.tiles(2, NK, D)] if kind == 2 else rows
            stat, = (a[0:NP] for a in cut.tiles(1, NK, 6))
            mv, = (a[0:NP] for a in cut.tiles(1, NK, 2))
            rstd, shift = cut(NK)[0:NP], [cut(NK)[0:NP] for _ in range(2)]
            rs2 = [cut(NK)[0:NP] for _ in range(2)]

            def steps(eng, body):
                body(0, 0, 1)
                with eng.Fori(0, NS // 2) as i:
                    body(i * 2 + 1, 1, i + 1)
                    body(i * 2 + 2, 0, i + 2)

            def tile(s, p, k):
                return s * NK + k, (p * NK + k) % 2

            def rows_of(ap, s):
                return ap[bass.ds(s * NK * NP, NK * NP), :].rearrange("(k p) d -> p k d", p=NP)

            with ExitStack() as ps, nc.Block() as block:
                p_xt = [bank(ps, f"p_pxt{p}", [P, FC, P]) for p in range(2)]
                p_o = [bank(ps, f"p_o{p}", [P, NK + 1, D]) for p in range(2)]

                @block.sync
                def _(sp):
                    if kind == 0:
                        sp.dma_start(g_bc, ln_g.unsqueeze(0).broadcast_to([NP, D])).then_inc(w_in, 16)
                        sp.dma_start(b_bc, ln_b.unsqueeze(0).broadcast_to([NP, D])).then_inc(w_in, 16)
                    else:
                        basis, root, bias = ((basis1, root1, bias1), (basis2, root2, bias2))[kind - 1]
                        for f in range(FC):
                            sp.dma_start(bas[:, f, 0:B, :], basis[:, f * P:(f + 1) * P, :].rearrange("b k o -> k b o"))\
                                .then_inc(w_in, 16)
                            sp.dma_start(bas[:, f, B, :], root[f * P:(f + 1) * P, :]).then_inc(w_in, 16)
                        sp.dma_start(bs, bias.unsqueeze(0)).then_inc(w_in, 16)

                    def body(s, p, use):
                        sp.wait_ge(used, after(used, s - 2))
                        sp.dma_start(rows[p], rows_of(table, s)).then_inc(x_in[p], 16)
                        if kind == 2:
                            sp.dma_start(res[p], rows_of(x1tab, s)).then_inc(x_in[p], 16)
                    steps(sp, body)

                @block.scalar
                def _(act):
                    if kind:
                        start(act, xt_copied)
                    start(act, done)
                    if kind == 1:
                        start(act, used)

                    def finish(s, p):
                        act.wait_ge(kept, after(kept, s - 2))
                        if kind == 1:
                            act.wait_ge(made, after(made, s * NK + NK - 1))
                            nc.scalar.activation(fin[p], p_o[p][0:NP, 0:NK, :], ACT.Relu).then_inc(done, 1)
                            act.sem_inc(used, 1)
                        else:
                            act.wait_ge(ready, after(ready, s))
                            for k in range(NK):
                                ins = nc.scalar.activation(fin[p][:, k, :], y[:, k, :], ACT.Identity,
                                                           bias=shift[p][:, k:k + 1], scale=rs2[p][:, k:k + 1])
                            ins.then_inc(done, 1)

                    def body(s, p, use):
                        for k in range(NK):
                            n, q = tile(s, p, k)
                            act.wait_ge(made, after(made, n - 2))
                            for f in range(FC):
                                sums = src_acc[:, f, bass.ds(n * NP * C, NP * C)].rearrange("p (n c) -> p c n", c=C)
                                ins = nc.scalar.copy(laid_sb[q][:, f, :, :], sums)
                            ins.then_inc(laid, 1)
                            if kind:
                                act.wait_ge(xt_made, after(xt_made, n))
                                nc.scalar.copy(xt_sb[q], p_xt[q][:, :, 0:NP]).then_inc(xt_copied, 1)
                        for r in range(NORMS):
                            act.wait_ge(var, s * NORMS + r + 1)
                            nc.scalar.activation(mv[:, :, 1], mv[:, :, 1], ACT.Sqrt, bias=eps1[0:NP, :]).then_inc(dev, 1)
                        finish(s, p)
                    steps(act, body)

                @block.tensor
                def _(pe):
                    start(pe, made)
                    pe.wait_ge(w_in, 16 * (2 if kind == 0 else 2 * FC + 1))

                    def body(s, p, use):
                        if kind:
                            pe.wait_ge(x_in[p], use * 16 * loads)
                            pe.wait_ge(done, after(done, s - 2))
                        else:
                            pe.wait_ge(used, after(used, s - 2))
                        for k in range(NK):
                            n, q = tile(s, p, k)
                            if kind:
                                pe.wait_ge(xt_copied, after(xt_copied, n - 2))
                                for f in range(FC):
                                    ins = nc.tensor.transpose(p_xt[q][:, f, 0:NP], rows[p][:, k, f * P:(f + 1) * P],
                                                              ident[0:NP, 0:NP])
                                ins.then_inc(xt_made, 1)
                            pe.wait_ge(laid, after(laid, n))
                            to = p_o[p][0:NP, k, :]
                            if kind == 0:
                                for f in range(FC):
                                    for t in range(ET):
                                        ins = nc.tensor.matmul(to[:, f * P:(f + 1) * P], laid_sb[q][:, f, t, :],
                                                               bd_m[:, f, t, :], start=(t == 0), stop=(t == ET - 1))
                                ins.then_inc(made, 1)
                            else:
                                for f in range(FC):
                                    for c in range(B):
                                        nc.tensor.matmul(to, laid_sb[q][:, f, c, :], bas[:, f, c, :],
                                                         start=(f == 0 and c == 0), stop=False)
                                pe.wait_ge(xt_copied, after(xt_copied, n))
                                for f in range(FC):
                                    nc.tensor.matmul(to, xt_sb[q][:, f, :], bas[:, f, B, :], start=False, stop=False)
                                nc.tensor.matmul(to, ones[0:1, 0:NP], bs, start=False, stop=True).then_inc(made, 1)
                    steps(pe, body)

                if kind != 1:
                    @block.vector
                    def _(dve):
                        start(dve, used)
                        STEPS = 8 if kind == 0 else 3

                        def body(s, p, use):
                            k, r = [0], [0]

                            def link(ins):
                                k[0] += 1
                                ins.then_inc(vec, 1)
                                dve.wait_ge(vec, s * STEPS + k[0])

                            def moments():
                                for j in range(NK):
                                    ins = nc.vector.bn_stats(stat[:, j, :], y[:, j, :])
                                ins.then_inc(vec, 1)
                                k[0] += 1
                                dve.wait_ge(vec, s * STEPS + k[0])
                                dve.sem_inc(chunk, 1)
                                for j in range(NK):
                                    ins = nc.vector.bn_aggr(mv[:, j, :], stat[:, j, :])
                                ins.then_inc(var, 1)
                                r[0] += 1
                                dve.wait_ge(dev, s * NORMS + r[0])

                            dve.wait_ge(x_in[p], use * 16 * loads)
                            dve.wait_ge(made, after(made, s * NK + NK - 1))
                            dve.wait_ge(done, after(done, s - 1))
                            ins = nc.vector.tensor_tensor(y, p_o[p][0:NP, 0:NK, :], res[p], ALU.add)
                            link(ins)
                            if kind == 2:
                                dve.sem_inc(used, 1)
                            moments()
                            if kind == 0:
                                link(nc.vector.reciprocal(rstd, mv[:, :, 1]))
                                for j in range(NK):
                                    ins = nc.vector.tensor_scalar(y[:, j, :], y[:, j, :], mv[:, j, 0:1], rstd[:, j:j + 1],
                                                                  ALU.subtract, ALU.mult)
                                link(ins)
                                link(nc.vector.tensor_tensor(y, y, bc(g_bc.unsqueeze(1), [NP, NK, D]), ALU.mult))
                                dve.wait_ge(own_ready, after(own_ready, s))
                                ins = nc.vector.tensor_tensor(y, y, own_b[p], ALU.add)
                                link(ins)
                                dve.sem_inc(used, 1)
                                moments()
                            link(nc.vector.reciprocal(rs2[p], mv[:, :, 1]))
                            nc.vector.scalar_tensor_tensor(shift[p], mv[:, :, 0], -1.0, rs2[p], ALU.mult, ALU.mult)\
                                .then_inc(ready, 1)
                            dve.wait_ge(ready, after(ready, s))
                            assert k[0] == STEPS, k
                        steps(dve, body)

                @block.gpsimd
                def _(pool):
                    start(pool, kept)
                    if kind == 0:
                        pool.wait_ge(w_in, 32)

                    def store(s, p):
                        pool.wait_ge(done, after(done, s))
                        pool.dma_start(rows_of(dest, s), fin[p]).then_inc(stored, 16)
                        pool.wait_ge(stored, (s + 1) * 16)
                        pool.sem_inc(kept, 1)

                    def body(s, p, use):
                        if kind == 0:
                            pool.wait_ge(x_in[p], use * 16)
                            pool.wait_ge(used, after(used, s - 2))
                            nc.gpsimd.tensor_tensor(own_b[p], rows[p], bc(b_bc.unsqueeze(1), [NP, NK, D]), ALU.add)\
                                .then_inc(own_ready, 1)
                        store(s, p)
                    steps(pool, body)
            st.close()

        bas = score[:, :, :, :].rearrange("p g q h -> p (g q h)")[:, 0:FC * (B + 1) * D]\
            .rearrange("p (f c o) -> p f c o", f=FC, c=B + 1)
        passes = nc.values_load(n_pass[0:1, 0:1], min_val=1, max_val=PASSES)
        ordered = nc.values_load(in_order[0:1, 0:1], min_val=0, max_val=1)
        over_windows(scores)
        softmax()
        with nc.If(ordered > 0):
            values(finish=True)
            convolve(0, x1tab, finish=True)
            convolve(1, htab, finish=True)
        with nc.Else():
            all_windows(values)
            post(0)
            clear(acc[:, :])
            clear(coef[:, :, :, :].rearrange("p g q c -> p (g q c)"))
            all_windows(lambda: convolve(0, x1tab))
            post(1)
            clear(acc[:, :])
            all_windows(lambda: convolve(1, htab))
            post(2)


_INS = ["x", "src", "dst", "edge_type_3", "edge_type_8", "node_type_6",
        "L0_gnn_Wk", "L0_gnn_bk", "L0_gnn_Wq", "L0_gnn_bq", "L0_gnn_Wv", "L0_gnn_bv",
        "L0_gnn_relation_pri", "L0_gnn_Wa", "L0_gnn_Wm", "L0_gnn_ln_g", "L0_gnn_ln_b",
        "L1_gnn_basis1", "L1_gnn_comp1", "L1_gnn_root1", "L1_gnn_bias1",
        "L1_gnn_basis2", "L1_gnn_comp2", "L1_gnn_root2", "L1_gnn_bias2"]


def kernel(**inputs):
    import numpy as _np
    import concourse.bacc as _bacc
    from concourse import mybir as _mybir
    from concourse.bass_utils import run_bass_kernel_spmd as _run

    nc = _bacc.Bacc("TRN2", target_bir_lowering=False, num_devices=1)
    arrays, args = {}, []
    for name in _INS:
        a = _np.ascontiguousarray(inputs[name])
        arrays[f"in_{name}"] = a
        args.append(nc.dram_tensor(f"in_{name}", a.shape, _mybir.dt.from_np(a.dtype), kind="ExternalInput").ap())
    args.append(nc.dram_tensor("out_0", inputs["x"].shape, _mybir.dt.float32, kind="ExternalOutput").ap())
    gnn_kernel(nc, *args)
    r = _run(nc, [arrays], core_ids=[0])
    return r.results[0]["out_0"]
```
